# Optimizing a Trainium2 kernel written in Bass

```python
import numpy as np
import jax
import jax.numpy as jnp

def _softmax(x, axis=-1):
    return jax.nn.softmax(x, axis=axis)

def _gelu(x):
    return jax.nn.gelu(x, approximate=True)

def _silu(x):
    return jax.nn.silu(x)

def _sigmoid(x):
    return jax.nn.sigmoid(x)

def _layernorm(x, axis=-1, eps=1e-05):
    m = jnp.mean(x, axis=axis, keepdims=True)
    v = jnp.var(x, axis=axis, keepdims=True)
    return (x - m) / jnp.sqrt(v + eps)

def _scatter_add(tgt, idx, src, axis=0):
    return tgt.at[idx].add(src)

def _segment_sum(src, seg, n):
    return jax.ops.segment_sum(src, seg, n)
kernel_name = 'mk_gps_d2_gnn_r16_b4cb25'

def setup_inputs(seed: int=0):
    np.random.seed(seed)
    _w = jnp.asarray

    def _rec_inputs():
        import jax
        import jax.numpy as jnp
        _gk = jax.random.key(seed)
        x = -0.0003713 + 1 * jax.random.normal(jax.random.fold_in(_gk, 1), (6250, 256), jnp.float32)
        _s = jax.random.randint(jax.random.fold_in(_gk, 2), (50000,), 0, 6250, jnp.int32)
        _d = jax.random.randint(jax.random.fold_in(_gk, 3), (50000,), 0, 6250, jnp.int32)
        _loop = jnp.arange(6250, dtype=jnp.int32)
        src = jnp.concatenate([_s, _d, _loop])
        dst = jnp.concatenate([_d, _s, _loop])
        _o = jnp.argsort(dst, stable=True)
        src = src[_o]
        dst = dst[_o]
        return (x, src, dst)
    x, src, dst = _rec_inputs()

    def _L0_gnn_setup():
        import jax, jax.numpy as jnp
        import numpy as np
        N_NODES = 3125
        N_EDGES = 100000
        H_SIZE = 256
        HEADS = 8
        HEAD_DIM = H_SIZE // HEADS
        NEG_SLOPE = 0.2
        key = jax.random.key(seed)
        k_x, k_e, k_w, k_as, k_ad, k_b = jax.random.split(key, 6)
        x = jax.random.normal(k_x, (N_NODES, H_SIZE), dtype=jnp.float32)
        edge_index = jax.random.randint(k_e, (2, N_EDGES), 0, N_NODES, dtype=jnp.int64)
        scale = 1.0 / np.sqrt(H_SIZE)
        W = jax.random.normal(k_w, (H_SIZE, HEADS, HEAD_DIM), dtype=jnp.float32) * scale
        att_src = jax.random.normal(k_as, (HEADS, HEAD_DIM), dtype=jnp.float32) * scale
        att_dst = jax.random.normal(k_ad, (HEADS, HEAD_DIM), dtype=jnp.float32) * scale
        bias = jnp.zeros((H_SIZE,), dtype=jnp.float32)
        return {'x': x, 'edge_index': edge_index, 'W': W, 'att_src': att_src, 'att_dst': att_dst, 'bias': bias}
    _L0_gnn_all = _L0_gnn_setup()
    _L0_gnn_in = {k: v for k, v in _L0_gnn_all.items() if k in ('W', 'att_src', 'att_dst', 'bias')}
    del _L0_gnn_all

    def _L0_mix_setup():
        import jax, jax.numpy as jnp
        import numpy as np
        N, F, C, H = (32, 256, 256, 8)
        D = C // H
        EPS_ATTN = 1e-06
        EPS_LN = 1e-05

        def layer_norm(x, g, b):
            mu = jnp.mean(x, axis=-1, keepdims=True)
            var = jnp.var(x, axis=-1, keepdims=True)
            return (x - mu) * jax.lax.rsqrt(var + EPS_LN) * g + b
        key = jax.random.key(seed)
        ks = jax.random.split(key, 8)
        s = 1.0 / np.sqrt(C)
        return {'x': jax.random.normal(ks[0], (N, F, C), jnp.float32), 'Wqkv': jax.random.uniform(ks[1], (3 * C, C), jnp.float32, -s, s), 'ln1_g': jnp.ones((C,), jnp.float32), 'ln1_b': jnp.zeros((C,), jnp.float32), 'W1': jax.random.uniform(ks[2], (C, C), jnp.float32, -s, s), 'b1': jax.random.uniform(ks[3], (C,), jnp.float32, -s, s), 'W2': jax.random.uniform(ks[4], (C, C), jnp.float32, -s, s), 'b2': jax.random.uniform(ks[5], (C,), jnp.float32, -s, s), 'ln2_g': jnp.ones((C,), jnp.float32), 'ln2_b': jnp.zeros((C,), jnp.float32)}
    _L0_mix_all = _L0_mix_setup()
    _L0_mix_in = {k: v for k, v in _L0_mix_all.items() if k in ('Wqkv', 'ln1_g', 'ln1_b', 'W1', 'b1', 'W2', 'b2', 'ln2_g', 'ln2_b')}
    del _L0_mix_all

    def _L0_ffn_setup():
        import jax, jax.numpy as jnp
        import numpy as np
        NUM_EXPERTS = 8
        TOP_K = 2
        B, S, D = (8, 512, 256)

        def _moe(tokens, router_w, w1, b1, w2, b2):
            N = tokens.shape[0]
            E = router_w.shape[0]
            logits = tokens.astype(jnp.float32) @ router_w.astype(jnp.float32).T
            probs = jax.nn.softmax(logits, axis=-1)
            rw, re = jax.lax.top_k(probs, TOP_K)
            if TOP_K > 1:
                rw = rw / jnp.maximum(rw.sum(-1, keepdims=True), 1e-12)
            rw = rw.astype(tokens.dtype)
            combine = jnp.zeros((N, E), tokens.dtype).at[jnp.arange(N)[:, None], re].set(rw)
            out = tokens
            for e in range(E):
                h = jax.nn.gelu(tokens @ w1[e] + b1[e], approximate=False)
                y = h @ w2[e] + b2[e]
                out = out + combine[:, e:e + 1] * y
            return out
        key = jax.random.key(seed)
        ks = jax.random.split(key, 4)
        scale = 1.0 / np.sqrt(D).astype(np.float32)
        return {'input_embeddings': jax.random.normal(ks[0], (B, S, D), jnp.float32), 'router_w': jax.random.normal(ks[1], (NUM_EXPERTS, D), jnp.float32) * scale, 'w1': jax.random.normal(ks[2], (NUM_EXPERTS, D, D), jnp.float32) * scale, 'b1': jnp.zeros((NUM_EXPERTS, D), jnp.float32), 'w2': jax.random.normal(ks[3], (NUM_EXPERTS, D, D), jnp.float32) * scale, 'b2': jnp.zeros((NUM_EXPERTS, D), jnp.float32)}
    _L0_ffn_all = _L0_ffn_setup()
    _L0_ffn_in = {k: v for k, v in _L0_ffn_all.items() if k in ('router_w', 'w1', 'b1', 'w2', 'b2')}
    del _L0_ffn_all

    def _L1_gnn_setup():
        import jax, jax.numpy as jnp
        import numpy as np
        N = 3125
        E_RAND = 50000
        IN_DIM = 256
        HID = 64
        HEADS = 4
        OUT_DIM = 256
        NEG_SLOPE = 0.01

        def _xavier(key, shape, fan_in, fan_out):
            gain = np.sqrt(2.0)
            std = gain * np.sqrt(2.0 / (fan_in + fan_out))
            return jax.random.normal(key, shape, dtype=jnp.float32) * std

        def _leaky(x):
            return jnp.where(x > 0, x, NEG_SLOPE * x)

        def _segment_softmax(e, dst, n):
            m = jax.ops.segment_max(e, dst, num_segments=n)
            m = jnp.where(jnp.isfinite(m), m, 0.0)
            ex = jnp.exp(e - m[dst])
            s = jax.ops.segment_sum(ex, dst, num_segments=n)
            return ex / s[dst]
        key = jax.random.key(seed)
        k = jax.random.split(key, 8)
        h = jax.random.normal(k[0], (N, IN_DIM), dtype=jnp.float32)
        src = jnp.concatenate([jax.random.randint(k[1], (E_RAND,), 0, N), jnp.arange(N)]).astype(jnp.int32)
        dst = jnp.concatenate([jax.random.randint(k[2], (E_RAND,), 0, N), jnp.arange(N)]).astype(jnp.int32)
        W1 = _xavier(k[3], (HEADS, HID, IN_DIM), IN_DIM, HID)
        a1 = _xavier(k[4], (HEADS, 2 * HID), 2 * HID, 1)
        W2 = _xavier(k[5], (OUT_DIM, HID * HEADS), HID * HEADS, OUT_DIM)
        a2 = _xavier(k[6], (2 * OUT_DIM,), 2 * OUT_DIM, 1)
        return {'h': h, 'W1': W1, 'a1': a1, 'W2': W2, 'a2': a2, 'src': src, 'dst': dst}
    _L1_gnn_all = _L1_gnn_setup()
    _L1_gnn_in = {k: v for k, v in _L1_gnn_all.items() if k in ('W1', 'a1', 'W2', 'a2')}
    del _L1_gnn_all

    def _L1_mix_setup():
        import math
        import jax, jax.numpy as jnp
        import numpy as np
        EPS_DIV = 1e-07
        EPS_NORM = 1e-12

        def _l2_normalize(x, axis):
            n = jnp.sqrt(jnp.sum(x * x, axis=axis, keepdims=True))
            return x / jnp.maximum(n, EPS_NORM)
        key = jax.random.key(seed)
        ks = jax.random.split(key, 5)
        b, N, C = (8, 256, 256)
        x = jax.random.normal(ks[0], (b, N, C), dtype=jnp.float32)
        W_qkv = jax.random.normal(ks[1], (C, 3 * C), dtype=jnp.float32) * (1.0 / math.sqrt(C))
        b_qkv = jax.random.normal(ks[2], (3 * C,), dtype=jnp.float32) * 0.02
        W_out = jax.random.normal(ks[3], (C, C), dtype=jnp.float32) * (1.0 / math.sqrt(C))
        b_out = jax.random.normal(ks[4], (C,), dtype=jnp.float32) * 0.02
        return {'x': x, 'W_qkv': W_qkv, 'b_qkv': b_qkv, 'W_out': W_out, 'b_out': b_out}
    _L1_mix_all = _L1_mix_setup()
    _L1_mix_in = {k: v for k, v in _L1_mix_all.items() if k in ('W_qkv', 'b_qkv', 'W_out', 'b_out')}
    del _L1_mix_all

    def _L1_ffn_setup():
        import jax, jax.numpy as jnp
        import numpy as np
        C = 256
        HID = 1024
        E = 8
        TEMP = 1.0
        key = jax.random.key(seed)
        ks = jax.random.split(key, 7)
        x = jax.random.normal(ks[0], (8, 1024, C), dtype=jnp.float32)
        W1 = jax.random.normal(ks[1], (C, HID), dtype=jnp.float32) * 0.02
        b1 = jnp.zeros((HID,), dtype=jnp.float32)
        Wg = jax.random.normal(ks[2], (HID, E), dtype=jnp.float32) * 0.02
        bg = jnp.zeros((E,), dtype=jnp.float32)
        Wd = jax.random.normal(ks[3], (E, HID, C), dtype=jnp.float32) * 0.02
        bd = jnp.zeros((E, C), dtype=jnp.float32)
        return {'x': x, 'W1': W1, 'b1': b1, 'Wg': Wg, 'bg': bg, 'Wd': Wd, 'bd': bd}
    _L1_ffn_all = _L1_ffn_setup()
    _L1_ffn_in = {k: v for k, v in _L1_ffn_all.items() if k in ('W1', 'b1', 'Wg', 'bg', 'Wd', 'bd')}
    del _L1_ffn_all
    return {'x': x, 'src': src, 'dst': dst, 'L0_gnn_W': _L0_gnn_in['W'], 'L0_gnn_att_src': _L0_gnn_in['att_src'], 'L0_gnn_att_dst': _L0_gnn_in['att_dst'], 'L0_gnn_bias': _L0_gnn_in['bias'], 'L0_mix_Wqkv': _L0_mix_in['Wqkv'], 'L0_mix_ln1_g': _L0_mix_in['ln1_g'], 'L0_mix_ln1_b': _L0_mix_in['ln1_b'], 'L0_mix_W1': _L0_mix_in['W1'], 'L0_mix_b1': _L0_mix_in['b1'], 'L0_mix_W2': _L0_mix_in['W2'], 'L0_mix_b2': _L0_mix_in['b2'], 'L0_mix_ln2_g': _L0_mix_in['ln2_g'], 'L0_mix_ln2_b': _L0_mix_in['ln2_b'], 'L0_ffn_router_w': _L0_ffn_in['router_w'], 'L0_ffn_w1': _L0_ffn_in['w1'], 'L0_ffn_b1': _L0_ffn_in['b1'], 'L0_ffn_w2': _L0_ffn_in['w2'], 'L0_ffn_b2': _L0_ffn_in['b2'], 'L1_gnn_W1': _L1_gnn_in['W1'], 'L1_gnn_a1': _L1_gnn_in['a1'], 'L1_gnn_W2': _L1_gnn_in['W2'], 'L1_gnn_a2': _L1_gnn_in['a2'], 'L1_mix_W_qkv': _L1_mix_in['W_qkv'], 'L1_mix_b_qkv': _L1_mix_in['b_qkv'], 'L1_mix_W_out': _L1_mix_in['W_out'], 'L1_mix_b_out': _L1_mix_in['b_out'], 'L1_ffn_W1': _L1_ffn_in['W1'], 'L1_ffn_b1': _L1_ffn_in['b1'], 'L1_ffn_Wg': _L1_ffn_in['Wg'], 'L1_ffn_bg': _L1_ffn_in['bg'], 'L1_ffn_Wd': _L1_ffn_in['Wd'], 'L1_ffn_bd': _L1_ffn_in['bd']}

def reference(x, src, dst, L0_gnn_W, L0_gnn_att_src, L0_gnn_att_dst, L0_gnn_bias, L0_mix_Wqkv, L0_mix_ln1_g, L0_mix_ln1_b, L0_mix_W1, L0_mix_b1, L0_mix_W2, L0_mix_b2, L0_mix_ln2_g, L0_mix_ln2_b, L0_ffn_router_w, L0_ffn_w1, L0_ffn_b1, L0_ffn_w2, L0_ffn_b2, L1_gnn_W1, L1_gnn_a1, L1_gnn_W2, L1_gnn_a2, L1_mix_W_qkv, L1_mix_b_qkv, L1_mix_W_out, L1_mix_b_out, L1_ffn_W1, L1_ffn_b1, L1_ffn_Wg, L1_ffn_bg, L1_ffn_Wd, L1_ffn_bd):
    import jax
    import jax.numpy as jnp

    def _L0_gnn_ref(x, edge_index, W, att_src, att_dst, bias):
        import jax, jax.numpy as jnp
        import numpy as np
        N_NODES = 3125
        N_EDGES = 100000
        H_SIZE = 256
        HEADS = 8
        HEAD_DIM = H_SIZE // HEADS
        NEG_SLOPE = 0.2
        'GATConv (concat heads) -> relu -> dropout(eval=identity).\n\n            x: [N, F]; edge_index: [2, E] with (src=row0, dst=row1) meaning message j->i.\n            '
        N = x.shape[0]
        h = jnp.einsum('nf,fhd->nhd', x, W)
        a_src = jnp.sum(h * att_src, axis=-1)
        a_dst = jnp.sum(h * att_dst, axis=-1)
        src = edge_index[0]
        dst = edge_index[1]
        e = jax.nn.leaky_relu(a_src[src] + a_dst[dst], NEG_SLOPE)
        e_max = jax.ops.segment_max(e, dst, num_segments=N)
        e_exp = jnp.exp(e - e_max[dst])
        denom = jax.ops.segment_sum(e_exp, dst, num_segments=N)
        alpha = e_exp / (denom[dst] + 1e-16)
        msg = h[src] * alpha[:, :, None]
        out = jax.ops.segment_sum(msg, dst, num_segments=N)
        out = out.reshape(N, -1) + bias
        return jax.nn.relu(out)

    def _L0_mix_ref(x, Wqkv, ln1_g, ln1_b, W1, b1, W2, b2, ln2_g, ln2_b):
        import jax, jax.numpy as jnp
        import numpy as np
        N, F, C, H = (32, 256, 256, 8)
        D = C // H
        EPS_ATTN = 1e-06
        EPS_LN = 1e-05

        def layer_norm(x, g, b):
            mu = jnp.mean(x, axis=-1, keepdims=True)
            var = jnp.var(x, axis=-1, keepdims=True)
            return (x - mu) * jax.lax.rsqrt(var + EPS_LN) * g + b
        n, f, c = x.shape
        qkv = jnp.einsum('nfc,oc->nfo', x, Wqkv)
        q, k, v = jnp.split(qkv, 3, axis=-1)
        q = q.reshape(n, f, H, D)
        k = k.reshape(n, f, H, D)
        v = v.reshape(n, f, H, D)
        q = jax.nn.elu(q) + 1.0
        k = jax.nn.elu(k) + 1.0
        kv = jnp.einsum('nshd,nshm->nhmd', k, v)
        ksum = jnp.sum(k, axis=1)
        z = 1.0 / (jnp.einsum('nlhd,nhd->nlh', q, ksum) + EPS_ATTN)
        t = jnp.einsum('nlhd,nhmd,nlh->nlhm', q, kv, z)
        t = t.reshape(n, f, c)
        x1 = layer_norm(t + x, ln1_g, ln1_b)
        h = jax.nn.gelu(jnp.einsum('nfc,oc->nfo', x1, W1) + b1, approximate=False)
        y = jnp.einsum('nfc,oc->nfo', h, W2) + b2
        return layer_norm(y + x1, ln2_g, ln2_b)

    def _L0_ffn_ref(input_embeddings, router_w, w1, b1, w2, b2):
        import jax, jax.numpy as jnp
        import numpy as np
        NUM_EXPERTS = 8
        TOP_K = 2
        B, S, D = (8, 512, 256)

        def _moe(tokens, router_w, w1, b1, w2, b2):
            N = tokens.shape[0]
            E = router_w.shape[0]
            logits = tokens.astype(jnp.float32) @ router_w.astype(jnp.float32).T
            probs = jax.nn.softmax(logits, axis=-1)
            rw, re = jax.lax.top_k(probs, TOP_K)
            if TOP_K > 1:
                rw = rw / jnp.maximum(rw.sum(-1, keepdims=True), 1e-12)
            rw = rw.astype(tokens.dtype)
            combine = jnp.zeros((N, E), tokens.dtype).at[jnp.arange(N)[:, None], re].set(rw)
            out = tokens
            for e in range(E):
                h = jax.nn.gelu(tokens @ w1[e] + b1[e], approximate=False)
                y = h @ w2[e] + b2[e]
                out = out + combine[:, e:e + 1] * y
            return out
        b, s, d = input_embeddings.shape
        tokens = input_embeddings.reshape(b * s, d)
        return _moe(tokens, router_w, w1, b1, w2, b2).reshape(b, s, d)

    def _L1_gnn_ref(h, W1, a1, W2, a2, src, dst):
        import jax, jax.numpy as jnp
        import numpy as np
        N = 3125
        E_RAND = 50000
        IN_DIM = 256
        HID = 64
        HEADS = 4
        OUT_DIM = 256
        NEG_SLOPE = 0.01

        def _xavier(key, shape, fan_in, fan_out):
            gain = np.sqrt(2.0)
            std = gain * np.sqrt(2.0 / (fan_in + fan_out))
            return jax.random.normal(key, shape, dtype=jnp.float32) * std

        def _leaky(x):
            return jnp.where(x > 0, x, NEG_SLOPE * x)

        def _segment_softmax(e, dst, n):
            m = jax.ops.segment_max(e, dst, num_segments=n)
            m = jnp.where(jnp.isfinite(m), m, 0.0)
            ex = jnp.exp(e - m[dst])
            s = jax.ops.segment_sum(ex, dst, num_segments=n)
            return ex / s[dst]
        n = h.shape[0]
        z = jnp.einsum('ni,hoi->nho', h, W1)
        a_s, a_d = (a1[:, :HID], a1[:, HID:])
        es = jnp.einsum('nho,ho->nh', z, a_s)
        ed = jnp.einsum('nho,ho->nh', z, a_d)
        e = _leaky(es[src] + ed[dst])
        alpha = _segment_softmax(e, dst, n)
        m = jax.ops.segment_sum(alpha[:, :, None] * z[src], dst, num_segments=n)
        h1 = jax.nn.elu(m.reshape(n, HEADS * HID))
        z2 = h1 @ W2.T
        e2 = _leaky((z2 @ a2[:OUT_DIM])[src] + (z2 @ a2[OUT_DIM:])[dst])
        alpha2 = _segment_softmax(e2, dst, n)
        out = jax.ops.segment_sum(alpha2[:, None] * z2[src], dst, num_segments=n)
        return out

    def _L1_mix_ref(x, W_qkv, b_qkv, W_out, b_out):
        import math
        import jax, jax.numpy as jnp
        import numpy as np
        EPS_DIV = 1e-07
        EPS_NORM = 1e-12

        def _l2_normalize(x, axis):
            n = jnp.sqrt(jnp.sum(x * x, axis=axis, keepdims=True))
            return x / jnp.maximum(n, EPS_NORM)
        b, N, C = x.shape
        qkv = x @ W_qkv + b_qkv
        q, k, v = jnp.split(qkv, 3, axis=2)
        q = q - jnp.mean(q, axis=2, keepdims=True)
        k = k - jnp.mean(k, axis=2, keepdims=True)
        q2 = q * q
        k2 = k * k
        q2s = jnp.sum(q2, axis=2, keepdims=True)
        k2s = jnp.sum(k2, axis=2, keepdims=True)
        k2 = _l2_normalize(k2 / (k2s + EPS_DIV), axis=-2)
        q2 = _l2_normalize(q2 / (q2s + EPS_DIV), axis=-1)
        kv = jnp.einsum('bnc,bnd->bcd', k2, v)
        t2 = jnp.einsum('bnc,bcd->bnd', q2, kv) / math.sqrt(N)
        attn = v + t2
        return attn @ W_out + b_out

    def _L1_ffn_ref(x, W1, b1, Wg, bg, Wd, bd):
        import jax, jax.numpy as jnp
        import numpy as np
        C = 256
        HID = 1024
        E = 8
        TEMP = 1.0
        orig_shape = x.shape
        xf = x.reshape(-1, orig_shape[-1])
        H = jax.nn.gelu(xf @ W1 + b1, approximate=False)
        probs = jax.nn.softmax((H @ Wg + bg) / TEMP, axis=-1)
        assign = jnp.argmax(probs, axis=-1)
        out = jnp.zeros_like(xf)
        for e in range(Wd.shape[0]):
            y = H @ Wd[e] + bd[e]
            sel = (assign == e)[:, None]
            out = out + jnp.where(sel, probs[:, e:e + 1] * y, 0.0)
        return out.reshape(orig_shape)
    edge_index = jnp.stack([src, dst])
    xn = _layernorm(x, axis=-1)
    x = x + _L0_gnn_ref(xn, edge_index, L0_gnn_W, L0_gnn_att_src, L0_gnn_att_dst, L0_gnn_bias) + _L0_mix_ref(xn[None], L0_mix_Wqkv, L0_mix_ln1_g, L0_mix_ln1_b, L0_mix_W1, L0_mix_b1, L0_mix_W2, L0_mix_b2, L0_mix_ln2_g, L0_mix_ln2_b)[0]
    x = x + _L0_ffn_ref(_layernorm(x, axis=-1)[None], L0_ffn_router_w, L0_ffn_w1, L0_ffn_b1, L0_ffn_w2, L0_ffn_b2)[0]
    xn = _layernorm(x, axis=-1)
    x = x + _L1_gnn_ref(xn, L1_gnn_W1, L1_gnn_a1, L1_gnn_W2, L1_gnn_a2, src, dst) + _L1_mix_ref(xn[None], L1_mix_W_qkv, L1_mix_b_qkv, L1_mix_W_out, L1_mix_b_out)[0]
    x = x + _L1_ffn_ref(_layernorm(x, axis=-1)[None], L1_ffn_W1, L1_ffn_b1, L1_ffn_Wg, L1_ffn_bg, L1_ffn_Wd, L1_ffn_bd)[0]
    return x

_drawn_inputs = setup_inputs


def setup_inputs(seed=0):
    import zlib

    import numpy as np

    out = dict(_drawn_inputs(seed))
    spreads = {'L0_gnn_bias': (0.0, 0.1),
     'L0_mix_ln1_g': (1.0, 0.2),
     'L0_mix_ln1_b': (0.0, 0.1),
     'L0_mix_ln2_g': (1.0, 0.2),
     'L0_mix_ln2_b': (0.0, 0.1),
     'L0_ffn_b1': (0.0, 0.383),
     'L0_ffn_b2': (0.0, 0.1),
     'L1_ffn_b1': (0.0, 0.8),
     'L1_ffn_bg': (0.0, 0.8),
     'L1_ffn_bd': (0.0, 0.8)}
    factors = {'L0_gnn_att_dst': 4.289,
     'L0_mix_Wqkv': 4.294,
     'L0_mix_b1': 4.22,
     'L1_mix_b_out': 8.0,
     'L1_ffn_W1': 8.0,
     'L1_ffn_Wg': 8.0,
     'L1_ffn_Wd': 8.0}
    for name, (base, spread) in spreads.items():
        noise = np.random.default_rng([zlib.crc32(name.encode()), seed]).standard_normal(out[name].shape)
        drawn = base * np.exp(spread * noise) if base else spread * noise
        out[name] = jnp.asarray(drawn.astype(out[name].dtype))
    for name, factor in factors.items():
        out[name] = (out[name] * factor).astype(out[name].dtype)
    return out
```

```python
from contextlib import ExitStack

import numpy as np

import concourse.bass as bass
from concourse import mybir

F32 = mybir.dt.float32
I32 = mybir.dt.int32
U32 = mybir.dt.uint32
BF16 = mybir.dt.bfloat16
ALU = mybir.AluOpType
ACT = mybir.ActivationFunctionType
AX = mybir.AxisListType

N = 6250
NB = 49
NP = NB * 128
LAST = N - 48 * 128
E = 106250
NT = 832
NS = NT + 48
NSP = 896
BIG = 1e30
ENGINES = ("sync", "scalar", "vector", "tensor", "gpsimd")


class Queues:

    def __init__(self, nc, ctx):
        self.nc, self.ctx = nc, ctx
        self.q = {e: [] for e in ENGINES}
        self.n_sems = 0
        self.sem = {}
        self.count = {}
        self.dmas = []
        self.phase("p")

    def new_sem(self, name):
        self.n_sems += 1
        return self.ctx.enter_context(self.nc.semaphore(f"{name}_{self.n_sems}"))

    def phase(self, name):
        for e in ENGINES:
            self.sem[e] = self.new_sem(f"{name}_{e}")
            self.count[e] = 0

    def op(self, eng, fns, *waits):
        if not isinstance(fns, (list, tuple)):
            fns = [fns]
        self.count[eng] += 1
        self.q[eng].append(([w for w in waits if w], fns, self.sem[eng], 1))
        return (self.sem[eng], self.count[eng])

    def last(self, eng):
        return (self.sem[eng], self.count[eng]) if self.count[eng] else None

    def dma(self, eng, slot, fn, *waits):
        slot.n += 16
        self.q[eng].append(([w for w in waits if w], [fn], slot.sem, 16))
        return (slot.sem, slot.n)

    def barrier(self, name, *slots):
        marks = [self.last(e) for e in ENGINES] + [(s.sem, s.n) for s in slots if s.n]
        for e in ENGINES:
            self.q[e].append(([m for m in marks if m], [], None, 0))
        self.phase(name)

    def play(self, eng, e):
        seen = {}
        for waits, fns, sem, inc in self.q[eng]:
            for s, v in waits:
                if seen.get(id(s), 0) < v:
                    e.wait_ge(s, v)
                    seen[id(s)] = v
            for f in fns:
                r = f(e)
            if inc:
                r.then_inc(sem, inc)


class Slot:

    def __init__(self, Q, name):
        self.sem, self.n = Q.new_sem(name), 0


class Ring:

    def __init__(self, aps):
        self.aps, self.i = aps, 0
        self.freed = [() for _ in aps]

    def get(self):
        k = self.i % len(self.aps)
        self.i += 1
        assert self.freed[k] is not None, "a buffer is still in use"
        w, self.freed[k] = self.freed[k], None
        return k, self.aps[k], w

    def free(self, k, *tokens):
        self.freed[k] = tokens


def pipeline(gens):
    gens, live = list(gens), []
    while gens or live:
        if gens:
            live.append(gens.pop(0))
        for g in list(live):
            try:
                next(g)
            except StopIteration:
                live.remove(g)


class Arena:
    def __init__(self, t, size):
        self.t, self.size, self.at = t, size, 0

    def reset(self, at=0):
        self.at = at

    def take(self, *shape, dt=F32):
        n = int(np.prod(shape))
        words = n if dt in (F32, I32, U32) else (n + 1) // 2
        words += words % 2
        assert self.at + words <= self.size, (self.at, words, self.size)
        v = self.t[:, self.at:self.at + words]
        self.at += words
        if dt != F32:
            v = v.bitcast(dt)
        v = v[:, 0:n]
        if len(shape) == 2:
            v = v.rearrange("p (a b) -> p a b", b=shape[1])
        elif len(shape) == 3:
            v = v.rearrange("p (a b c) -> p a b c", b=shape[1], c=shape[2])
        return v


def program(nc, A, out, debug=None):
    ctx = ExitStack()
    with ctx:
        def sb(name, shape, dt=F32):
            return ctx.enter_context(nc.sbuf_tensor(name, shape, dt))

        Q = Queues(nc, ctx)
        op, dma = Q.op, Q.dma
        X = sb("X", [128, NB, 256])
        ART = sb("AR", [128, 33500])
        AR = Arena(ART, 33500)
        ident = sb("ident", [128, 128])
        iota_n = sb("iota_n", [128, 128])
        iota8 = sb("iota8", [128, 8])
        ones = sb("ones", [128, 8])
        hmask = sb("hmask", [128, 132])
        eps = sb("eps", [128, 1])
        REL = sb("REL", [128, NSP])
        SRCI = sb("SRCI", [128, NSP], I32)
        DSTI = sb("DSTI", [128, NSP], I32)
        BROW = sb("BROW", [1, NSP], I32)
        MV = sb("MV", [128, NB, 2])
        RS = sb("RS", [128, NB])
        BN = sb("BN", [128, 8, 6])
        banks = [ctx.enter_context(nc.psum_tensor(f"ps{i}", [128, 512], F32)) for i in range(8)]

        def scratch(name, shape, dt=F32):
            return nc.dram_tensor(name, shape, dt, kind="Internal").ap()

        D_se = scratch("D_se", (NT, 128), I32)
        D_de = scratch("D_de", (NT, 128), I32)
        D_b = scratch("D_b", (7, 128), I32)
        D_key = scratch("D_key", (NSP * 128 + 2, 1))
        D_h = scratch("D_h", (NP, 256))
        D_as8, D_ad8 = scratch("D_as8", (NP, 8)), scratch("D_ad8", (NP, 8))
        D_z = scratch("D_z", (NP, 256))
        D_as4, D_ad4 = scratch("D_as4", (NP, 4)), scratch("D_ad4", (NP, 4))
        D_z2 = scratch("D_z2", (NP, 256))
        D_as1, D_ad1 = scratch("D_as1", (NP, 1)), scratch("D_ad1", (NP, 1))

        slots = [Slot(Q, f"d{i}") for i in range(12)]
        wslots = [Slot(Q, f"w{i}") for i in range(4)]
        gslots = [Slot(Q, f"g{i}") for i in range(12)]

        def copy_act(o, i):
            return lambda e: e.activation(o, i, ACT.Copy)

        def tt(o, a, b, f):
            return lambda e: e.tensor_tensor(o, a, b, f)

        def ts(o, a, s1, s2, f1, f2=None):
            if f2 is None:
                return lambda e: e.tensor_scalar(o, a, s1, None, f1)
            return lambda e: e.tensor_scalar(o, a, s1, s2, f1, f2)

        def stt(o, a, s, b, f1, f2):
            return lambda e: e.scalar_tensor_tensor(out=o, in0=a, scalar=s, in1=b, op0=f1, op1=f2)

        def rcp(o, i):
            return lambda e: e.reciprocal(o, i)

        def top8(o, i):
            return lambda e: e.max(o, i)

        def top8_at(o, v, i):
            return lambda e: e.max_index(o, v, i)

        def cp(o, i):
            return lambda e: e.tensor_copy(o, i)

        def mm(o, l, r, start=True, stop=True):
            return lambda e: e.matmul(o, l, r, start=start, stop=stop)

        def tr(o, i, k=128):
            return lambda e: e.transpose(o, i, ident[0:k, 0:k])

        def chain(*fns):
            t = None
            for f in fns:
                t = op("vector", f, Q.last("vector"))
            return t

        class Loader:

            def __init__(self):
                self.toks = []

            def load(self, o, i):
                s = slots[len(self.toks) % len(slots)]
                self.toks.append(dma("sync", s, lambda e: e.dma_start(o, i), (s.sem, s.n) if s.n else None))
                return self.toks[-1]

        L = Loader()
        w_edge = [dma("sync", slots[0], lambda e: e.dma_start(D_se.rearrange("t e -> (t e)")[0:E].rearrange("(a b) -> a b", a=10), A["src"].rearrange("(a b) -> a b", a=10))),
                  dma("sync", slots[1], lambda e: e.dma_start(D_de.rearrange("t e -> (t e)")[0:E].rearrange("(a b) -> a b", a=10), A["dst"].rearrange("(a b) -> a b", a=10)))]
        m0 = op("vector", lambda e: e.memset(X[:, NB - 1, :], 0.0))
        wx = [dma("sync", slots[2], lambda e: e.dma_start(X[:, 0:48, :], A["x"][0:6144, :].rearrange("(b p) f -> p b f", p=128))),
              dma("sync", slots[3], lambda e: e.dma_start(X[0:LAST, 48, :], A["x"][6144:N, :]), m0)]
        AR.reset()
        padi = AR.take(2, 246, dt=I32)
        sval = AR.take(7)
        gi = AR.take(NT, dt=I32)
        gf = AR.take(NT)
        it = AR.take(NT)
        gb = AR.take(NT)
        gm = AR.take(NT)
        cnt = AR.take(7)
        tsf = AR.take(7)
        tsi = AR.take(7, dt=I32)
        bsf = AR.take(7)
        bsi = AR.take(7, dt=I32)
        b128 = AR.take(7)
        guard = AR.take(2)
        seven = AR.take(8)
        di = AR.take(7, 128, dt=I32)
        si = AR.take(7, 128, dt=I32)
        df = AR.take(7, 128)
        sf = AR.take(7, 128)
        rel = AR.take(7, 128)
        key = AR.take(7, 128)
        vm = AR.take(7, 128)

        c1 = op("gpsimd", [lambda e: e.memset(ident[:, :], 0.0), lambda e: e.memset(padi[:, 0, :], 0),
                           lambda e: e.memset(padi[:, 1, :], NP - 1), lambda e: e.memset(eps[:, :], 1e-5),
                           lambda e: e.memset(ones[:, :], 1.0), lambda e: e.memset(guard[:, :], -7.0),])
        op("vector", lambda e: e.memset(hmask[:, :], 0.0))
        op("vector", [(lambda h: lambda e: e.memset(hmask[32 * h:32 * h + 32, 32 * h:32 * h + 32], 1.0))(h) for h in range(4)]
           + [(lambda h: lambda e: e.memset(hmask[32 * h:32 * h + 32, 128 + h:129 + h], 1.0))(h) for h in range(4)], Q.last("vector"))
        c2 = op("gpsimd", [lambda e: e.affine_select(out=ident[:, :], in_=ident[:, :], compare_op=ALU.not_equal, fill=1.0, base=0, pattern=[[-1, 128]], channel_multiplier=1)]
                + [lambda e: e.iota(iota_n[:, :], pattern=[[1, 128]], base=0, channel_multiplier=0, allow_small_or_imprecise_dtypes=True),
                   lambda e: e.iota(iota8[:, :], pattern=[[1, 8]], base=0, channel_multiplier=0, allow_small_or_imprecise_dtypes=True),
                   lambda e: e.iota(sval[:, :], pattern=[[128, 7]], base=0, channel_multiplier=1, allow_small_or_imprecise_dtypes=True),
                   lambda e: e.iota(it[:, :], pattern=[[1, NT]], base=0, channel_multiplier=0, allow_small_or_imprecise_dtypes=True)], c1)
        w_edge += [dma("sync", slots[4], lambda e: e.dma_start(D_se.rearrange("t e -> (t e)")[E:NT * 128].unsqueeze(0), padi[0:1, 0, :]), c1),
                   dma("sync", slots[5], lambda e: e.dma_start(D_de.rearrange("t e -> (t e)")[E:NT * 128].unsqueeze(0), padi[0:1, 1, :]), c1),
                   dma("sync", slots[6], lambda e: e.dma_start(D_key[0:1, :], guard[0:1, 0:1]), c1),
                   dma("sync", slots[7], lambda e: e.dma_start(D_key[NSP * 128 + 1:NSP * 128 + 2, :], guard[0:1, 0:1]), c1)]
        wg = dma("sync", slots[8], lambda e: e.dma_start(gi[0:1, :], D_de[:, 127:128].rearrange("t a -> a t")), *w_edge)
        op("vector", lambda e: e.tensor_scalar(gi[0:1, :], gi[0:1, :], 7, None, ALU.logical_shift_right), wg, c2)
        g = chain(cp(gf[0:1, :], gi[0:1, :]), tt(gf[0:1, :], gf[0:1, :], it[0:1, :], ALU.add),
                  cp(seven[0:1, :], ones[0:1, :]))
        onesrow = iota_n
        orow = AR.take(128)
        g = op("vector", lambda e: e.memset(orow[:, :], 1.0), g)
        p = op("tensor", [mm(banks[0][:, 0:416], orow[0:1, :], gf[0:1, 0:416]), mm(banks[1][:, 0:416], orow[0:1, :], gf[0:1, 416:832])], g)
        op("vector", [cp(gb[:, 0:416], banks[0][:, 0:416]), cp(gb[:, 416:832], banks[1][:, 0:416])], p)
        for j in range(7):
            chain(ts(gm[:, :], gb[:, :], sval[:, j:j + 1], None, ALU.is_lt),
                  (lambda j: lambda e: e.tensor_reduce(cnt[:, j:j + 1], gm[:, :], AX.X, ALU.add))(j))
        t = chain(ts(tsf[:, :], cnt[:, :], float(NT - 1), None, ALU.min), cp(tsi[:, :], tsf[:, :]),
                  tt(bsf[:, :], sval[:, :], cnt[:, :], ALU.subtract), cp(bsi[:, :], bsf[:, :]),
                  ts(b128[:, :], bsf[:, :], 128.0, None, ALU.mult))
        wb = dma("sync", slots[9], lambda e: e.dma_start(D_b.rearrange("j p -> p j"), bsi[:, :]), t)
        wb = dma("sync", slots[10], lambda e: e.dma_start(BROW[0:1, :], D_b.rearrange("j p -> (j p)").unsqueeze(0)), wb)
        for j in range(7):
            a = dma("gpsimd", gslots[0], (lambda j: lambda e: e.indirect_dma_start(
                out=di[:, j, :], out_offset=None, in_=D_de, in_offset=bass.IndirectOffsetOnAxis(ap=tsi[:, j:j + 1], axis=0)))(j), t, (gslots[0].sem, gslots[0].n), *w_edge)
            b = dma("gpsimd", gslots[1], (lambda j: lambda e: e.indirect_dma_start(
                out=si[:, j, :], out_offset=None, in_=D_se, in_offset=bass.IndirectOffsetOnAxis(ap=tsi[:, j:j + 1], axis=0)))(j), t, (gslots[1].sem, gslots[1].n))
            op("vector", cp(df[:, j, :], di[:, j, :]), a)
            u = chain(ts(rel[:, j, :], df[:, j, :], b128[:, j:j + 1], None, ALU.subtract))
            v = op("vector", cp(sf[:, j, :], si[:, j, :]), b)
            k = chain(ts(vm[:, j, :], rel[:, j, :], -0.5, None, ALU.is_gt),
                      stt(vm[:, j, :], rel[:, j, :], 127.5, vm[:, j, :], ALU.is_lt, ALU.mult),
                      stt(key[:, j, :], df[:, j, :], 1.0, vm[:, j, :], ALU.add, ALU.mult),
                      ts(key[:, j, :], key[:, j, :], -1.0, None, ALU.add))
            dma("sync", slots[0], (lambda j: lambda e: e.dma_start(
                D_key[1 + j * 16384:1 + (j + 1) * 16384, :].rearrange("(s e) a -> s (e a)", e=128), key[:, j, :]))(j), k, (slots[0].sem, slots[0].n))
            c = slice(128 * j, 128 * j + 128)
            pe = op("tensor", [tr(banks[2][:, 0:128], rel[:, j, :]), tr(banks[2][:, 128:256], sf[:, j, :]), tr(banks[2][:, 256:384], df[:, j, :])], k, v)
            op("vector", [cp(REL[:, c], banks[2][:, 0:128]), cp(SRCI[:, c], banks[2][:, 128:256]), cp(DSTI[:, c], banks[2][:, 256:384])], pe)
        for b in range(NB):
            op("vector", (lambda b: lambda e: e.bn_stats(BN[:, b % 8, :], X[:, b, :]))(b), wx[0] if b < 48 else wx[1], wx[1], Q.last("vector"))
            op("vector", (lambda b: lambda e: e.bn_aggr(MV[:, b, :], BN[:, b % 8, :]))(b), Q.last("vector"))
        Q.barrier("t0", *slots, *gslots)

        def stats():
            for b in range(NB):
                op("vector", (lambda b: lambda e: e.bn_stats(BN[:, b % 8, :], X[:, b, :]))(b), Q.last("vector"))
                op("vector", (lambda b: lambda e: e.bn_aggr(MV[:, b, :], BN[:, b % 8, :]))(b), Q.last("vector"))

        def rstd():
            a = op("scalar", lambda e: e.activation(RS[:, :], MV[:, :, 1], ACT.Sqrt, bias=eps[:, 0:1]), Q.last("vector"))
            return op("vector", lambda e: e.reciprocal(RS[:, :], RS[:, :]), a)

        def ring(n, *shape):
            return Ring([AR.take(*shape) for _ in range(n)])

        def xn_of(o, b):
            return ts(o, X[:, b, :], MV[:, b, 0:1], RS[:, b:b + 1], ALU.subtract, ALU.mult)

        def transposed(src_of, dstT, r_x, r_ps, *w):
            toks = [None] * NB

            def one(b):
                k, xt, fw = r_x.get()
                v = op("vector", src_of(b, xt), *fw, *w)
                yield
                kp, ps, fp = r_ps.get()
                pe = op("tensor", [tr(ps[:, 0:128], xt[:, 0:128]), tr(ps[:, 128:256], xt[:, 128:256])], v, *fp)
                r_x.free(k, pe)
                yield
                a = op("scalar", copy_act(dstT[:, :, 128 * b:128 * b + 128], ps[:, 0:256].rearrange("p (k t) -> p k t", k=2)), pe)
                r_ps.free(kp, a)
                toks[b] = a

            pipeline(one(b) for b in range(NB))
            return toks

        def att_columns(WA, base, W_view, a_src, a_dst, H, L):
            D = 256 // H
            tmp = AR.take(256)
            wb = AR.take(2, 256)
            t = [L.load(wb[:, 0, :], a_src.partition_broadcast(128)), L.load(wb[:, 1, :], a_dst.partition_broadcast(128))]
            r = None
            for k in range(2):
                for n in range(2):
                    op("vector", tt(tmp[:, :], W_view[:, k, 0:256], wb[:, n, :], ALU.mult), *L.toks, Q.last("vector"))
                    r = chain((lambda k, n: lambda e: e.tensor_reduce(WA[:, k, base + n * H:base + (n + 1) * H], tmp[:, :].rearrange("p (h d) -> p h d", h=H), AX.X, ALU.add))(k, n))
            return r

        def tables(XT, toks, WA, H, D_row, D_as, D_ad, r_o, r_ps, wslots, *w):
            def one(b):
                kp, ps, fp = r_ps.get()
                pe = op("tensor", [mm(ps[:, 0:256 + 2 * H], XT[:, k, 128 * b:128 * b + 128], WA[:, k, 0:256 + 2 * H], k == 0, k == 1) for k in range(2)], toks[b], *w, *fp)
                yield
                ko, o, fo = r_o.get()
                a = op("scalar", copy_act(o[:, 0:256 + 2 * H], ps[:, 0:256 + 2 * H]), pe, *fo)
                r_ps.free(kp, a)
                yield
                s = wslots[b % len(wslots)]
                rows = slice(128 * b, 128 * b + 128)
                t = [dma("sync", s, lambda e: e.dma_start(D_row[rows, :], o[:, 0:256]), a),
                     dma("sync", s, lambda e: e.dma_start(D_as[rows, :], o[:, 256:256 + H]), a),
                     dma("sync", s, lambda e: e.dma_start(D_ad[rows, :], o[:, 256 + H:256 + 2 * H]), a)]
                r_o.free(ko, t[-1])

            pipeline(one(b) for b in range(NB))

        def ln_tile(src, dst, g, bb, sm, *w):
            op("vector", lambda e: e.bn_stats(sm[:, 0:6], src), *w, Q.last("vector"))
            v = chain(lambda e: e.bn_aggr(sm[:, 6:8], sm[:, 0:6]))
            yield v
            a = op("scalar", lambda e: e.activation(sm[:, 8:9], sm[:, 7:8], ACT.Sqrt, bias=eps[:, 0:1]), v)
            yield a
            op("vector", lambda e: e.reciprocal(sm[:, 9:10], sm[:, 8:9]), a)
            v = chain(ts(dst, src, sm[:, 6:7], sm[:, 9:10], ALU.subtract, ALU.mult),
                      tt(dst, dst, g, ALU.mult), tt(dst, dst, bb, ALU.add))
            yield v

        rstd()
        AR.reset()
        XT = AR.take(2, NP)
        WA = AR.take(2, 272)
        Wkv = AR.take(2, 768)
        W1 = AR.take(2, 256)
        W2 = AR.take(2, 256)
        bcs = AR.take(5, 256)
        b1c = AR.take(2)
        KVB = AR.take(2, 132)
        L = Loader()
        L.load(WA[:, :, 0:256], A["gW0"].rearrange("(k p) n -> p k n", p=128))
        L.load(Wkv[:, :, :], A["qkv0T"].rearrange("(k p) n -> p k n", p=128))
        L.load(W1[:, :, :], A["m0W1T"].rearrange("(k p) n -> p k n", p=128))
        L.load(W2[:, :, :], A["m0W2T"].rearrange("(k p) n -> p k n", p=128))
        for i, n in enumerate(("L0_mix_ln1_g", "L0_mix_ln1_b", "L0_mix_b2", "L0_mix_ln2_g", "L0_mix_ln2_b")):
            L.load(bcs[:, i, :], A[n].partition_broadcast(128))
        L.load(b1c[:, :], A["L0_mix_b1"].rearrange("(k p) -> p k", p=128))
        mark = AR.at
        wa = att_columns(WA, 256, WA, A["ga_s0"], A["ga_d0"], 8, L)
        rp = Ring(banks[0:4])
        toks = transposed(lambda b, o: xn_of(o, b), XT, ring(3, 256), rp, Q.last("vector"))
        tables(XT, toks, WA, 8, D_h, D_as8, D_ad8, ring(4, 272), rp, wslots, wa)
        Q.barrier("mix0a", *slots, *wslots)

        AR.reset(mark)
        rk, rv, re = ring(4, 256), ring(4, 2, 130), ring(4, 256)
        m1 = op("gpsimd", [(lambda r: lambda e: e.memset(r[:, :, 128:130], 1.0))(r) for r in rv.aps])
        rp = Ring(banks[0:4])
        acc = []

        def kv_tile(b):
            K = 128 if b < 48 else LAST
            kp, ps, fp = rp.get()
            pe = op("tensor", [mm(ps[:, 0:512], XT[:, k, 128 * b:128 * b + 128], Wkv[:, k, 256:768], k == 0, k == 1) for k in range(2)], *fp)
            yield
            ke, e_, fe = re.get()
            kk, kt, fk = rk.get()
            kv, vt, fv = rv.get()
            v = op("vector", ts(e_[:, :], ps[:, 0:256], 0.0, None, ALU.min), pe, *fe)
            a2 = op("scalar", copy_act(vt[:, :, 0:128], ps[:, 256:512].rearrange("p (j n) -> p j n", j=2)), v, *fv, m1)
            a = op("scalar", lambda e: e.activation(e_[:, :], e_[:, :], ACT.Exp), v)
            yield
            v = op("vector", stt(kt[:, :], ps[:, 0:256], 0.0, e_[:, :], ALU.max, ALU.add), a, *fk)
            rp.free(kp, v, a2)
            re.free(ke, v)
            yield
            pe = op("tensor", [mm(banks[6 + j][:, 0:129], kt[0:K, 128 * j:128 * j + 128], vt[0:K, j, 0:129], b == 0, b == NB - 1) for j in range(2)], v, a2)
            rk.free(kk, pe)
            rv.free(kv, pe)
            acc.append(pe)

        pipeline(kv_tile(b) for b in range(NB))
        for j in range(2):
            op("vector", tt(KVB[:, j, 0:128], banks[6 + j][:, 0:128], hmask[:, 0:128], ALU.mult), acc[-1])
            chain(ts(KVB[:, j, 128:132], hmask[:, 128:132], banks[6 + j][:, 128:129], None, ALU.mult))
        Q.barrier("mix0b")

        AR.reset(mark)
        groups = [(4 * g, 4) for g in range(12)] + [(48, 1)]
        rq, rqe = ring(2, 2, 512), ring(1, 2, 512)
        rx1T = rhT = None
        r1 = ring(5, 256)
        rt = ring(2, 256)
        rx1T = ring(1, 2, 512)
        rhT = ring(1, 2, 512)
        rsm = ring(4, 10)
        rz = ring(2, 8)
        rp = Ring(banks[0:8])

        def mix0_group(b0, nb):
            w = 128 * nb
            kq, qt, fq = rq.get()
            ke, qe, fe = rqe.get()
            vs = []
            for m in range(2):
                kp, ps, fp = rp.get()
                pe = op("tensor", [mm(ps[:, 0:w], Wkv[:, k, 128 * m:128 * m + 128], XT[:, k, 128 * b0:128 * b0 + w], k == 0, k == 1) for k in range(2)], *fp)
                v = op("vector", ts(qe[:, m, 0:w], ps[:, 0:w], 0.0, None, ALU.min), pe, *fe)
                a = op("scalar", (lambda m: lambda e: e.activation(qe[:, m, 0:w], qe[:, m, 0:w], ACT.Exp))(m), v)
                v = op("vector", stt(qt[:, m, 0:w], ps[:, 0:w], 0.0, qe[:, m, 0:w], ALU.max, ALU.add), a, *fq)
                rp.free(kp, v)
                vs.append(v)
            rqe.free(ke, v)
            sms, x1s = [], []
            for i in range(nb):
                b = b0 + i
                kp, ps, fp = rp.get()
                pe = op("tensor", [mm(ps[:, 132 * j:132 * j + 132], qt[:, j, 128 * i:128 * i + 128], KVB[:, j, :]) for j in range(2)], v, *fp)
                kt, t_, ft = rt.get()
                kz, z_, fz = rz.get()
                k1, x1, f1 = r1.get()
                ks, sm, fs = rsm.get()
                pv = ps[:, 0:264].rearrange("p (j n) -> p j n", j=2)
                op("vector", ts(z_[:, 0:8].rearrange("p (j h) -> p j h", j=2), pv[:, :, 128:132], 1e-6, None, ALU.add), pe, *fz, *ft, *f1, *fs)
                v1 = chain(rcp(z_[:, 0:8], z_[:, 0:8]),
                           tt(t_[:, :].rearrange("p (j h d) -> p j h d", j=2, h=4), pv[:, :, 0:128].rearrange("p j (h d) -> p j h d", h=4),
                              z_[:, 0:8].rearrange("p (j h) -> p j h", j=2).unsqueeze(3).to_broadcast([128, 2, 4, 32]), ALU.mult))
                rp.free(kp, v1)
                op("vector", xn_of(x1[:, :], b))
                v1 = chain(tt(x1[:, :], x1[:, :], t_[:, :], ALU.add))
                rt.free(kt, v1)
                rz.free(kz, v1)
                gen = ln_tile(x1[:, :], x1[:, :], bcs[:, 0, :], bcs[:, 1, :], sm, v1)
                next(gen)
                sms.append((ks, gen))
                x1s.append((k1, x1))
            rq.free(kq, pe)
            for _, g in sms:
                next(g)
            for ks, g in sms:
                v = next(g)
                rsm.free(ks, v)
            kT, x1T, fT = rx1T.get()
            for i in range(nb):
                x1 = x1s[i][1]
                kp, ps, fp = rp.get()
                pe = op("tensor", [tr(ps[:, 0:128], x1[:, 0:128]), tr(ps[:, 128:256], x1[:, 128:256])], v, *fp)
                a = op("scalar", copy_act(x1T[:, :, 128 * i:128 * i + 128], ps[:, 0:256].rearrange("p (k t) -> p k t", k=2)), pe, *fT)
                rp.free(kp, a)
            kh, hT, fh = rhT.get()
            for m in range(2):
                kp, ps, fp = rp.get()
                pe = op("tensor", [mm(ps[:, 0:w], W1[:, k, 128 * m:128 * m + 128], x1T[:, k, 0:w], k == 0, k == 1) for k in range(2)], a, *fp)
                a2 = op("scalar", (lambda m, ps: lambda e: e.activation(hT[:, m, 0:w], ps[:, 0:w], ACT.Gelu, bias=b1c[:, m:m + 1]))(m, ps), pe, *fh)
                rp.free(kp, a2)
            rx1T.free(kT, pe)
            sms = []
            for i in range(nb):
                k1, x1 = x1s[i]
                kp, ps, fp = rp.get()
                pe = op("tensor", [mm(ps[:, 0:256], hT[:, k, 128 * i:128 * i + 128], W2[:, k, :], k == 0, k == 1) for k in range(2)], a2, *fp)
                op("vector", tt(x1[:, :], x1[:, :], bcs[:, 2, :], ALU.add), a)
                v = op("vector", tt(x1[:, :], x1[:, :], ps[:, 0:256], ALU.add), pe, Q.last("vector"))
                rp.free(kp, v)
                ks, sm, fs = rsm.get()
                gen = ln_tile(x1[:, :], x1[:, :], bcs[:, 3, :], bcs[:, 4, :], sm, v, *fs)
                next(gen)
                sms.append((ks, gen))
            rhT.free(kh, pe)
            for _, g in sms:
                next(g)
            for i, (ks, g) in enumerate(sms):
                k1, x1 = x1s[i]
                v = next(g)
                rsm.free(ks, v)
                v = chain(tt(X[:, b0 + i, :], X[:, b0 + i, :], x1[:, :], ALU.add))
                r1.free(k1, v)

        for b0, nb in groups:
            mix0_group(b0, nb)
        Q.barrier("gnn0")

        def gnn(H, C, J, slope, D_row, D_as, D_ad, name):
            W = J * 128
            P = C * H
            assert P == 128 and C * J == NSP
            AR.reset()
            SC = AR.take(W)
            B1 = AR.take(max(W, NSP * H))
            B2 = AR.take(max(W + 2, NSP * H))
            FA = AR.take(W, dt=BF16)
            FB = AR.take(W, dt=BF16)
            sm = AR.take(8)
            row = AR.take(6, 128)
            E1, E2 = B1[:, 0:NSP * H], B2[:, 0:NSP * H]
            at = lambda T, s: T[:, (s % J * C + s // J) * H:(s % J * C + s // J + 1) * H]
            n = 0
            for D_t, E_t, idx in ((D_as, E1, SRCI), (D_ad, E2, DSTI)):
                for s in range(NSP):
                    g = gslots[n % 12]
                    dma("gpsimd", g, (lambda D_t, E_t, idx, s: lambda e: e.indirect_dma_start(
                        out=at(E_t, s), out_offset=None, in_=D_t,
                        in_offset=bass.IndirectOffsetOnAxis(ap=idx[:, s:s + 1], axis=0)))(D_t, E_t, idx, s))
                    n += 1
            op("vector", tt(E1, E1, E2, ALU.add), *[(g.sem, g.n) for g in gslots])
            v = chain(stt(E1, E1, slope, E1, ALU.mult, ALU.max))
            KW = B2[:, 0:W + 2]
            win = bass.AP(D_key.tensor, D_key.offset, [[W, C], [0, H], [1, W + 2]])
            wk = dma("sync", slots[0], lambda e: e.dma_start(KW, win), v)
            rp = Ring(banks[0:6])
            for j0 in range(0, J, 4):
                nj = min(4, J - j0)
                kp, ps, fp = rp.get()
                pe = op("tensor", [tr(ps[:, 128 * i:128 * i + 128], E1[:, 128 * (j0 + i):128 * (j0 + i) + 128]) for i in range(nj)], v, *fp)
                a = op("scalar", copy_act(SC[:, 128 * j0:128 * (j0 + nj)], ps[:, 0:128 * nj]), pe)
                rp.free(kp, a)
            op("vector", tt(FA[:, :], KW[:, 1:W + 1], KW[:, 0:W], ALU.is_equal), wk, a, v)
            op("vector", tt(FB[:, :], KW[:, 1:W + 1], KW[:, 2:W + 2], ALU.is_equal))
            for F in (FA, FB):
                chain(ts(F[:, :], F[:, :], -1.0, BIG, ALU.add, ALU.mult))

            def segscan(o, x, F, op0, op1, neutral, rev):
                d = (lambda ap: ap[:, ::-1]) if rev else (lambda ap: ap)
                end = 0 if rev else W - 1
                scan = lambda init: (lambda e: e.tensor_tensor_scan(d(o), d(F), d(x), init, op0, op1))
                op("vector", scan(neutral), Q.last("vector"), Q.last("scalar"))
                v = chain(lambda e: e.tensor_reduce(sm[:, 1:2], F[:, :], AX.X, ALU.min), cp(sm[:, 0:1], o[:, end:end + 1]))
                pe = op("tensor", [tr(banks[7][0:1, 0:128], sm[:, 0:1]), tr(banks[7][0:1, 128:256], sm[:, 1:2])], v)
                r = lambda i: row[0:1, i, :]
                op("vector", [cp(r(0).rearrange("p (h c) -> p h c", h=H), banks[7][0:1, 0:128].rearrange("p (c h) -> p h c", h=H)),
                              cp(r(1).rearrange("p (h c) -> p h c", h=H), banks[7][0:1, 128:256].rearrange("p (c h) -> p h c", h=H)),
                              lambda e: e.memset(r(3), neutral)], pe)
                hc = r(2).rearrange("p (h c) -> p h c", h=H)
                ch = r(3).rearrange("p (c h) -> p h c", h=H)
                v = chain(lambda e: e.tensor_tensor_scan(d(r(2)), d(r(1)), d(r(0)), neutral, op0, op1),
                          cp(ch[:, :, 0:C - 1], hc[:, :, 1:C]) if rev else cp(ch[:, :, 1:C], hc[:, :, 0:C - 1]))
                pe = op("tensor", mm(banks[7][:, 256:257], row[0:1, 3, :], ones[0:1, 0:1]), v)
                op("vector", cp(sm[:, 2:3], banks[7][:, 256:257]), pe)
                return chain(scan(sm[:, 2:3]))

            segscan(B1[:, 0:W], SC[:, :], FA[:, :], ALU.add, ALU.max, -BIG, False)
            segscan(B2[:, 0:W], B1[:, 0:W], FB[:, :], ALU.add, ALU.max, -BIG, True)
            v = chain(tt(SC[:, :], SC[:, :], B2[:, 0:W], ALU.subtract),
                      ts(FA[:, :], FA[:, :], -1.0, None, ALU.is_gt), ts(FB[:, :], FB[:, :], -1.0, None, ALU.is_gt))
            a = op("scalar", lambda e: e.activation(SC[:, :], SC[:, :], ACT.Exp), v)
            segscan(B1[:, 0:W], SC[:, :], FA[:, :], ALU.mult, ALU.add, 0.0, False)
            segscan(B2[:, 0:W], B1[:, 0:W], FB[:, :], ALU.mult, ALU.max, 0.0, True)
            v = chain(ts(B2[:, 0:W], B2[:, 0:W], 1e-16, None, ALU.add) if H == 8 else cp(sm[:, 3:4], sm[:, 2:3]),
                      lambda e: e.reciprocal(B2[:, 0:W], B2[:, 0:W]),
                      tt(SC[:, :], SC[:, :], B2[:, 0:W], ALU.mult))
            AL = E1
            for j0 in range(0, J, 4):
                nj = min(4, J - j0)
                kp, ps, fp = rp.get()
                pe = op("tensor", [tr(ps[:, 128 * i:128 * i + 128], SC[:, 128 * (j0 + i):128 * (j0 + i) + 128]) for i in range(nj)], v, *fp)
                a = op("scalar", copy_act(AL[:, 128 * j0:128 * (j0 + nj)], ps[:, 0:128 * nj]), pe)
                rp.free(kp, a)
            Q.barrier(name + "b", *slots, *gslots)

            AR.reset()
            AR.take(W)
            assert AR.take(max(W, NSP * H)) is not None
            Y = AR.take(NB, 256)
            G = ring(10, 256)
            M = ring(3, 256)
            S = ring(3, 128)
            rp = Ring(banks[0:4])
            Yf = Y.rearrange("p b n -> p (b n)")
            m = op("scalar", lambda e: e.activation(Yf, Yf, ACT.MemsetZero)) if False else op("vector", lambda e: e.memset(Yf, 0.0))
            state = {"y": m}

            def step(s):
                kg, gt, fg = G.get()
                sl = gslots[s % 10]
                gk = dma("gpsimd", sl, lambda e: e.indirect_dma_start(
                    out=gt[:, :], out_offset=None, in_=D_row,
                    in_offset=bass.IndirectOffsetOnAxis(ap=SRCI[:, s:s + 1], axis=0)), *fg)
                for _ in range(6):
                    yield
                kS, st, fS = S.get()
                if H == 1:
                    v = op("vector", ts(st[:, :], iota_n[:, :], REL[:, s:s + 1], at(AL, s), ALU.is_equal, ALU.mult), *fS)
                    mt = gt
                    w = gk
                else:
                    kM, mt, fM = M.get()
                    op("vector", ts(st[:, :], iota_n[:, :], REL[:, s:s + 1], None, ALU.is_equal), *fS)
                    w = v = op("vector", tt(mt[:, :].rearrange("p (h d) -> p h d", h=H), gt[:, :].rearrange("p (h d) -> p h d", h=H),
                                            at(AL, s).unsqueeze(2).to_broadcast([128, H, 256 // H]), ALU.mult), gk, *fM)
                    G.free(kg, v)
                kp, ps, fp = rp.get()
                pe = op("tensor", mm(ps[:, 0:256], st[:, :], mt[:, :]), v, w, *fp)
                S.free(kS, pe)
                if H == 1:
                    G.free(kg, pe)
                else:
                    M.free(kM, pe)
                yield

                def add(e):
                    r = e.value_load(BROW[0:1, s:s + 1], min_val=0, max_val=48)
                    o = Yf[:, bass.ds(r * 256, 256)]
                    return e.tensor_tensor(o, ps[:, 0:256], o, ALU.add)

                v = op("vector", add, pe, state["y"])
                state["y"] = v
                rp.free(kp, v)

            pipeline(step(s) for s in range(NS))
            Q.barrier(name + "c", *gslots)
            return Y, AR.at

        Y, at = gnn(8, 16, 56, 0.2, D_h, D_as8, D_ad8, "g0")
        bg = AR.take(256)
        L = Loader()
        t = L.load(bg[:, :], A["L0_gnn_bias"].partition_broadcast(128))
        for b in range(NB):
            op("vector", tt(Y[:, b, :], Y[:, b, :], bg[:, :], ALU.add), t)
            chain(stt(X[:, b, :], Y[:, b, :], 0.0, X[:, b, :], ALU.max, ALU.add))
        v = Q.last("vector")
        if debug is not None and debug == 0:
            return finish(nc, ctx, Q, X, out, slots)
        stats()
        Q.barrier("ffn0", *slots)

        rstd()
        AR.reset()
        RW = AR.take(2, 8)
        W1e, W2e = ring(3, 2, 256), ring(3, 2, 256)
        b1e = AR.take(8, 2)
        b2e = AR.take(256)
        XT = AR.take(2, NP)
        OUT = AR.take(4, 256)
        L = Loader()
        L.load(RW[:, :, :], A["routerT"].rearrange("(k p) n -> p k n", p=128))
        L.load(b1e[:, :, :], A["L0_ffn_b1"].rearrange("e (k p) -> p e k", p=128))
        L.load(b2e[0:8, :], A["L0_ffn_b2"])
        rx = ring(3, 256)
        rp = Ring(banks[0:8])
        toks = transposed(lambda b, o: xn_of(o, b), XT, rx, rp, Q.last("vector"))
        sm = ring(4, 64)
        COMB = AR.take(NB, 8)
        ct = AR.take(2, 128)
        rc = Ring([ct[:, 0, :], ct[:, 1, :]])
        rh = ring(2, 2, 512)

        def softmax8(ps, s_, pe, *w):
            v = op("vector", lambda e: e.tensor_reduce(s_[:, 8:9], ps, AX.X, ALU.max), pe, *w)
            v = chain(ts(s_[:, 9:10], s_[:, 8:9], -1.0, None, ALU.mult))
            a = op("scalar", lambda e: e.activation(s_[:, 0:8], ps, ACT.Exp, bias=s_[:, 9:10], accum_out=s_[:, 10:11]), v)
            op("vector", lambda e: e.reciprocal(s_[:, 11:12], s_[:, 10:11]), a)
            return chain(ts(s_[:, 0:8], s_[:, 0:8], s_[:, 11:12], None, ALU.mult)), a

        def route(b):
            kp, ps, fp = rp.get()
            pe = op("tensor", [mm(ps[:, 0:8], XT[:, k, 128 * b:128 * b + 128], RW[:, k, :], k == 0, k == 1) for k in range(2)], toks[b], *L.toks, *fp)
            yield
            k, s_, fs = sm.get()
            v, a = softmax8(ps[:, 0:8], s_, pe, *fs)
            rp.free(kp, a)
            yield
            iu = s_[:, 24:32].bitcast(U32)
            v = chain(top8(s_[:, 16:24], s_[:, 0:8]), top8_at(iu, s_[:, 16:24], s_[:, 0:8]),
                      cp(s_[:, 32:40], iu), tt(s_[:, 40:41], s_[:, 16:17], s_[:, 17:18], ALU.add),
                      ts(s_[:, 40:41], s_[:, 40:41], 1e-12, None, ALU.max),
                      lambda e: e.reciprocal(s_[:, 41:42], s_[:, 40:41]),
                      ts(s_[:, 42:44], s_[:, 16:18], s_[:, 41:42], None, ALU.mult),
                      ts(s_[:, 48:56], iota8[:, :], s_[:, 32:33], s_[:, 42:43], ALU.is_equal, ALU.mult),
                      ts(s_[:, 56:64], iota8[:, :], s_[:, 33:34], s_[:, 43:44], ALU.is_equal, ALU.mult),
                      tt(COMB[:, b, :], s_[:, 48:56], s_[:, 56:64], ALU.add))
            sm.free(k, v)

        pipeline(route(b) for b in range(NB))
        Q.barrier("ffn0b", *slots)
        rp = Ring(banks[0:8])

        def base(b):
            kp, ps, fp = rp.get()
            pe = op("tensor", tr(ps[0:8, 0:128], COMB[:, b, :]), *fp)
            yield
            kc, c_, fc = rc.get()
            a = op("scalar", copy_act(c_[0:8, :], ps[0:8, 0:128]), pe, *fc)
            rp.free(kp, a)
            kp, ps, fp = rp.get()
            pe = op("tensor", mm(ps[:, 0:256], c_[0:8, :], b2e[0:8, :]), a, *fp)
            rc.free(kc, pe)
            yield
            kx, x_, fx = rx.get()
            v = op("vector", xn_of(x_[:, :], b), *fx)
            chain(tt(x_[:, :], x_[:, :], ps[:, 0:256], ALU.add)) if False else op("vector", tt(x_[:, :], x_[:, :], ps[:, 0:256], ALU.add), pe, v)
            v = chain(tt(X[:, b, :], X[:, b, :], x_[:, :], ALU.add))
            rp.free(kp, v)
            rx.free(kx, v)

        pipeline(base(b) for b in range(NB))
        Q.barrier("ffn0c")
        rp = Ring(banks[0:8])
        for e_ in range(8):
            k1, w1, f1 = W1e.get()
            k2, w2, f2 = W2e.get()
            s1, s2 = wslots[e_ % 2], wslots[2 + e_ % 2]
            t1 = dma("sync", s1, (lambda e_, w1: lambda e: e.dma_start(w1[:, :, :], A["L0_ffn_w1"][e_].rearrange("(k p) n -> p k n", p=128)))(e_, w1), *f1, (s1.sem, s1.n))
            t2 = dma("sync", s2, (lambda e_, w2: lambda e: e.dma_start(w2[:, :, :], A["L0_ffn_w2"][e_].rearrange("(k p) n -> p k n", p=128)))(e_, w2), *f2, (s2.sem, s2.n))

            def group(b0, nb, e_=e_, w1=w1, w2=w2, t1=t1, t2=t2):
                w = 128 * nb
                kh, h, fh = rh.get()
                for m in range(2):
                    kp, ps, fp = rp.get()
                    pe = op("tensor", [mm(ps[:, 0:w], w1[:, k, 128 * m:128 * m + 128], XT[:, k, 128 * b0:128 * b0 + w], k == 0, k == 1) for k in range(2)], t1, *fp)
                    a = op("scalar", (lambda m, ps: lambda e: e.activation(h[:, m, 0:w], ps[:, 0:w], ACT.Gelu, bias=b1e[:, e_, m:m + 1]))(m, ps), pe, *fh)
                    rp.free(kp, a)
                yield
                for i in range(nb):
                    b = b0 + i
                    kp, ps, fp = rp.get()
                    pe = op("tensor", [mm(ps[:, 0:256], h[:, k, 128 * i:128 * i + 128], w2[:, k, :], k == 0, k == 1) for k in range(2)], a, t2, *fp)
                    v = op("vector", stt(X[:, b, :], ps[:, 0:256], COMB[:, b, e_:e_ + 1], X[:, b, :], ALU.mult, ALU.add), pe)
                    rp.free(kp, v)
                rh.free(kh, pe)

            pipeline(group(b0, nb) for b0, nb in groups)
            W1e.free(k1, Q.last("tensor"))
            W2e.free(k2, Q.last("tensor"))
        v = Q.last("vector")
        if debug is not None and debug == 1:
            return finish(nc, ctx, Q, X, out, slots)
        Q.op("vector", lambda e: e.memset(BN[:, 0, 0:1], 0.0), v)
        stats()
        Q.barrier("t1", *wslots)

        rstd()
        AR.reset()
        XT = AR.take(2, NP)
        WA = AR.take(2, 264)
        Wq = AR.take(2, 768)
        bq = AR.take(768)
        Wo = AR.take(2, 256)
        bo = AR.take(256)
        L = Loader()
        L.load(WA[:, :, 0:256], A["gW1T"].rearrange("(k p) n -> p k n", p=128))
        L.load(Wq[:, :, :], A["L1_mix_W_qkv"].rearrange("(k p) n -> p k n", p=128))
        L.load(bq[:, :], A["L1_mix_b_qkv"].partition_broadcast(128))
        L.load(Wo[:, :, :], A["L1_mix_W_out"].rearrange("(k p) n -> p k n", p=128))
        L.load(bo[:, :], A["L1_mix_b_out"].partition_broadcast(128))
        KV = AR.take(2, 256)
        mark = AR.at
        wa = att_columns(WA, 256, WA, A["ga_s1"], A["ga_d1"], 4, L)
        rp = Ring(banks[0:4])
        toks = transposed(lambda b, o: xn_of(o, b), XT, ring(3, 256), rp, Q.last("vector"))
        tables(XT, toks, WA, 4, D_z, D_as4, D_ad4, ring(4, 264), rp, wslots, wa)
        Q.barrier("mix1a", *slots, *wslots)

        AR.reset(mark)
        rp = Ring(banks[0:4])
        rkv, rsq = ring(4, 512), ring(4, 512)
        rs = ring(4, 8)
        acc = []

        def centered_square(kv, sq, sm, v, b):
            v = op("vector", lambda e: e.tensor_reduce(sm[:, 0:1], kv[:, 0:256], AX.X, ALU.add), v)
            v = chain(ts(sm[:, 0:1], sm[:, 0:1], -1.0 / 256, None, ALU.mult))
            a = op("scalar", lambda e: e.activation(sq[:, 0:256], kv[:, 0:256], ACT.Square, bias=sm[:, 0:1], accum_out=sm[:, 1:2]), v)
            op("vector", ts(sm[:, 2:3], sm[:, 1:2], 1e-7, None, ALU.add), a)
            return chain(lambda e: e.reciprocal(sm[:, 3:4], sm[:, 2:3]), ts(sq[:, 0:256], sq[:, 0:256], sm[:, 3:4], None, ALU.mult))

        def kv1(b):
            K = 128 if b < 48 else LAST
            kp, ps, fp = rp.get()
            pe = op("tensor", [mm(ps[:, 0:512], XT[:, k, 128 * b:128 * b + 128], Wq[:, k, 256:768], k == 0, k == 1) for k in range(2)], *fp)
            yield
            kk, kv, fk = rkv.get()
            kq, sq, fq = rsq.get()
            k3, sm, f3 = rs.get()
            v = op("vector", tt(kv[:, :], ps[:, :], bq[:, 256:768], ALU.add), pe, *fk)
            rp.free(kp, v)
            v = centered_square(kv, sq, sm, v, b) if not (fq or f3) else centered_square(kv, sq, sm, v, b)
            a = op("scalar", lambda e: e.activation(sq[:, 256:512], sq[:, 0:256], ACT.Square), v, *fq, *f3)
            rs.free(k3, a)
            yield
            pe = op("tensor", [mm(banks[4 + j][:, 0:256], sq[0:K, 128 * j:128 * j + 128], kv[0:K, 256:512], b == 0, b == NB - 1) for j in range(2)]
                    + [mm(banks[6 + j][:, 0:1], sq[0:K, 256 + 128 * j:384 + 128 * j], ones[0:K, 0:1], b == 0, b == NB - 1) for j in range(2)], v, a)
            rkv.free(kk, pe)
            rsq.free(kq, pe)
            acc.append(pe)

        pipeline(kv1(b) for b in range(NB))
        nm = AR.take(8)
        for j in range(2):
            a = op("scalar", (lambda j: lambda e: e.activation(nm[:, j:j + 1], banks[6 + j][:, 0:1], ACT.Sqrt))(j), acc[-1])
            op("vector", ts(nm[:, 2 + j:3 + j], nm[:, j:j + 1], 1e-12, None, ALU.max), a)
            chain((lambda j: lambda e: e.reciprocal(nm[:, 4 + j:5 + j], nm[:, 2 + j:3 + j]))(j),
                  ts(KV[:, j, :], banks[4 + j][:, 0:256], nm[:, 4 + j:5 + j], None, ALU.mult))
        Q.barrier("mix1b")

        AR.reset(mark)
        rp = Ring(banks[0:8])
        rq, rs = ring(4, 512), ring(4, 16)
        rsq, rT, rat, raT = ring(4, 512), ring(4, 256), ring(4, 256), ring(4, 256)

        def out1(b):
            kp, ps, fp = rp.get()
            xs = lambda k: XT[:, k, 128 * b:128 * b + 128]
            pe = op("tensor", [mm(ps[:, 0:256], xs(k), Wq[:, k, 0:256], k == 0, k == 1) for k in range(2)]
                    + [mm(ps[:, 256:512], xs(k), Wq[:, k, 512:768], k == 0, k == 1) for k in range(2)], *fp)
            yield
            kk, q, fk = rq.get()
            kq, sq, fq = rsq.get()
            k3, sm, f3 = rs.get()
            op("vector", tt(q[:, 0:256], ps[:, 0:256], bq[:, 0:256], ALU.add), pe, *fk, *fq, *f3)
            v = chain(tt(q[:, 256:512], ps[:, 256:512], bq[:, 512:768], ALU.add))
            rp.free(kp, v)
            v = centered_square(q, sq, sm, v, b)
            a = op("scalar", lambda e: e.activation(sq[:, 256:512], sq[:, 0:256], ACT.Square, accum_out=sm[:, 4:5]), v)
            a = op("scalar", lambda e: e.activation(sm[:, 5:6], sm[:, 4:5], ACT.Sqrt), a)
            op("vector", ts(sm[:, 6:7], sm[:, 5:6], 1e-12, None, ALU.max), a)
            v2 = chain(lambda e: e.reciprocal(sm[:, 7:8], sm[:, 6:7]), ts(sm[:, 8:9], sm[:, 7:8], float(N) ** -0.5, None, ALU.mult))
            kp, ps, fp = rp.get()
            pe = op("tensor", [tr(ps[:, 0:128], sq[:, 0:128]), tr(ps[:, 128:256], sq[:, 128:256])], v, *fp)
            rsq.free(kq, pe, a)
            yield
            kt, qT, ft = rT.get()
            a = op("scalar", copy_act(qT[:, :], ps[:, 0:256]), pe, *ft)
            rp.free(kp, a)
            kp, ps, fp = rp.get()
            pe = op("tensor", [mm(ps[:, 0:256], qT[:, 128 * j:128 * j + 128], KV[:, j, :], j == 0, j == 1) for j in range(2)], a, *fp)
            rT.free(kt, pe)
            yield
            ka, at, fa = rat.get()
            v = op("vector", stt(at[:, :], ps[:, 0:256], sm[:, 8:9], q[:, 256:512], ALU.mult, ALU.add), pe, v2, *fa)
            rp.free(kp, v)
            rs.free(k3, v)
            rq.free(kk, v)
            kp, ps, fp = rp.get()
            pe = op("tensor", [tr(ps[:, 0:128], at[:, 0:128]), tr(ps[:, 128:256], at[:, 128:256])], v, *fp)
            rat.free(ka, pe)
            yield
            kt, aT, ft = raT.get()
            a = op("scalar", copy_act(aT[:, :], ps[:, 0:256]), pe, *ft)
            rp.free(kp, a)
            kp, ps, fp = rp.get()
            pe = op("tensor", [mm(ps[:, 0:256], aT[:, 128 * k:128 * k + 128], Wo[:, k, :], k == 0, k == 1) for k in range(2)], a, *fp)
            raT.free(kt, pe)
            yield
            op("vector", tt(X[:, b, :], X[:, b, :], bo[:, :], ALU.add))
            v = op("vector", tt(X[:, b, :], X[:, b, :], ps[:, 0:256], ALU.add), pe, Q.last("vector"))
            rp.free(kp, v)

        pipeline(out1(b) for b in range(NB))
        Q.barrier("gnn1")
        Y, at = gnn(4, 32, 28, 0.01, D_z, D_as4, D_ad4, "g1")
        base_y = 7168 // 2 + 3584
        AR.reset(3584 + 3584)
        Y = AR.take(NB, 256)
        WA = AR.take(2, 258)
        L = Loader()
        L.load(WA[:, :, 0:256], A["gW2T"].rearrange("(k p) n -> p k n", p=128))
        wa = att_columns(WA, 256, WA, A["ga_s2"], A["ga_d2"], 1, L)
        t1 = ring(3, 256)
        t2 = ring(3, 256)
        tT = ring(3, 2, 128)
        ro = ring(4, 258)
        rp = Ring(banks[0:8])

        def z2_tile(b):
            k1, u, f1 = t1.get()
            v = op("vector", ts(u[:, :], Y[:, b, :], 0.0, None, ALU.min), *f1, wa)
            a = op("scalar", lambda e: e.activation(u[:, :], u[:, :], ACT.Exp), v)
            yield
            k2, h, f2 = t2.get()
            op("vector", ts(u[:, :], u[:, :], -1.0, None, ALU.add), a)
            v = op("vector", stt(h[:, :], Y[:, b, :], 0.0, u[:, :], ALU.max, ALU.add), Q.last("vector"), *f2)
            t1.free(k1, v)
            kp, ps, fp = rp.get()
            pe = op("tensor", [tr(ps[:, 0:128], h[:, 0:128]), tr(ps[:, 128:256], h[:, 128:256])], v, *fp)
            t2.free(k2, pe)
            yield
            kt, hT, ft = tT.get()
            a = op("scalar", copy_act(hT[:, :, :], ps[:, 0:256].rearrange("p (k t) -> p k t", k=2)), pe, *ft)
            rp.free(kp, a)
            kp, ps, fp = rp.get()
            pe = op("tensor", [mm(ps[:, 0:258], hT[:, k, :], WA[:, k, :], k == 0, k == 1) for k in range(2)], a, *fp)
            tT.free(kt, pe)
            yield
            ko, o, fo = ro.get()
            a = op("scalar", copy_act(o[:, 0:258], ps[:, 0:258]), pe, *fo)
            rp.free(kp, a)
            s = wslots[b % 4]
            rows = slice(128 * b, 128 * b + 128)
            t = [dma("sync", s, lambda e: e.dma_start(D_z2[rows, :], o[:, 0:256]), a),
                 dma("sync", s, lambda e: e.dma_start(D_as1[rows, :], o[:, 256:257]), a),
                 dma("sync", s, lambda e: e.dma_start(D_ad1[rows, :], o[:, 257:258]), a)]
            ro.free(ko, t[-1])

        pipeline(z2_tile(b) for b in range(NB))
        Q.barrier("gnn2", *slots, *wslots)
        Y, at = gnn(1, 128, 7, 0.01, D_z2, D_as1, D_ad1, "g2")
        for b in range(NB):
            op("vector", tt(X[:, b, :], X[:, b, :], Y[:, b, :], ALU.add))
        if debug is not None and debug == 2:
            return finish(nc, ctx, Q, X, out, slots)
        Q.op("vector", lambda e: e.memset(BN[:, 0, 0:1], 0.0), Q.last("vector"))
        stats()
        Q.barrier("ffn1")

        rstd()
        AR.reset()
        Wd = AR.take(8, 8, 256)
        W1 = AR.take(2, 1024)
        Wg = AR.take(8, 8)
        b1 = AR.take(8)
        bgb = AR.take(8)
        bd = AR.take(256)
        L = Loader()
        L.load(W1[:, :, :], A["L1_ffn_W1"].rearrange("(k p) n -> p k n", p=128))
        L.load(Wg[:, :, :], A["L1_ffn_Wg"].rearrange("(m p) n -> p m n", p=128))
        L.load(b1[:, :], A["L1_ffn_b1"].rearrange("(m p) -> p m", p=128))
        L.load(bgb[:, :], A["L1_ffn_bg"].partition_broadcast(128))
        L.load(bd[0:8, :], A["L1_ffn_bd"])
        for e_ in range(8):
            L.load(Wd[:, :, e_, :], A["L1_ffn_Wd"][e_].rearrange("(m p) n -> p m n", p=128))
        rxt = ring(1, 2, 512)
        rH = ring(1, 8, 512)
        rx = ring(2, 256)
        sm = ring(4, 32)
        rc = ring(2, 128)
        rl = ring(2, 8)
        rp = Ring(banks[0:8])

        def ffn1(b0, nb):
            w = 128 * nb
            kX, xt, fX = rxt.get()
            for i in range(nb):
                k, x_, fx = rx.get()
                v = op("vector", xn_of(x_[:, :], b0 + i), *fx, Q.last("vector"))
                kp, ps, fp = rp.get()
                pe = op("tensor", [tr(ps[:, 0:128], x_[:, 0:128]), tr(ps[:, 128:256], x_[:, 128:256])], v, *fp)
                rx.free(k, pe)
                a = op("scalar", copy_act(xt[:, :, 128 * i:128 * i + 128], ps[:, 0:256].rearrange("p (k t) -> p k t", k=2)), pe, *fX)
                rp.free(kp, a)
            kH, h, fH = rH.get()
            for m in range(8):
                kp, ps, fp = rp.get()
                pe = op("tensor", [mm(ps[:, 0:w], W1[:, k, 128 * m:128 * m + 128], xt[:, k, 0:w], k == 0, k == 1) for k in range(2)], a, *L.toks, *fp)
                a2 = op("scalar", (lambda m, ps: lambda e: e.activation(h[:, m, 0:w], ps[:, 0:w], ACT.Gelu, bias=b1[:, m:m + 1]))(m, ps), pe, *fH)
                rp.free(kp, a2)
            rxt.free(kX, pe)
            for i in range(nb):
                b = b0 + i
                hs = lambda m: h[:, m, 128 * i:128 * i + 128]
                kp, ps, fp = rp.get()
                pe = op("tensor", [mm(ps[:, 0:8], hs(m), Wg[:, m, :], m == 0, m == 7) for m in range(8)], a2, *fp)
                k, s_, fs = sm.get()
                kl, l_, fl = rl.get()
                v = op("vector", tt(l_[:, :], ps[:, 0:8], bgb[:, :], ALU.add), pe, *fl, *fs)
                rp.free(kp, v)
                v, a = softmax8(l_[:, :], s_, v)
                rl.free(kl, a)
                iu = s_[:, 24:32].bitcast(U32)
                v = chain(top8(s_[:, 16:24], s_[:, 0:8]), top8_at(iu, s_[:, 16:24], s_[:, 0:8]),
                          cp(s_[:, 12:13], iu[:, 0:1]),
                          ts(s_[:, 0:8], iota8[:, :], s_[:, 12:13], s_[:, 16:17], ALU.is_equal, ALU.mult))
                for q in range(4):
                    kp, ps, fp = rp.get()
                    pe = op("tensor", [mm(ps[:, :], hs(m), Wd[:, m, 2 * q:2 * q + 2, :], m == 0, m == 7) for m in range(8)], *fp)
                    for r in range(2):
                        e_ = 2 * q + r
                        v = op("vector", stt(X[:, b, :], ps[:, 256 * r:256 * r + 256], s_[:, e_:e_ + 1], X[:, b, :], ALU.mult, ALU.add), pe, v)
                    rp.free(kp, v)
                kp, ps, fp = rp.get()
                pe = op("tensor", tr(ps[0:8, 0:128], s_[:, 0:8]), v, *fp)
                kc, c_, fc = rc.get()
                a = op("scalar", copy_act(c_[0:8, :], ps[0:8, 0:128]), pe, *fc)
                rp.free(kp, a)
                sm.free(k, pe, v)
                kp, ps, fp = rp.get()
                pe = op("tensor", mm(ps[:, 0:256], c_[0:8, :], bd[0:8, :]), a, *fp)
                rc.free(kc, pe)
                v = op("vector", tt(X[:, b, :], X[:, b, :], ps[:, 0:256], ALU.add), pe, v)
                rp.free(kp, v)
            rH.free(kH, pe)

        for b0, nb in groups:
            ffn1(b0, nb)
        finish(nc, ctx, Q, X, out, slots)


def finish(nc, ctx, Q, X, out, slots):
    v = Q.last("vector")
    s = slots[0]
    Q.dma("sync", s, lambda e: e.dma_start(out[0:6144, :].rearrange("(b p) f -> p b f", p=128), X[:, 0:48, :]), v, (s.sem, s.n))
    t = Q.dma("sync", slots[1], lambda e: e.dma_start(out[6144:N, :], X[0:LAST, 48, :]), v, (slots[1].sem, slots[1].n))
    Q.q["sync"].append(([t, (s.sem, s.n)], [], None, 0))
    ctx.enter_context(nc.allow_non_contiguous_dma(reason="short columns of tables"))
    block = ctx.enter_context(nc.Block())

    @block.sync
    def _(e):
        Q.play("sync", e)

    @block.scalar
    def _(e):
        Q.play("scalar", e)

    @block.vector
    def _(e):
        Q.play("vector", e)

    @block.tensor
    def _(e):
        Q.play("tensor", e)

    @block.gpsimd
    def _(e):
        Q.play("gpsimd", e)


def kernel(debug=None, **inputs):
    import numpy as _np
    import concourse.bacc as _bacc
    from concourse import mybir as _mybir
    from concourse.bass_utils import run_bass_kernel_spmd as _run

    x = {k: _np.asarray(v) for k, v in inputs.items()}
    w1 = x["L1_gnn_W1"]
    arrays = {
        "x": x["x"], "src": x["src"], "dst": x["dst"],
        "gW0": x["L0_gnn_W"].reshape(256, 256),
        "ga_s0": x["L0_gnn_att_src"].reshape(256), "ga_d0": x["L0_gnn_att_dst"].reshape(256),
        "qkv0T": x["L0_mix_Wqkv"].T, "m0W1T": x["L0_mix_W1"].T, "m0W2T": x["L0_mix_W2"].T,
        "routerT": x["L0_ffn_router_w"].T,
        "gW1T": w1.reshape(256, 256).T,
        "ga_s1": x["L1_gnn_a1"][:, :64].reshape(256), "ga_d1": x["L1_gnn_a1"][:, 64:].reshape(256),
        "gW2T": x["L1_gnn_W2"].T,
        "ga_s2": x["L1_gnn_a2"][:256], "ga_d2": x["L1_gnn_a2"][256:],
    }
    for k in ("L0_gnn_bias", "L0_mix_ln1_g", "L0_mix_ln1_b", "L0_mix_b1", "L0_mix_b2", "L0_mix_ln2_g", "L0_mix_ln2_b",
              "L0_ffn_w1", "L0_ffn_b1", "L0_ffn_w2", "L0_ffn_b2", "L1_mix_W_qkv", "L1_mix_b_qkv", "L1_mix_W_out", "L1_mix_b_out",
              "L1_ffn_W1", "L1_ffn_b1", "L1_ffn_Wg", "L1_ffn_bg", "L1_ffn_Wd", "L1_ffn_bd"):
        arrays[k] = x[k]
    nc = _bacc.Bacc("TRN2", target_bir_lowering=False, num_devices=1)
    fed, args = {}, {}
    for k, v in arrays.items():
        v = _np.ascontiguousarray(v)
        fed[f"in_{k}"] = v
        args[k] = nc.dram_tensor(f"in_{k}", v.shape, _mybir.dt.from_np(v.dtype), kind="ExternalInput").ap()
    out = nc.dram_tensor("out_0", (N, 256), _mybir.dt.float32, kind="ExternalOutput").ap()
    program(nc, args, out, debug)
    r = _run(nc, [fed], core_ids=[0])
    return r.results[0]["out_0"]
```

```python
from contextlib import ExitStack

import numpy as np

import concourse.bass as bass
from concourse import mybir

F32 = mybir.dt.float32
I32 = mybir.dt.int32
U32 = mybir.dt.uint32
BF16 = mybir.dt.bfloat16
ALU = mybir.AluOpType
ACT = mybir.ActivationFunctionType
AX = mybir.AxisListType

N = 6250
NB = 49
NP = NB * 128
LAST = N - 48 * 128
E = 106250
NT = 832
NS = NT + 48
NSP = 896
NW = 37
BIG = 1e30
ENGINES = ("sync", "scalar", "vector", "tensor", "gpsimd")


class Queues:

    def __init__(self, nc, ctx):
        self.nc, self.ctx = nc, ctx
        self.q = {e: [] for e in ENGINES}
        self.n_sems = 0
        self.sem = {}
        self.count = {}
        self.dmas = []
        self.phase("p")

    def new_sem(self, name):
        self.n_sems += 1
        return self.ctx.enter_context(self.nc.semaphore(f"{name}_{self.n_sems}"))

    def phase(self, name, engines=ENGINES):
        for e in engines:
            self.sem[e] = self.new_sem(f"{name}_{e}")
            self.count[e] = 0

    def op(self, eng, fns, *waits):
        if not isinstance(fns, (list, tuple)):
            fns = [fns]
        self.count[eng] += 1
        self.q[eng].append(([w for w in waits if w], fns, self.sem[eng], 1))
        return (self.sem[eng], self.count[eng])

    def free(self, eng, fn):
        self.q[eng].append(([], [fn], None, 0))

    def last(self, eng):
        return (self.sem[eng], self.count[eng]) if self.count[eng] else None

    def dma(self, eng, slot, fn, *waits):
        slot.n += 16
        self.q[eng].append(([w for w in waits if w], [fn], slot.sem, 16))
        return (slot.sem, slot.n)

    def barrier(self, name, *slots, pool=True):
        engines = ENGINES if pool else ENGINES[:-1]
        marks = [self.last(e) for e in engines] + [(s.sem, s.n) for s in slots if s.n]
        for e in engines:
            self.q[e].append(([m for m in marks if m], [], None, 0))
        self.phase(name, engines)

    def play(self, eng, e):
        seen = {}
        for waits, fns, sem, inc in self.q[eng]:
            for s, v in waits:
                if seen.get(id(s), 0) < v:
                    e.wait_ge(s, v)
                    seen[id(s)] = v
            for f in fns:
                r = f(e)
            if inc:
                r.then_inc(sem, inc)


class Slot:

    def __init__(self, Q, name):
        self.sem, self.n = Q.new_sem(name), 0


class Ring:

    def __init__(self, aps):
        self.aps, self.i = aps, 0
        self.freed = [() for _ in aps]

    def get(self):
        k = self.i % len(self.aps)
        self.i += 1
        assert self.freed[k] is not None, "a buffer is still in use"
        w, self.freed[k] = self.freed[k], None
        return k, self.aps[k], w

    def free(self, k, *tokens):
        self.freed[k] = tokens


def pipeline(gens):
    gens, live = list(gens), []
    while gens or live:
        if gens:
            live.append(gens.pop(0))
        for g in list(live):
            try:
                next(g)
            except StopIteration:
                live.remove(g)


class Arena:
    def __init__(self, t, size):
        self.t, self.size, self.at = t, size, 0

    def reset(self, at=0):
        self.at = at

    def take(self, *shape, dt=F32):
        n = int(np.prod(shape))
        words = n if dt in (F32, I32, U32) else (n + 1) // 2
        words += words % 2
        assert self.at + words <= self.size, (self.at, words, self.size)
        v = self.t[:, self.at:self.at + words]
        self.at += words
        if dt != F32:
            v = v.bitcast(dt)
        v = v[:, 0:n]
        if len(shape) == 2:
            v = v.rearrange("p (a b) -> p a b", b=shape[1])
        elif len(shape) == 3:
            v = v.rearrange("p (a b c) -> p a b c", b=shape[1], c=shape[2])
        return v


def program(nc, A, out, debug=None):
    ctx = ExitStack()
    with ctx:
        def sb(name, shape, dt=F32):
            return ctx.enter_context(nc.sbuf_tensor(name, shape, dt))

        Q = Queues(nc, ctx)
        op, dma = Q.op, Q.dma
        X = sb("X", [128, NB, 256])
        ART = sb("AR", [128, 33500])
        AR = Arena(ART, 33500)
        ident = sb("ident", [128, 128])
        iota_n = sb("iota_n", [128, 128])
        iota8 = sb("iota8", [128, 8])
        ones = sb("ones", [128, 8])
        hmask = sb("hmask", [128, 132])
        eps = sb("eps", [128, 1])
        REL = sb("REL", [128, NSP])
        SRCI = sb("SRCI", [128, NSP], I32)
        HI = sb("HI", [128, NSP])
        WORDS = sb("WORDS", [1, NW], I32)
        iota_p = sb("iota_p", [128, 1])
        ADS = sb("ADS", [128, NB * 8])
        ASS = sb("ASS", [128, NB])
        FAX = sb("FAX", [128, 392])
        rows4 = sb("rows4", [1, 4, 128])
        MV = sb("MV", [128, NB, 2])
        RS = sb("RS", [128, NB])
        BN = sb("BN", [128, 8, 6])
        banks = [ctx.enter_context(nc.psum_tensor(f"ps{i}", [128, 512], F32)) for i in range(8)]

        def scratch(name, shape, dt=F32):
            return nc.dram_tensor(name, shape, dt, kind="Internal").ap()

        D_se = scratch("D_se", (NT, 128), I32)
        D_de = scratch("D_de", (NT, 128), I32)
        D_b = scratch("D_b", (7, 128), I32)
        D_rel = scratch("D_rel", (NSP, 128))
        D_lo = scratch("D_lo", (NSP, 128))
        D_key = scratch("D_key", (NSP * 128 + 2, 1))
        D_h = scratch("D_h", (NP, 256))
        D_as8 = scratch("D_as8", (NP, 8))
        D_z = scratch("D_z", (NP, 256))
        D_as4 = scratch("D_as4", (NP, 4))
        D_z2 = scratch("D_z2", (NP, 256))
        

        slots = [Slot(Q, f"d{i}") for i in range(12)]
        wslots = [Slot(Q, f"w{i}") for i in range(4)]
        D_xt = scratch("D_xt", (NP, 260))
        D_idx = scratch("D_idx", (NP, 1), I32)
        oslot8 = [Slot(Q, f"o{i}") for i in range(8)]
        ARK = sb("ARK", [128, 256])
        O0 = sb("O0", [128, NB])
        gslots = [Slot(Q, f"g{i}") for i in range(12)]

        def copy_act(o, i):
            return lambda e: e.activation(o, i, ACT.Copy)

        def tt(o, a, b, f):
            return lambda e: e.tensor_tensor(o, a, b, f)

        def ts(o, a, s1, s2, f1, f2=None):
            if f2 is None:
                return lambda e: e.tensor_scalar(o, a, s1, None, f1)
            return lambda e: e.tensor_scalar(o, a, s1, s2, f1, f2)

        def stt(o, a, s, b, f1, f2):
            return lambda e: e.scalar_tensor_tensor(out=o, in0=a, scalar=s, in1=b, op0=f1, op1=f2)

        def rcp(o, i):
            return lambda e: e.reciprocal(o, i)

        def top8(o, i):
            return lambda e: e.max(o, i)

        def top8_at(o, v, i):
            return lambda e: e.max_index(o, v, i)

        def gelu(o, i, b):
            return lambda e: e.activation(o, i, ACT.Gelu, bias=b)

        def cp(o, i):
            return lambda e: e.tensor_copy(o, i)

        def mm(o, l, r, start=True, stop=True):
            return lambda e: e.matmul(o, l, r, start=start, stop=stop)

        def tr(o, i, k=128):
            return lambda e: e.transpose(o, i, ident[0:k, 0:k])

        def chain(*fns):
            t = None
            for f in fns:
                t = op("vector", f, Q.last("vector"))
            return t

        class Loader:

            def __init__(self):
                self.toks = []

            def load(self, o, i):
                s = slots[len(self.toks) % len(slots)]
                self.toks.append(dma("sync", s, lambda e: e.dma_start(o, i), (s.sem, s.n) if s.n else None))
                return self.toks[-1]

        L = Loader()
        w_edge = [dma("sync", slots[0], lambda e: e.dma_start(D_se.rearrange("t e -> (t e)")[0:E].rearrange("(a b) -> a b", a=10), A["src"].rearrange("(a b) -> a b", a=10))),
                  dma("sync", slots[1], lambda e: e.dma_start(D_de.rearrange("t e -> (t e)")[0:E].rearrange("(a b) -> a b", a=10), A["dst"].rearrange("(a b) -> a b", a=10)))]
        m0 = op("vector", lambda e: e.memset(X[:, NB - 1, :], 0.0))
        wx = [dma("sync", slots[2], lambda e: e.dma_start(X[:, 0:48, :], A["x"][0:6144, :].rearrange("(b p) f -> p b f", p=128))),
              dma("sync", slots[3], lambda e: e.dma_start(X[0:LAST, 48, :], A["x"][6144:N, :]), m0)]
        AR.reset()
        padi = AR.take(2, 246, dt=I32)
        sval = AR.take(7)
        gi = AR.take(NT, dt=I32)
        gf = AR.take(NT)
        it = AR.take(NT)
        gb = AR.take(NT)
        gm = AR.take(NT)
        cnt = AR.take(7)
        tsf = AR.take(7)
        tsi = AR.take(7, dt=I32)
        bsf = AR.take(7)
        bsi = AR.take(7, dt=I32)
        b128 = AR.take(7)
        guard = AR.take(2)
        seven = AR.take(8)
        di = AR.take(7, 128, dt=I32)
        si = AR.take(7, 128, dt=I32)
        df = AR.take(7, 128)
        sf = AR.take(7, 128)
        rel = AR.take(7, 128)
        key = AR.take(7, 128)
        vm = AR.take(7, 128)
        hi_, lo_ = AR.take(7, 128, dt=I32), AR.take(7, 128, dt=I32)
        hf, lf = AR.take(7, 128), AR.take(7, 128)
        bi, bf, dl, pw, wf = AR.take(NSP + 2, dt=I32), AR.take(NSP + 2), AR.take(NW * 24), AR.take(NW * 24), AR.take(NW)

        c1 = op("gpsimd", [lambda e: e.memset(ident[:, :], 0.0), lambda e: e.memset(padi[:, 0, :], 0),
                           lambda e: e.memset(padi[:, 1, :], NP - 1), lambda e: e.memset(eps[:, :], 1e-5),
                           lambda e: e.memset(ones[:, :], 1.0), lambda e: e.memset(guard[:, :], -7.0),])
        op("vector", lambda e: e.memset(hmask[:, :], 0.0))
        op("vector", [(lambda h: lambda e: e.memset(hmask[32 * h:32 * h + 32, 32 * h:32 * h + 32], 1.0))(h) for h in range(4)]
           + [(lambda h: lambda e: e.memset(hmask[32 * h:32 * h + 32, 128 + h:129 + h], 1.0))(h) for h in range(4)], Q.last("vector"))
        c2 = op("gpsimd", [lambda e: e.affine_select(out=ident[:, :], in_=ident[:, :], compare_op=ALU.not_equal, fill=1.0, base=0, pattern=[[-1, 128]], channel_multiplier=1)]
                + [lambda e: e.iota(iota_n[:, :], pattern=[[1, 128]], base=0, channel_multiplier=0, allow_small_or_imprecise_dtypes=True),
                   lambda e: e.iota(iota_p[:, :], pattern=[[0, 1]], base=0, channel_multiplier=1, allow_small_or_imprecise_dtypes=True),
                   lambda e: e.iota(iota8[:, :], pattern=[[1, 8]], base=0, channel_multiplier=0, allow_small_or_imprecise_dtypes=True),
                   lambda e: e.iota(sval[:, :], pattern=[[128, 7]], base=0, channel_multiplier=1, allow_small_or_imprecise_dtypes=True),
                   lambda e: e.iota(it[:, :], pattern=[[1, NT]], base=0, channel_multiplier=0, allow_small_or_imprecise_dtypes=True)], c1)
        w_edge += [dma("sync", slots[4], lambda e: e.dma_start(D_se.rearrange("t e -> (t e)")[E:NT * 128].unsqueeze(0), padi[0:1, 0, :]), c1),
                   dma("sync", slots[5], lambda e: e.dma_start(D_de.rearrange("t e -> (t e)")[E:NT * 128].unsqueeze(0), padi[0:1, 1, :]), c1),
                   dma("sync", slots[6], lambda e: e.dma_start(D_key[0:1, :], guard[0:1, 0:1]), c1),
                   dma("sync", slots[7], lambda e: e.dma_start(D_key[NSP * 128 + 1:NSP * 128 + 2, :], guard[0:1, 0:1]), c1)]
        wg = dma("sync", slots[8], lambda e: e.dma_start(gi[0:1, :], D_de[:, 127:128].rearrange("t a -> a t")), *w_edge)
        op("vector", lambda e: e.tensor_scalar(gi[0:1, :], gi[0:1, :], 7, None, ALU.logical_shift_right), wg, c2)
        g = chain(cp(gf[0:1, :], gi[0:1, :]), tt(gf[0:1, :], gf[0:1, :], it[0:1, :], ALU.add),
                  cp(seven[0:1, :], ones[0:1, :]))
        onesrow = iota_n
        orow = AR.take(128)
        g = op("vector", lambda e: e.memset(orow[:, :], 1.0), g)
        p = op("tensor", [mm(banks[0][:, 0:416], orow[0:1, :], gf[0:1, 0:416]), mm(banks[1][:, 0:416], orow[0:1, :], gf[0:1, 416:832])], g)
        op("vector", [cp(gb[:, 0:416], banks[0][:, 0:416]), cp(gb[:, 416:832], banks[1][:, 0:416])], p)
        for j in range(7):
            chain(ts(gm[:, :], gb[:, :], sval[:, j:j + 1], None, ALU.is_lt),
                  (lambda j: lambda e: e.tensor_reduce(cnt[:, j:j + 1], gm[:, :], AX.X, ALU.add))(j))
        t = chain(ts(tsf[:, :], cnt[:, :], float(NT - 1), None, ALU.min), cp(tsi[:, :], tsf[:, :]),
                  tt(bsf[:, :], sval[:, :], cnt[:, :], ALU.subtract), cp(bsi[:, :], bsf[:, :]),
                  ts(b128[:, :], bsf[:, :], 128.0, None, ALU.mult))
        wb = dma("sync", slots[9], lambda e: e.dma_start(D_b.rearrange("j p -> p j"), bsi[:, :]), t)
        wb = dma("sync", slots[10], lambda e: e.dma_start(bi[0:1, 1:NSP + 1], D_b.rearrange("j p -> (j p)").unsqueeze(0)), wb)
        wp = dma("sync", slots[11], lambda e: e.dma_start(pw[0:1, :], A["pow2"].unsqueeze(0)))
        op("vector", cp(bf[0:1, 1:NSP + 1], bi[0:1, 1:NSP + 1]), wb)
        op("vector", lambda e: e.memset(bf[0:1, 0:1], 0.0))
        op("vector", tt(dl[0:1, :], bf[0:1, 1:NW * 24 + 1], bf[0:1, 0:NW * 24], ALU.subtract), Q.last("vector"), wp)
        chain(tt(dl[0:1, :], dl[0:1, :], pw[0:1, :], ALU.mult),
              lambda e: e.tensor_reduce(wf[0:1, :], dl[0:1, :].rearrange("p (w i) -> p w i", i=24), AX.X, ALU.add),
              cp(WORDS[0:1, :], wf[0:1, :]))
        for j in range(7):
            a = dma("gpsimd", gslots[0], (lambda j: lambda e: e.indirect_dma_start(
                out=di[:, j, :], out_offset=None, in_=D_de, in_offset=bass.IndirectOffsetOnAxis(ap=tsi[:, j:j + 1], axis=0)))(j), t, (gslots[0].sem, gslots[0].n), *w_edge)
            b = dma("gpsimd", gslots[1], (lambda j: lambda e: e.indirect_dma_start(
                out=si[:, j, :], out_offset=None, in_=D_se, in_offset=bass.IndirectOffsetOnAxis(ap=tsi[:, j:j + 1], axis=0)))(j), t, (gslots[1].sem, gslots[1].n))
            op("vector", cp(df[:, j, :], di[:, j, :]), a)
            u = chain(ts(rel[:, j, :], df[:, j, :], b128[:, j:j + 1], None, ALU.subtract))
            v = op("vector", cp(sf[:, j, :], si[:, j, :]), b)
            op("vector", ts(hi_[:, j, :], si[:, j, :], 7, None, ALU.logical_shift_right))
            op("vector", ts(lo_[:, j, :], si[:, j, :], 127, None, ALU.bitwise_and))
            op("vector", [cp(hf[:, j, :], hi_[:, j, :]), cp(lf[:, j, :], lo_[:, j, :])], Q.last("vector"))
            k = chain(ts(vm[:, j, :], rel[:, j, :], -0.5, None, ALU.is_gt),
                      stt(vm[:, j, :], rel[:, j, :], 127.5, vm[:, j, :], ALU.is_lt, ALU.mult),
                      stt(key[:, j, :], df[:, j, :], 1.0, vm[:, j, :], ALU.add, ALU.mult),
                      ts(key[:, j, :], key[:, j, :], -1.0, None, ALU.add))
            dma("sync", slots[0], (lambda j: lambda e: e.dma_start(
                D_key[1 + j * 16384:1 + (j + 1) * 16384, :].rearrange("(s e) a -> s (e a)", e=128), key[:, j, :]))(j), k, (slots[0].sem, slots[0].n))
            for q, D_t, T in ((2, D_rel, rel), (3, D_lo, lf)):
                dma("sync", slots[q], (lambda D_t, T, j: lambda e: e.dma_start(D_t[128 * j:128 * j + 128, :], T[:, j, :]))(D_t, T, j), k, (slots[q].sem, slots[q].n))
            c = slice(128 * j, 128 * j + 128)
            pe = op("tensor", [tr(banks[2][:, 0:128], rel[:, j, :]), tr(banks[2][:, 128:256], sf[:, j, :]), tr(banks[2][:, 256:384], hf[:, j, :])], k, v)
            op("vector", [cp(REL[:, c], banks[2][:, 0:128]), cp(SRCI[:, c], banks[2][:, 128:256]), cp(HI[:, c], banks[2][:, 256:384])], pe)
        for b in range(NB):
            op("vector", (lambda b: lambda e: e.bn_stats(BN[:, b % 8, :], X[:, b, :]))(b), wx[0] if b < 48 else wx[1], wx[1], Q.last("vector"))
            op("vector", (lambda b: lambda e: e.bn_aggr(MV[:, b, :], BN[:, b % 8, :]))(b), Q.last("vector"))
        Q.barrier("t0", *slots, *gslots)

        def stats():
            for b in range(NB):
                op("vector", (lambda b: lambda e: e.bn_stats(BN[:, b % 8, :], X[:, b, :]))(b), Q.last("vector"))
                op("vector", (lambda b: lambda e: e.bn_aggr(MV[:, b, :], BN[:, b % 8, :]))(b), Q.last("vector"))

        def rstd():
            a = op("scalar", lambda e: e.activation(RS[:, :], MV[:, :, 1], ACT.Sqrt, bias=eps[:, 0:1]), Q.last("vector"))
            return op("vector", lambda e: e.reciprocal(RS[:, :], RS[:, :]), a)

        def ring(n, *shape):
            return Ring([AR.take(*shape) for _ in range(n)])

        def xn_of(o, b):
            return ts(o, X[:, b, :], MV[:, b, 0:1], RS[:, b:b + 1], ALU.subtract, ALU.mult)

        def transposed(src_of, dstT, r_x, r_ps, *w):
            toks = [None] * NB

            def one(b):
                k, xt, fw = r_x.get()
                v = op("vector", src_of(b, xt), *fw, *w)
                yield
                kp, ps, fp = r_ps.get()
                pe = op("tensor", [tr(ps[:, 0:128], xt[:, 0:128]), tr(ps[:, 128:256], xt[:, 128:256])], v, *fp)
                r_x.free(k, pe)
                yield
                a = op("scalar", copy_act(dstT[:, :, 128 * b:128 * b + 128], ps[:, 0:256].rearrange("p (k t) -> p k t", k=2)), pe)
                r_ps.free(kp, a)
                toks[b] = a

            pipeline(one(b) for b in range(NB))
            return toks

        def att_columns(WA, base, W_view, a_src, a_dst, H, L):
            D = 256 // H
            tmp = AR.take(256)
            wb = AR.take(2, 256)
            t = [L.load(wb[:, 0, :], a_src.partition_broadcast(128)), L.load(wb[:, 1, :], a_dst.partition_broadcast(128))]
            r = None
            for k in range(2):
                for n in range(2):
                    op("vector", tt(tmp[:, :], W_view[:, k, 0:256], wb[:, n, :], ALU.mult), *L.toks, Q.last("vector"))
                    r = chain((lambda k, n: lambda e: e.tensor_reduce(WA[:, k, base + n * H:base + (n + 1) * H], tmp[:, :].rearrange("p (h d) -> p h d", h=H), AX.X, ALU.add))(k, n))
            return r

        def tables(XT, toks, WA, H, D_row, D_as, ADS, r_o, r_ps, wslots, *w):
            def one(b):
                kp, ps, fp = r_ps.get()
                pe = op("tensor", [mm(ps[:, 0:256 + 2 * H], XT[:, k, 128 * b:128 * b + 128], WA[:, k, 0:256 + 2 * H], k == 0, k == 1) for k in range(2)], toks[b], *w, *fp)
                yield
                ko, o, fo = r_o.get()
                a = op("scalar", [copy_act(o[:, 0:256 + H], ps[:, 0:256 + H]), copy_act(ADS[:, b * H:b * H + H], ps[:, 256 + H:256 + 2 * H])], pe, *fo)
                r_ps.free(kp, a)
                yield
                s = wslots[b % len(wslots)]
                rows = slice(128 * b, 128 * b + 128)
                t = [dma("sync", s, lambda e: e.dma_start(D_row[rows, :], o[:, 0:256]), a),
                     dma("sync", s, lambda e: e.dma_start(D_as[rows, :], o[:, 256:256 + H]), a)]
                r_o.free(ko, t[-1])

            pipeline(one(b) for b in range(NB))

        def ln_tile(src, dst, g, bb, sm, *w):
            op("vector", lambda e: e.bn_stats(sm[:, 0:6], src), *w, Q.last("vector"))
            v = chain(lambda e: e.bn_aggr(sm[:, 6:8], sm[:, 0:6]))
            yield v
            a = op("scalar", lambda e: e.activation(sm[:, 8:9], sm[:, 7:8], ACT.Sqrt, bias=eps[:, 0:1]), v)
            yield a
            op("vector", lambda e: e.reciprocal(sm[:, 9:10], sm[:, 8:9]), a)
            v = chain(ts(dst, src, sm[:, 6:7], sm[:, 9:10], ALU.subtract, ALU.mult),
                      tt(dst, dst, g, ALU.mult), tt(dst, dst, bb, ALU.add))
            yield v

        regs = {}

        def block_of(e, name, s, scale, words=None, most=48):
            words = WORDS if words is None else words
            if name not in regs:
                regs[name] = [e.alloc_register(f"{name}_{r}") for r in ("at", "word", "bit")]
            at_, word, bit = regs[name]
            if s == 0:
                e.reg_mov(at_, 0)
            if s % 24 == 0:
                e.reg_load(word, words[0:1, s // 24:s // 24 + 1])
            e.reg_alu(bit, word, 1, ALU.bitwise_and)
            e.reg_alu(word, word, 1, ALU.logical_shift_right)
            e.reg_mul(bit, bit, scale)
            e.reg_add(at_, at_, bit)
            return e.snap(at_, min_val=0, max_val=most * scale)

        EDGE = ART[:, 26332:33500]

        def place(H, C, J, s):
            return EDGE[:, (s % J * C + s // J) * H:(s % J * C + s // J + 1) * H]

        def gather_scores(H, C, J, D_as):
            for s in range(NSP):
                g = gslots[s % 12]
                dma("gpsimd", g, (lambda s: lambda e: e.indirect_dma_start(
                    out=place(H, C, J, s), out_offset=None, in_=D_as,
                    in_offset=bass.IndirectOffsetOnAxis(ap=SRCI[:, s:s + 1], axis=0)))(s))
            return [(g.sem, g.n) for g in gslots]

        def onehots(D_t, r_b, r_t, slot0, use):
            def one(q):
                kb, rb, fb = r_b.get()
                sl = slots[slot0 + q % len(r_b.aps)]
                w = dma("sync", sl, lambda e: e.dma_start(rb, D_t[8 * q:8 * q + 8, :].rearrange("s e -> (s e)").partition_broadcast(128)), *fb, (sl.sem, sl.n))
                yield
                kt, st, ft = r_t.get()
                v = op("vector", ts(st, rb, iota_p[:, 0:1], None, ALU.is_equal), w, *ft)
                r_b.free(kb, v)
                yield
                for i in range(8):
                    pe = use(8 * q + i, st[:, 128 * i:128 * i + 128], v)
                r_t.free(kt, pe)

            pipeline(one(q) for q in range(NSP // 8))

        def gnn(H, C, J, slope, D_row, name, gathered):
            W = J * 128
            assert C * H == 128 and C * J == NSP
            YW = 256 + H
            CH = 448 // (J * H)
            AR.reset()
            SC = AR.take(7168)
            ADV = SC[:, 0:NSP * H] if H > 1 else SC[:, 1024:1024 + NSP]
            B2 = AR.take(7170)
            at_ = AR.at
            r_b, r_t = ring(4, 1024), ring(2, 1024)
            AR.reset(at_)
            FA = AR.take(7168, dt=BF16)
            FB = AR.take(7168, dt=BF16)
            SC, B2w, FA, FB = SC[:, 0:W], B2[:, 0:W], FA[:, 0:W], FB[:, 0:W]
            B1 = EDGE[:, 0:W]
            E1 = EDGE[:, 0:NSP * H]
            sm = AR.take(8)
            row = rows4
            ad_by_chunk = ADV.rearrange("p (j c h) -> p c j h", j=J, h=H)
            by_chunk = E1.rearrange("p (j c h) -> p c j h", j=J, h=H)

            KW = B2[:, 0:W + 2]
            win = bass.AP(D_key.tensor, D_key.offset, [[W, C], [0, H], [1, W + 2]])
            wk = dma("sync", slots[8], lambda e: e.dma_start(KW, win))
            ASV = None
            if H == 1:
                ASV = SC
                mk = FAX
                r_p = Ring(banks[2:6])
                box = {}

                def use(s, st, v):
                    if s % 8 == 0:
                        box["k"], box["ps"], box["w"] = r_p.get()
                    ps = box["ps"]
                    pe = op("tensor", mm(ps[:, 49 * (s % 8):49 * (s % 8) + 49], st, ASS[:, :]), v, *box["w"])
                    if s % 8 == 7:
                        op("vector", tt(mk[:, :].rearrange("p (s b) -> p s b", b=49), iota_n[:, 0:49].unsqueeze(1).to_broadcast([128, 8, 49]),
                                        HI[:, s - 7:s + 1].unsqueeze(2).to_broadcast([128, 8, 49]), ALU.is_equal), Q.last("vector"))
                        op("vector", tt(mk[:, :], mk[:, :], ps[:, 0:392], ALU.mult), pe, Q.last("vector"))
                        v = chain((lambda s: lambda e: e.tensor_reduce(ASV[:, s - 7:s + 1], mk[:, :].rearrange("p (s b) -> p s b", b=49), AX.X, ALU.add))(s))
                        r_p.free(box["k"], v)
                    return pe

                onehots(D_lo, r_b, r_t, 0, use)

            r_p = Ring(banks[0:2])
            acc_ = {}

            def use2(s, st, v):
                i = s % (448 // H)
                if i == 0:
                    acc_["k"], acc_["ps"], acc_["w"] = r_p.get()
                ps = acc_["ps"]

                box = []
                if s < NS:
                    Q.free("tensor", lambda e: box.append(block_of(e, "pe", s, H)))

                def f(e):
                    if s < NS:
                        return e.matmul(ps[:, H * i:H * i + H], st, ADS[:, bass.ds(box[0], H)], start=True, stop=True)
                    return e.matmul(ps[:, H * i:H * i + H], st, ADS[:, 48 * H:49 * H], start=True, stop=True)

                pe = op("tensor", f, v, *acc_["w"])
                if i == 448 // H - 1:
                    c0 = s // (448 // H) * CH
                    a_ = op("scalar", copy_act(ad_by_chunk[:, c0:c0 + CH, :, :], ps[:, 0:448].rearrange("p (c j h) -> p c j h", j=J, h=H)), pe)
                    r_p.free(acc_["k"], a_)
                return pe

            onehots(D_rel, r_b, r_t, 4, use2)
            if H == 1:
                v = op("vector", tt(by_chunk[:, :, :, 0], ad_by_chunk[:, :, :, 0], ASV[:, 0:NSP].rearrange("p (c j) -> p c j", j=J), ALU.add), Q.last("scalar"), Q.last("vector"))
            else:
                v = op("vector", tt(E1, E1, ADV, ALU.add), *gathered, Q.last("scalar"))
            v = chain(stt(E1, E1, slope, E1, ALU.mult, ALU.max))

            rp = Ring(banks[0:6])
            for j0 in range(0, J, 4):
                nj = min(4, J - j0)
                kp, ps, fp = rp.get()
                pe = op("tensor", [tr(ps[:, 128 * i:128 * i + 128], E1[:, 128 * (j0 + i):128 * (j0 + i) + 128]) for i in range(nj)], v, *fp)
                a = op("scalar", copy_act(SC[:, 128 * j0:128 * (j0 + nj)], ps[:, 0:128 * nj]), pe)
                rp.free(kp, a)
            op("vector", tt(FA, KW[:, 1:W + 1], KW[:, 0:W], ALU.is_equal), wk, v, Q.last("tensor"))
            v = op("vector", tt(FB, KW[:, 1:W + 1], KW[:, 2:W + 2], ALU.is_equal))
            for F in (FA, FB):
                op("vector", ts(F, F, -1.0, BIG, ALU.add, ALU.mult), v)

            def segscan(o, x, F, rev):
                d = (lambda ap: ap[:, ::-1]) if rev else (lambda ap: ap)
                end = 0 if rev else W - 1
                scan = lambda init: (lambda e: e.tensor_tensor_scan(d(o), d(F), d(x), init, ALU.add, ALU.max))
                v = chain(lambda e: e.tensor_reduce(sm[:, 1:2], F, AX.X, ALU.min))
                op("vector", scan(-BIG), v, Q.last("scalar"))
                v = chain(cp(sm[:, 0:1], o[:, end:end + 1]))
                pe = op("tensor", [tr(banks[7][0:1, 0:128], sm[:, 0:1]), tr(banks[7][0:1, 128:256], sm[:, 1:2])], v)
                r = lambda i: row[0:1, i, :]
                op("vector", [cp(r(0).rearrange("p (h c) -> p h c", h=H), banks[7][0:1, 0:128].rearrange("p (c h) -> p h c", h=H)),
                              cp(r(1).rearrange("p (h c) -> p h c", h=H), banks[7][0:1, 128:256].rearrange("p (c h) -> p h c", h=H)),
                              lambda e: e.memset(r(3), -BIG)], pe)
                hc = r(2).rearrange("p (h c) -> p h c", h=H)
                ch = r(3).rearrange("p (c h) -> p h c", h=H)
                v = chain(lambda e: e.tensor_tensor_scan(d(r(2)), d(r(1)), d(r(0)), -BIG, ALU.add, ALU.max),
                          cp(ch[:, :, 0:C - 1], hc[:, :, 1:C]) if rev else cp(ch[:, :, 1:C], hc[:, :, 0:C - 1]))
                pe = op("tensor", mm(banks[7][:, 256:257], row[0:1, 3, :], ones[0:1, 0:1]), v)
                op("vector", cp(sm[:, 2:3], banks[7][:, 256:257]), pe)
                return chain(scan(sm[:, 2:3]))

            segscan(B1, SC, FA, False)
            segscan(B2w, B1, FB, True)
            v = chain(tt(SC, SC, B2w, ALU.subtract))
            a = op("scalar", lambda e: e.activation(SC, SC, ACT.Exp), v)
            for j0 in range(0, J, 4):
                nj = min(4, J - j0)
                kp, ps, fp = rp.get()
                pe = op("tensor", [tr(ps[:, 128 * i:128 * i + 128], SC[:, 128 * (j0 + i):128 * (j0 + i) + 128]) for i in range(nj)], a, *fp)
                a2 = op("scalar", copy_act(E1[:, 128 * j0:128 * (j0 + nj)], ps[:, 0:128 * nj]), pe)
                rp.free(kp, a2)
            Q.barrier(name + "b", *slots, *gslots)

            AR.reset()
            Yf = AR.take(NB * YW)
            G = ring(10, 256)
            M = ring(4, 256)
            S = ring(4, 128)
            rp = Ring(banks[0:8])
            state = {"y": op("vector", lambda e: e.memset(Yf, 0.0))}

            def step(s):
                kg, gt, fg = G.get()
                sl = gslots[s % 10]
                gk = dma("gpsimd", sl, lambda e: e.indirect_dma_start(
                    out=gt[:, :], out_offset=None, in_=D_row,
                    in_offset=bass.IndirectOffsetOnAxis(ap=SRCI[:, s:s + 1], axis=0)), *fg)
                for _ in range(6):
                    yield
                kS, st, fS = S.get()
                ee = place(H, C, J, s)
                if H == 1:
                    w = v = op("vector", ts(st[:, :], iota_n[:, :], REL[:, s:s + 1], ee, ALU.is_equal, ALU.mult), *fS)
                    mt, w, sums = gt, gk, ones[:, 0:1]
                else:
                    kM, mt, fM = M.get()
                    op("vector", ts(st[:, :], iota_n[:, :], REL[:, s:s + 1], None, ALU.is_equal), *fS)
                    w = v = op("vector", tt(mt[:, :].rearrange("p (h d) -> p h d", h=H), gt[:, :].rearrange("p (h d) -> p h d", h=H),
                                            ee.unsqueeze(2).to_broadcast([128, H, 256 // H]), ALU.mult), gk, *fM)
                    G.free(kg, v)
                    sums = ee
                kp, ps, fp = rp.get()
                pe = op("tensor", [mm(ps[:, 0:256], st[:, :], mt[:, :]), mm(ps[:, 256:YW], st[:, :], sums)], v, w, *fp)
                S.free(kS, pe)
                if H == 1:
                    G.free(kg, pe)
                else:
                    M.free(kM, pe)
                for _ in range(4):
                    yield
                box = []
                Q.free("vector", lambda e: box.append(block_of(e, "dve", s, YW)))

                def add(e):
                    o = Yf[:, bass.ds(box[0], YW)]
                    return e.tensor_tensor(o, ps[:, 0:YW], o, ALU.add)

                v = op("vector", add, pe, state["y"])
                state["y"] = v
                rp.free(kp, v)

            pipeline(step(s) for s in range(NS))
            Y = Yf.rearrange("p (b n) -> p b n", b=NB)
            den = AR.take(NB, H)
            v = chain(ts(den[:, :, :], Y[:, :, 256:YW], 1e-16, None, ALU.add), rcp(den[:, :, :], den[:, :, :]))
            for b in range(NB):
                v2 = op("vector", tt(Y[:, b, 0:256].rearrange("p (h d) -> p h d", h=H), Y[:, b, 0:256].rearrange("p (h d) -> p h d", h=H),
                                     den[:, b, :].unsqueeze(2).to_broadcast([128, H, 256 // H]), ALU.mult), v)
            Q.barrier(name + "c", *gslots)
            return Y[:, :, 0:256]

        rstd()
        AR.reset()
        XT = AR.take(2, NP)
        WA = AR.take(2, 272)
        Wkv = AR.take(2, 768)
        W1 = AR.take(2, 256)
        W2 = AR.take(2, 256)
        bcs = AR.take(5, 256)
        b1c = AR.take(2)
        KVB = AR.take(2, 132)
        L = Loader()
        L.load(WA[:, :, 0:256], A["gW0"].rearrange("(k p) n -> p k n", p=128))
        L.load(Wkv[:, :, :], A["qkv0T"].rearrange("(k p) n -> p k n", p=128))
        L.load(W1[:, :, :], A["m0W1T"].rearrange("(k p) n -> p k n", p=128))
        L.load(W2[:, :, :], A["m0W2T"].rearrange("(k p) n -> p k n", p=128))
        for i, n in enumerate(("L0_mix_ln1_g", "L0_mix_ln1_b", "L0_mix_b2", "L0_mix_ln2_g", "L0_mix_ln2_b")):
            L.load(bcs[:, i, :], A[n].partition_broadcast(128))
        L.load(b1c[:, :], A["L0_mix_b1"].rearrange("(k p) -> p k", p=128))
        mark = AR.at
        wa = att_columns(WA, 256, WA, A["ga_s0"], A["ga_d0"], 8, L)
        rp = Ring(banks[0:4])
        toks = transposed(lambda b, o: xn_of(o, b), XT, ring(3, 256), rp, Q.last("vector"))
        tables(XT, toks, WA, 8, D_h, D_as8, ADS, ring(4, 272), rp, wslots, wa)
        Q.barrier("mix0a", *slots, *wslots)
        gathered = gather_scores(8, 16, 56, D_as8)

        AR.reset(mark)
        rk, rv, re = ring(4, 256), ring(4, 2, 130), ring(4, 256)
        m1 = op("vector", [(lambda r: lambda e: e.memset(r[:, :, 128:130], 1.0))(r) for r in rv.aps])
        rp = Ring(banks[0:4])
        acc = []

        def kv_tile(b):
            K = 128 if b < 48 else LAST
            kp, ps, fp = rp.get()
            pe = op("tensor", [mm(ps[:, 0:512], XT[:, k, 128 * b:128 * b + 128], Wkv[:, k, 256:768], k == 0, k == 1) for k in range(2)], *fp)
            yield
            ke, e_, fe = re.get()
            kk, kt, fk = rk.get()
            kv, vt, fv = rv.get()
            v = op("vector", ts(e_[:, :], ps[:, 0:256], 0.0, None, ALU.min), pe, *fe)
            a2 = op("scalar", copy_act(vt[:, :, 0:128], ps[:, 256:512].rearrange("p (j n) -> p j n", j=2)), v, *fv, m1)
            a = op("scalar", lambda e: e.activation(e_[:, :], e_[:, :], ACT.Exp), v)
            yield
            v = op("vector", stt(kt[:, :], ps[:, 0:256], 0.0, e_[:, :], ALU.max, ALU.add), a, *fk)
            rp.free(kp, v, a2)
            re.free(ke, v)
            yield
            pe = op("tensor", [mm(banks[6 + j][:, 0:129], kt[0:K, 128 * j:128 * j + 128], vt[0:K, j, 0:129], b == 0, b == NB - 1) for j in range(2)], v, a2)
            rk.free(kk, pe)
            rv.free(kv, pe)
            acc.append(pe)

        pipeline(kv_tile(b) for b in range(NB))
        for j in range(2):
            op("vector", tt(KVB[:, j, 0:128], banks[6 + j][:, 0:128], hmask[:, 0:128], ALU.mult), acc[-1])
            chain(ts(KVB[:, j, 128:132], hmask[:, 128:132], banks[6 + j][:, 128:129], None, ALU.mult))
        Q.barrier("mix0b", pool=False)

        AR.reset(mark)
        groups = [(4 * g, 4) for g in range(12)] + [(48, 1)]
        rq, rqe = ring(2, 2, 512), ring(1, 2, 512)
        rx1T = rhT = None
        r1 = ring(5, 256)
        rt = ring(2, 256)
        rx1T = ring(1, 2, 512)
        rhT = ring(1, 2, 512)
        rsm = ring(4, 10)
        rz = ring(2, 8)
        rp = Ring(banks[0:8])

        def mix0_group(b0, nb):
            w = 128 * nb
            kq, qt, fq = rq.get()
            ke, qe, fe = rqe.get()
            vs = []
            for m in range(2):
                kp, ps, fp = rp.get()
                pe = op("tensor", [mm(ps[:, 0:w], Wkv[:, k, 128 * m:128 * m + 128], XT[:, k, 128 * b0:128 * b0 + w], k == 0, k == 1) for k in range(2)], *fp)
                v = op("vector", ts(qe[:, m, 0:w], ps[:, 0:w], 0.0, None, ALU.min), pe, *fe)
                a = op("scalar", (lambda m: lambda e: e.activation(qe[:, m, 0:w], qe[:, m, 0:w], ACT.Exp))(m), v)
                v = op("vector", stt(qt[:, m, 0:w], ps[:, 0:w], 0.0, qe[:, m, 0:w], ALU.max, ALU.add), a, *fq)
                rp.free(kp, v)
                vs.append(v)
            rqe.free(ke, v)
            sms, x1s = [], []
            for i in range(nb):
                b = b0 + i
                kp, ps, fp = rp.get()
                pe = op("tensor", [mm(ps[:, 132 * j:132 * j + 132], qt[:, j, 128 * i:128 * i + 128], KVB[:, j, :]) for j in range(2)], v, *fp)
                kt, t_, ft = rt.get()
                kz, z_, fz = rz.get()
                k1, x1, f1 = r1.get()
                ks, sm, fs = rsm.get()
                pv = ps[:, 0:264].rearrange("p (j n) -> p j n", j=2)
                op("vector", ts(z_[:, 0:8].rearrange("p (j h) -> p j h", j=2), pv[:, :, 128:132], 1e-6, None, ALU.add), pe, *fz, *ft, *f1, *fs)
                v1 = chain(rcp(z_[:, 0:8], z_[:, 0:8]),
                           tt(t_[:, :].rearrange("p (j h d) -> p j h d", j=2, h=4), pv[:, :, 0:128].rearrange("p j (h d) -> p j h d", h=4),
                              z_[:, 0:8].rearrange("p (j h) -> p j h", j=2).unsqueeze(3).to_broadcast([128, 2, 4, 32]), ALU.mult))
                rp.free(kp, v1)
                op("vector", xn_of(x1[:, :], b))
                v1 = chain(tt(x1[:, :], x1[:, :], t_[:, :], ALU.add))
                rt.free(kt, v1)
                rz.free(kz, v1)
                gen = ln_tile(x1[:, :], x1[:, :], bcs[:, 0, :], bcs[:, 1, :], sm, v1)
                next(gen)
                sms.append((ks, gen))
                x1s.append((k1, x1))
            rq.free(kq, pe)
            for _, g in sms:
                next(g)
            for ks, g in sms:
                v = next(g)
                rsm.free(ks, v)
            kT, x1T, fT = rx1T.get()
            for i in range(nb):
                x1 = x1s[i][1]
                kp, ps, fp = rp.get()
                pe = op("tensor", [tr(ps[:, 0:128], x1[:, 0:128]), tr(ps[:, 128:256], x1[:, 128:256])], v, *fp)
                a = op("scalar", copy_act(x1T[:, :, 128 * i:128 * i + 128], ps[:, 0:256].rearrange("p (k t) -> p k t", k=2)), pe, *fT)
                rp.free(kp, a)
            kh, hT, fh = rhT.get()
            for m in range(2):
                kp, ps, fp = rp.get()
                pe = op("tensor", [mm(ps[:, 0:w], W1[:, k, 128 * m:128 * m + 128], x1T[:, k, 0:w], k == 0, k == 1) for k in range(2)], a, *fp)
                a2 = op("scalar", (lambda m, ps: lambda e: e.activation(hT[:, m, 0:w], ps[:, 0:w], ACT.Gelu, bias=b1c[:, m:m + 1]))(m, ps), pe, *fh)
                rp.free(kp, a2)
            rx1T.free(kT, pe)
            sms = []
            for i in range(nb):
                k1, x1 = x1s[i]
                kp, ps, fp = rp.get()
                pe = op("tensor", [mm(ps[:, 0:256], hT[:, k, 128 * i:128 * i + 128], W2[:, k, :], k == 0, k == 1) for k in range(2)], a2, *fp)
                op("vector", tt(x1[:, :], x1[:, :], bcs[:, 2, :], ALU.add), a)
                v = op("vector", tt(x1[:, :], x1[:, :], ps[:, 0:256], ALU.add), pe, Q.last("vector"))
                rp.free(kp, v)
                ks, sm, fs = rsm.get()
                gen = ln_tile(x1[:, :], x1[:, :], bcs[:, 3, :], bcs[:, 4, :], sm, v, *fs)
                next(gen)
                sms.append((ks, gen))
            rhT.free(kh, pe)
            for _, g in sms:
                next(g)
            for i, (ks, g) in enumerate(sms):
                k1, x1 = x1s[i]
                v = next(g)
                rsm.free(ks, v)
                v = chain(tt(X[:, b0 + i, :], X[:, b0 + i, :], x1[:, :], ALU.add))
                r1.free(k1, v)

        for b0, nb in groups:
            mix0_group(b0, nb)
        Q.barrier("gnn0", pool=False)

        Y = gnn(8, 16, 56, 0.2, D_h, "g0", gathered)
        AR.reset(NB * 264)
        bg = AR.take(256)
        L = Loader()
        t = L.load(bg[:, :], A["L0_gnn_bias"].partition_broadcast(128))
        for b in range(NB):
            op("vector", tt(Y[:, b, :], Y[:, b, :], bg[:, :], ALU.add), t)
            chain(stt(X[:, b, :], Y[:, b, :], 0.0, X[:, b, :], ALU.max, ALU.add))
        v = Q.last("vector")
        if debug is not None and debug == 0:
            return finish(nc, ctx, Q, X, out, slots)
        stats()
        Q.barrier("ffn0", *slots)

        rstd()
        AR.reset()
        RW = AR.take(2, 8)
        W1e, W2e = ring(3, 2, 256), ring(3, 2, 256)
        b1e = AR.take(8, 2)
        b2e = AR.take(256)
        XT = AR.take(2, NP)
        OUT = AR.take(4, 256)
        L = Loader()
        L.load(RW[:, :, :], A["routerT"].rearrange("(k p) n -> p k n", p=128))
        L.load(b1e[:, :, :], A["L0_ffn_b1"].rearrange("e (k p) -> p e k", p=128))
        L.load(b2e[0:8, :], A["L0_ffn_b2"])
        rx = ring(3, 256)
        rp = Ring(banks[0:8])
        toks = transposed(lambda b, o: xn_of(o, b), XT, rx, rp, Q.last("vector"))
        sm = ring(4, 64)
        COMB = AR.take(NB, 8)
        ct = AR.take(2, 128)
        rc = Ring([ct[:, 0, :], ct[:, 1, :]])
        rh = ring(2, 2, 512)

        def softmax8(ps, s_, pe, *w):
            v = op("vector", lambda e: e.tensor_reduce(s_[:, 8:9], ps, AX.X, ALU.max), pe, *w)
            v = chain(ts(s_[:, 9:10], s_[:, 8:9], -1.0, None, ALU.mult))
            a = op("scalar", lambda e: e.activation(s_[:, 0:8], ps, ACT.Exp, bias=s_[:, 9:10], accum_out=s_[:, 10:11]), v)
            op("vector", lambda e: e.reciprocal(s_[:, 11:12], s_[:, 10:11]), a)
            return chain(ts(s_[:, 0:8], s_[:, 0:8], s_[:, 11:12], None, ALU.mult)), a

        def route(b):
            kp, ps, fp = rp.get()
            pe = op("tensor", [mm(ps[:, 0:8], XT[:, k, 128 * b:128 * b + 128], RW[:, k, :], k == 0, k == 1) for k in range(2)], toks[b], *L.toks, *fp)
            yield
            k, s_, fs = sm.get()
            v, a = softmax8(ps[:, 0:8], s_, pe, *fs)
            rp.free(kp, a)
            yield
            iu = s_[:, 24:32].bitcast(U32)
            v = chain(top8(s_[:, 16:24], s_[:, 0:8]), top8_at(iu, s_[:, 16:24], s_[:, 0:8]),
                      cp(s_[:, 32:40], iu), tt(s_[:, 40:41], s_[:, 16:17], s_[:, 17:18], ALU.add),
                      ts(s_[:, 40:41], s_[:, 40:41], 1e-12, None, ALU.max),
                      lambda e: e.reciprocal(s_[:, 41:42], s_[:, 40:41]),
                      ts(s_[:, 42:44], s_[:, 16:18], s_[:, 41:42], None, ALU.mult),
                      ts(s_[:, 48:56], iota8[:, :], s_[:, 32:33], s_[:, 42:43], ALU.is_equal, ALU.mult),
                      ts(s_[:, 56:64], iota8[:, :], s_[:, 33:34], s_[:, 43:44], ALU.is_equal, ALU.mult),
                      tt(COMB[:, b, :], s_[:, 48:56], s_[:, 56:64], ALU.add))
            sm.free(k, v)

        pipeline(route(b) for b in range(NB))
        Q.barrier("ffn0b", *slots)
        rp = Ring(banks[0:8])

        def base(b):
            kp, ps, fp = rp.get()
            pe = op("tensor", tr(ps[0:8, 0:128], COMB[:, b, :]), *fp)
            yield
            kc, c_, fc = rc.get()
            a = op("scalar", copy_act(c_[0:8, :], ps[0:8, 0:128]), pe, *fc)
            rp.free(kp, a)
            kp, ps, fp = rp.get()
            pe = op("tensor", mm(ps[:, 0:256], c_[0:8, :], b2e[0:8, :]), a, *fp)
            rc.free(kc, pe)
            yield
            kx, x_, fx = rx.get()
            v = op("vector", xn_of(x_[:, :], b), *fx)
            chain(tt(x_[:, :], x_[:, :], ps[:, 0:256], ALU.add)) if False else op("vector", tt(x_[:, :], x_[:, :], ps[:, 0:256], ALU.add), pe, v)
            v = chain(tt(X[:, b, :], X[:, b, :], x_[:, :], ALU.add))
            rp.free(kp, v)
            rx.free(kx, v)

        pipeline(base(b) for b in range(NB))
        Q.barrier("ffn0c")
        rp = Ring(banks[0:8])
        for e_ in range(8):
            k1, w1, f1 = W1e.get()
            k2, w2, f2 = W2e.get()
            s1, s2 = wslots[e_ % 2], wslots[2 + e_ % 2]
            t1 = dma("sync", s1, (lambda e_, w1: lambda e: e.dma_start(w1[:, :, :], A["L0_ffn_w1"][e_].rearrange("(k p) n -> p k n", p=128)))(e_, w1), *f1, (s1.sem, s1.n))
            t2 = dma("sync", s2, (lambda e_, w2: lambda e: e.dma_start(w2[:, :, :], A["L0_ffn_w2"][e_].rearrange("(k p) n -> p k n", p=128)))(e_, w2), *f2, (s2.sem, s2.n))

            def group(b0, nb, e_=e_, w1=w1, w2=w2, t1=t1, t2=t2):
                w = 128 * nb
                kh, h, fh = rh.get()
                for m in range(2):
                    kp, ps, fp = rp.get()
                    pe = op("tensor", [mm(ps[:, 0:w], w1[:, k, 128 * m:128 * m + 128], XT[:, k, 128 * b0:128 * b0 + w], k == 0, k == 1) for k in range(2)], t1, *fp)
                    a = op("scalar", (lambda m, ps: lambda e: e.activation(h[:, m, 0:w], ps[:, 0:w], ACT.Gelu, bias=b1e[:, e_, m:m + 1]))(m, ps), pe, *fh)
                    rp.free(kp, a)
                yield
                for i in range(nb):
                    b = b0 + i
                    kp, ps, fp = rp.get()
                    pe = op("tensor", [mm(ps[:, 0:256], h[:, k, 128 * i:128 * i + 128], w2[:, k, :], k == 0, k == 1) for k in range(2)], a, t2, *fp)
                    v = op("vector", stt(X[:, b, :], ps[:, 0:256], COMB[:, b, e_:e_ + 1], X[:, b, :], ALU.mult, ALU.add), pe)
                    rp.free(kp, v)
                rh.free(kh, pe)

            pipeline(group(b0, nb) for b0, nb in groups)
            W1e.free(k1, Q.last("tensor"))
            W2e.free(k2, Q.last("tensor"))
        v = Q.last("vector")
        if debug is not None and debug == 1:
            return finish(nc, ctx, Q, X, out, slots)
        Q.op("vector", lambda e: e.memset(BN[:, 0, 0:1], 0.0), v)
        stats()
        Q.barrier("t1", *wslots)

        rstd()
        AR.reset()
        XT = AR.take(2, NP)
        WA = AR.take(2, 264)
        Wq = AR.take(2, 768)
        bq = AR.take(768)
        Wo = AR.take(2, 256)
        bo = AR.take(256)
        L = Loader()
        L.load(WA[:, :, 0:256], A["gW1T"].rearrange("(k p) n -> p k n", p=128))
        L.load(Wq[:, :, :], A["L1_mix_W_qkv"].rearrange("(k p) n -> p k n", p=128))
        L.load(bq[:, :], A["L1_mix_b_qkv"].partition_broadcast(128))
        L.load(Wo[:, :, :], A["L1_mix_W_out"].rearrange("(k p) n -> p k n", p=128))
        L.load(bo[:, :], A["L1_mix_b_out"].partition_broadcast(128))
        KV = AR.take(2, 256)
        mark = AR.at
        wa = att_columns(WA, 256, WA, A["ga_s1"], A["ga_d1"], 4, L)
        rp = Ring(banks[0:4])
        toks = transposed(lambda b, o: xn_of(o, b), XT, ring(3, 256), rp, Q.last("vector"))
        tables(XT, toks, WA, 4, D_z, D_as4, ADS, ring(4, 264), rp, wslots, wa)
        Q.barrier("mix1a", *slots, *wslots)
        gathered = gather_scores(4, 32, 28, D_as4)

        AR.reset(mark)
        rp = Ring(banks[0:4])
        rkv, rsq = ring(4, 512), ring(4, 512)
        rs = ring(4, 8)
        acc = []

        def centered_square(kv, sq, sm, v, b):
            v = op("vector", lambda e: e.tensor_reduce(sm[:, 0:1], kv[:, 0:256], AX.X, ALU.add), v)
            v = chain(ts(sm[:, 0:1], sm[:, 0:1], -1.0 / 256, None, ALU.mult))
            a = op("scalar", lambda e: e.activation(sq[:, 0:256], kv[:, 0:256], ACT.Square, bias=sm[:, 0:1], accum_out=sm[:, 1:2]), v)
            op("vector", ts(sm[:, 2:3], sm[:, 1:2], 1e-7, None, ALU.add), a)
            return chain(lambda e: e.reciprocal(sm[:, 3:4], sm[:, 2:3]), ts(sq[:, 0:256], sq[:, 0:256], sm[:, 3:4], None, ALU.mult))

        def kv1(b):
            K = 128 if b < 48 else LAST
            kp, ps, fp = rp.get()
            pe = op("tensor", [mm(ps[:, 0:512], XT[:, k, 128 * b:128 * b + 128], Wq[:, k, 256:768], k == 0, k == 1) for k in range(2)], *fp)
            yield
            kk, kv, fk = rkv.get()
            kq, sq, fq = rsq.get()
            k3, sm, f3 = rs.get()
            v = op("vector", tt(kv[:, :], ps[:, :], bq[:, 256:768], ALU.add), pe, *fk)
            rp.free(kp, v)
            v = centered_square(kv, sq, sm, v, b) if not (fq or f3) else centered_square(kv, sq, sm, v, b)
            a = op("scalar", lambda e: e.activation(sq[:, 256:512], sq[:, 0:256], ACT.Square), v, *fq, *f3)
            rs.free(k3, a)
            yield
            pe = op("tensor", [mm(banks[4 + j][:, 0:256], sq[0:K, 128 * j:128 * j + 128], kv[0:K, 256:512], b == 0, b == NB - 1) for j in range(2)]
                    + [mm(banks[6 + j][:, 0:1], sq[0:K, 256 + 128 * j:384 + 128 * j], ones[0:K, 0:1], b == 0, b == NB - 1) for j in range(2)], v, a)
            rkv.free(kk, pe)
            rsq.free(kq, pe)
            acc.append(pe)

        pipeline(kv1(b) for b in range(NB))
        nm = AR.take(8)
        for j in range(2):
            a = op("scalar", (lambda j: lambda e: e.activation(nm[:, j:j + 1], banks[6 + j][:, 0:1], ACT.Sqrt))(j), acc[-1])
            op("vector", ts(nm[:, 2 + j:3 + j], nm[:, j:j + 1], 1e-12, None, ALU.max), a)
            chain((lambda j: lambda e: e.reciprocal(nm[:, 4 + j:5 + j], nm[:, 2 + j:3 + j]))(j),
                  ts(KV[:, j, :], banks[4 + j][:, 0:256], nm[:, 4 + j:5 + j], None, ALU.mult))
        Q.barrier("mix1b", pool=False)

        AR.reset(mark)
        rp = Ring(banks[0:8])
        rq, rs = ring(4, 512), ring(4, 16)
        rsq, rT, rat, raT = ring(4, 512), ring(4, 256), ring(4, 256), ring(4, 256)

        def out1(b):
            kp, ps, fp = rp.get()
            xs = lambda k: XT[:, k, 128 * b:128 * b + 128]
            pe = op("tensor", [mm(ps[:, 0:256], xs(k), Wq[:, k, 0:256], k == 0, k == 1) for k in range(2)]
                    + [mm(ps[:, 256:512], xs(k), Wq[:, k, 512:768], k == 0, k == 1) for k in range(2)], *fp)
            yield
            kk, q, fk = rq.get()
            kq, sq, fq = rsq.get()
            k3, sm, f3 = rs.get()
            op("vector", tt(q[:, 0:256], ps[:, 0:256], bq[:, 0:256], ALU.add), pe, *fk, *fq, *f3)
            v = chain(tt(q[:, 256:512], ps[:, 256:512], bq[:, 512:768], ALU.add))
            rp.free(kp, v)
            v = centered_square(q, sq, sm, v, b)
            a = op("scalar", lambda e: e.activation(sq[:, 256:512], sq[:, 0:256], ACT.Square, accum_out=sm[:, 4:5]), v)
            a = op("scalar", lambda e: e.activation(sm[:, 5:6], sm[:, 4:5], ACT.Sqrt), a)
            op("vector", ts(sm[:, 6:7], sm[:, 5:6], 1e-12, None, ALU.max), a)
            v2 = chain(lambda e: e.reciprocal(sm[:, 7:8], sm[:, 6:7]), ts(sm[:, 8:9], sm[:, 7:8], float(N) ** -0.5, None, ALU.mult))
            kp, ps, fp = rp.get()
            pe = op("tensor", [tr(ps[:, 0:128], sq[:, 0:128]), tr(ps[:, 128:256], sq[:, 128:256])], v, *fp)
            rsq.free(kq, pe, a)
            yield
            kt, qT, ft = rT.get()
            a = op("scalar", copy_act(qT[:, :], ps[:, 0:256]), pe, *ft)
            rp.free(kp, a)
            kp, ps, fp = rp.get()
            pe = op("tensor", [mm(ps[:, 0:256], qT[:, 128 * j:128 * j + 128], KV[:, j, :], j == 0, j == 1) for j in range(2)], a, *fp)
            rT.free(kt, pe)
            yield
            ka, at, fa = rat.get()
            v = op("vector", stt(at[:, :], ps[:, 0:256], sm[:, 8:9], q[:, 256:512], ALU.mult, ALU.add), pe, v2, *fa)
            rp.free(kp, v)
            rs.free(k3, v)
            rq.free(kk, v)
            kp, ps, fp = rp.get()
            pe = op("tensor", [tr(ps[:, 0:128], at[:, 0:128]), tr(ps[:, 128:256], at[:, 128:256])], v, *fp)
            rat.free(ka, pe)
            yield
            kt, aT, ft = raT.get()
            a = op("scalar", copy_act(aT[:, :], ps[:, 0:256]), pe, *ft)
            rp.free(kp, a)
            kp, ps, fp = rp.get()
            pe = op("tensor", [mm(ps[:, 0:256], aT[:, 128 * k:128 * k + 128], Wo[:, k, :], k == 0, k == 1) for k in range(2)], a, *fp)
            raT.free(kt, pe)
            yield
            op("vector", tt(X[:, b, :], X[:, b, :], bo[:, :], ALU.add))
            v = op("vector", tt(X[:, b, :], X[:, b, :], ps[:, 0:256], ALU.add), pe, Q.last("vector"))
            rp.free(kp, v)

        pipeline(out1(b) for b in range(NB))
        Q.barrier("gnn1", pool=False)
        Y = gnn(4, 32, 28, 0.01, D_z, "g1", gathered)
        AR.reset(NB * 260)
        WA = AR.take(2, 258)
        L = Loader()
        L.load(WA[:, :, 0:256], A["gW2T"].rearrange("(k p) n -> p k n", p=128))
        wa = att_columns(WA, 256, WA, A["ga_s2"], A["ga_d2"], 1, L)
        t1 = ring(3, 256)
        t2 = ring(3, 256)
        tT = ring(3, 2, 128)
        ro = ring(4, 258)
        rp = Ring(banks[0:8])

        def z2_tile(b):
            k1, u, f1 = t1.get()
            v = op("vector", ts(u[:, :], Y[:, b, :], 0.0, None, ALU.min), *f1, wa)
            a = op("scalar", lambda e: e.activation(u[:, :], u[:, :], ACT.Exp), v)
            yield
            k2, h, f2 = t2.get()
            op("vector", ts(u[:, :], u[:, :], -1.0, None, ALU.add), a)
            v = op("vector", stt(h[:, :], Y[:, b, :], 0.0, u[:, :], ALU.max, ALU.add), Q.last("vector"), *f2)
            t1.free(k1, v)
            kp, ps, fp = rp.get()
            pe = op("tensor", [tr(ps[:, 0:128], h[:, 0:128]), tr(ps[:, 128:256], h[:, 128:256])], v, *fp)
            t2.free(k2, pe)
            yield
            kt, hT, ft = tT.get()
            a = op("scalar", copy_act(hT[:, :, :], ps[:, 0:256].rearrange("p (k t) -> p k t", k=2)), pe, *ft)
            rp.free(kp, a)
            kp, ps, fp = rp.get()
            pe = op("tensor", [mm(ps[:, 0:258], hT[:, k, :], WA[:, k, :], k == 0, k == 1) for k in range(2)], a, *fp)
            tT.free(kt, pe)
            yield
            ko, o, fo = ro.get()
            a = op("scalar", [copy_act(o[:, 0:256], ps[:, 0:256]), copy_act(ASS[:, b:b + 1], ps[:, 256:257]), copy_act(ADS[:, b:b + 1], ps[:, 257:258])], pe, *fo)
            rp.free(kp, a)
            s = wslots[b % 4]
            rows = slice(128 * b, 128 * b + 128)
            t = [dma("sync", s, lambda e: e.dma_start(D_z2[rows, :], o[:, 0:256]), a)]
            ro.free(ko, t[-1])

        pipeline(z2_tile(b) for b in range(NB))
        Q.barrier("gnn2", *slots, *wslots)
        Y = gnn(1, 128, 7, 0.01, D_z2, "g2", ())
        for b in range(NB):
            op("vector", tt(X[:, b, :], X[:, b, :], Y[:, b, :], ALU.add))
        if debug is not None and debug == 2:
            return finish(nc, ctx, Q, X, out, slots)
        Q.op("vector", lambda e: e.memset(BN[:, 0, 0:1], 0.0), Q.last("vector"))
        stats()
        Q.barrier("ffn1")

        rstd()
        AR.reset()
        NE = NB + 7
        NG = NE // 4
        Wd = AR.take(8, 2048)
        W1 = AR.take(2, 1024)
        Wg = AR.take(8, 8)
        b1 = AR.take(8)
        bgc = AR.take(2)
        bd = AR.take(2048)
        L = Loader()
        L.load(W1[:, :, :], A["L1_ffn_W1"].rearrange("(k p) n -> p k n", p=128))
        L.load(Wg[:, :, :], A["L1_ffn_Wg"].rearrange("(m p) n -> p m n", p=128))
        L.load(b1[:, :], A["L1_ffn_b1"].rearrange("(m p) -> p m", p=128))
        L.load(bgc[0:8, 0:1], A["L1_ffn_bg"].unsqueeze(1))
        LD = [dma("sync", wslots[0], lambda e: e.dma_start(bd[0:1, :], A["L1_ffn_bd"].rearrange("e n -> (e n)").unsqueeze(0)), (wslots[0].sem, wslots[0].n))]
        wxt = dma("sync", wslots[1], lambda e: e.dma_start(D_xt[:, 0:256].rearrange("(b p) f -> p b f", p=128), X[:, :, :]), (wslots[1].sem, wslots[1].n))
        for e_ in range(8):
            LD.append(dma("sync", wslots[2 + e_ % 2], (lambda e_: lambda e: e.dma_start(Wd[:, :, 256 * e_:256 * e_ + 256], A["L1_ffn_Wd"][e_].rearrange("(m p) n -> p m n", p=128)))(e_),
                          (wslots[2 + e_ % 2].sem, wslots[2 + e_ % 2].n)))
        mark = AR.at
        rxt = ring(2, 2, 512)
        rH = ring(1, 8, 512)
        rx = ring(3, 256)
        rl = ring(2, 512)
        rs = ring(3, 4, 32)
        aux = AR.take(NB, 4)
        rp = Ring(banks[0:8])
        op("vector", [cp(aux[:, :, 0], MV[:, :, 0]), cp(aux[:, :, 1], RS[:, :])], Q.last("vector"))

        def route1(b0, nb):
            w = 128 * nb
            kX, xt, fX = rxt.get()
            for i in range(nb):
                k, x_, fx = rx.get()
                v = op("vector", xn_of(x_[:, :], b0 + i), *fx)
                kp, ps, fp = rp.get()
                pe = op("tensor", [tr(ps[:, 0:128], x_[:, 0:128]), tr(ps[:, 128:256], x_[:, 128:256])], v, *fp)
                rx.free(k, pe)
                a = op("scalar", copy_act(xt[:, :, 128 * i:128 * i + 128], ps[:, 0:256].rearrange("p (k t) -> p k t", k=2)), pe, *fX)
                rp.free(kp, a)
            yield
            kH, h, fH = rH.get()
            for m in range(8):
                kp, ps, fp = rp.get()
                pe = op("tensor", [mm(ps[:, 0:w], W1[:, k, 128 * m:128 * m + 128], xt[:, k, 0:w], k == 0, k == 1) for k in range(2)], a, *L.toks, *fp)
                a2 = op("scalar", gelu(h[:, m, 0:w], ps[:, 0:w], b1[:, m:m + 1]), pe, *fH)
                rp.free(kp, a2)
            rxt.free(kX, pe)
            kp, ps, fp = rp.get()
            pe = op("tensor", [mm(ps[0:8, 0:w], Wg[:, m, :], h[:, m, 0:w], m == 0, m == 7) for m in range(8)], a2, *fp)
            rH.free(kH, pe)
            kl, l_, fl = rl.get()
            v = op("vector", ts(l_[0:8, 0:w], ps[0:8, 0:w], bgc[0:8, 0:1], None, ALU.add), pe, *fl)
            rp.free(kp, v)
            kp, ps, fp = rp.get()
            pe = op("tensor", [tr(ps[:, 8 * i:8 * i + 8], l_[0:8, 128 * i:128 * i + 128], 8) for i in range(nb)], v, *fp)
            rl.free(kl, pe)
            yield
            k, s_, fs = rs.get()
            lt = s_[:, 0, 0:8 * nb].rearrange("p (t e) -> p t e", e=8)
            top = s_[:, 1, 0:8 * nb].rearrange("p (t e) -> p t e", e=8)
            iu = s_[:, 2, :].bitcast(U32)[:, 0:8 * nb].rearrange("p (t e) -> p t e", e=8)
            q = lambda n: s_[:, 3, 4 * n:4 * n + nb]
            bc = lambda a: a.unsqueeze(2).to_broadcast([128, nb, 8])
            op("vector", cp(lt, ps[:, 0:8 * nb].rearrange("p (t e) -> p t e", e=8)), pe, *fs)
            v = chain(lambda e: e.tensor_reduce(q(0), lt, AX.X, ALU.max), tt(lt, lt, bc(q(0)), ALU.subtract))
            rp.free(kp, v)
            a = op("scalar", lambda e: e.activation(lt, lt, ACT.Exp), v)
            op("vector", lambda e: e.tensor_reduce(q(1), lt, AX.X, ALU.add), a)
            v = chain(rcp(q(2), q(1)), tt(lt, lt, bc(q(2)), ALU.mult))
            v = op("vector", [top8(top[:, i, :], lt[:, i, :]) for i in range(nb)], v)
            v = op("vector", [top8_at(iu[:, i, :], top[:, i, :], lt[:, i, :]) for i in range(nb)], v)
            v = op("vector", [cp(aux[:, b0:b0 + nb, 2], top[:, :, 0]), cp(aux[:, b0:b0 + nb, 3], iu[:, :, 0])], v)
            rs.free(k, v)

        pipeline(route1(b0, nb) for b0, nb in groups)
        wau = dma("sync", wslots[0], lambda e: e.dma_start(D_xt[:, 256:260].rearrange("(b p) f -> p b f", p=128), aux[:, :, :]), Q.last("vector"), (wslots[0].sem, wslots[0].n))
        Q.barrier("sort1", *slots, *wslots)

        AR.reset(mark)
        aux2 = AR.take(NB, 4)
        O, PF, BS = AR.take(NB, 8), AR.take(NB, 8), AR.take(8, NB)
        CUM, TE = AR.take(8 * NB), AR.take(8, NB)
        tri, one_ = AR.take(128), AR.take(128)
        pos, posi, ni = AR.take(NB), AR.take(NB, dt=I32), AR.take(NB, dt=I32)
        q127, itl = AR.take(NB), AR.take(NB)
        gt_, cmpt = AR.take(NB), AR.take(NE, NB)
        sr, ES, TS, QP = AR.take(NE), AR.take(NE), AR.take(NE), AR.take(NE)
        cs, tsp, cmp8 = AR.take(NB), AR.take(2), AR.take(NE, 8)
        eq, MK, IDF, IDI = AR.take(NE), AR.take(NE), AR.take(NE), AR.take(NE, dt=I32)
        tspi = AR.take(2, dt=I32)
        idr, idf = AR.take(128, dt=I32), AR.take(128)
        edl, ewf, ewi, pw1 = AR.take(72), AR.take(4), AR.take(4, dt=I32), AR.take(72)
        IDG = AR.take(NE, dt=I32)
        assert AR.at <= 33500
        wpw = dma("sync", slots[0], lambda e: e.dma_start(pw1[0:1, :], A["pow2"][0:72].unsqueeze(0)), (slots[0].sem, slots[0].n))
        IT = dict(allow_small_or_imprecise_dtypes=True)
        g1 = op("gpsimd", [lambda e: e.iota(ni[:, :], pattern=[[128, NB]], base=0, channel_multiplier=1),
                           lambda e: e.iota(q127[:, :], pattern=[[128, NB]], base=127, channel_multiplier=0, **IT),
                           lambda e: e.iota(itl[:, :], pattern=[[1, NB]], base=0, channel_multiplier=0, **IT),
                           lambda e: e.iota(sr[:, :], pattern=[[1, NE]], base=0, channel_multiplier=0, **IT)])
        EI = aux[:, :, 3]
        v = op("vector", cp(O0[:, :], EI))
        op("vector", lambda e: e.memset(one_[:, :], 1.0), v)
        op("vector", tt(O[:, :, :], iota8[:, :].unsqueeze(1).to_broadcast([128, NB, 8]), O0[:, :].unsqueeze(2).to_broadcast([128, NB, 8]), ALU.is_equal), v)
        v = op("vector", ts(tri[:, :], iota_n[:, :], iota_p[:, 0:1], None, ALU.is_gt))
        pe = op("tensor", [mm(banks[0][:, 0:392], tri[:, :], O[:, :, :].rearrange("p b e -> p (b e)")),
                           mm(banks[1][:, 0:392], one_[:, :], O[:, :, :].rearrange("p b e -> p (b e)"))], v)
        op("vector", [cp(PF[:, :, :].rearrange("p b e -> p (b e)"), banks[0][:, 0:392]),
                      cp(TE[:, :, :], banks[1][:, 0:392].rearrange("p (b e) -> p e b", e=8))], pe)
        TEf = TE[:, :, :].rearrange("p e b -> p (e b)")
        v = chain(lambda e: e.memset(cmp8[:, :, :].rearrange("p s e -> p (s e)")[:, 0:392], 1.0),
                  lambda e: e.tensor_tensor_scan(CUM[:, :], cmp8[:, :, :].rearrange("p s e -> p (s e)")[:, 0:392], TEf, 0.0, ALU.mult, ALU.add),
                  tt(BS[:, :, :].rearrange("p e b -> p (e b)"), CUM[:, :], TEf, ALU.subtract),
                  tt(PF[:, :, :], PF[:, :, :], BS[:, :, :].rearrange("p e b -> p b e"), ALU.add),
                  tt(PF[:, :, :], PF[:, :, :], O[:, :, :], ALU.mult),
                  lambda e: e.tensor_reduce(pos[:, :], PF[:, :, :], AX.X, ALU.add),
                  cp(posi[:, :], pos[:, :]))
        for b in range(NB):
            g_ = gslots[b % 12]
            dma("gpsimd", g_, (lambda b: lambda e: e.indirect_dma_start(
                out=D_idx, out_offset=bass.IndirectOffsetOnAxis(ap=posi[:, b:b + 1], axis=0), in_=ni[:, b:b + 1], in_offset=None))(b), v, g1)
        END = CUM[:, :].rearrange("p (e b) -> p e b", b=NB)[:, 0:7, NB - 1]
        op("vector", tt(cmp8[:, 0:NB, 0:7], END.unsqueeze(1).to_broadcast([128, NB, 7]), q127[:, :].unsqueeze(2).to_broadcast([128, NB, 7]), ALU.is_le), Q.last("vector"), g1)
        v = chain(lambda e: e.tensor_reduce(gt_[:, :], cmp8[:, 0:NB, 0:7], AX.X, ALU.add),
                  tt(gt_[:, :], gt_[:, :], itl[:, :], ALU.add),
                  tt(cmpt[:, :, :], gt_[:, :].unsqueeze(1).to_broadcast([128, NE, NB]), sr[:, :].unsqueeze(2).to_broadcast([128, NE, NB]), ALU.is_lt),
                  lambda e: e.tensor_reduce(TS[:, :], cmpt[:, :, :], AX.X, ALU.add),
                  tt(ES[:, :], sr[:, :], TS[:, :], ALU.subtract),
                  ts(cs[:, :], gt_[:, :], iota_p[:, 0:1], None, ALU.is_lt),
                  lambda e: e.tensor_reduce(tsp[:, 0:1], cs[:, :], AX.X, ALU.add),
                  ts(tsp[:, 0:1], tsp[:, 0:1], float(NB - 1), None, ALU.min), cp(tspi[:, 0:1], tsp[:, 0:1]))
        gi_ = dma("gpsimd", gslots[0], lambda e: e.indirect_dma_start(
            out=idr[0:NE, :], out_offset=None, in_=D_idx.rearrange("(t p) a -> t (p a)", p=128),
            in_offset=bass.IndirectOffsetOnAxis(ap=tspi[0:NE, 0:1], axis=0)), v, *[(g_.sem, g_.n) for g_ in gslots])
        v = chain(ts(QP[:, :], TS[:, :], 128.0, iota_p[:, 0:1], ALU.mult, ALU.add),
                  tt(cmp8[:, :, 0:7], END.unsqueeze(1).to_broadcast([128, NE, 7]), QP[:, :].unsqueeze(2).to_broadcast([128, NE, 7]), ALU.is_le),
                  lambda e: e.tensor_reduce(eq[:, :], cmp8[:, :, 0:7], AX.X, ALU.add),
                  tt(MK[:, :], eq[:, :], ES[:, :], ALU.is_equal))
        op("vector", cp(idf[0:NE, :], idr[0:NE, :]), gi_)
        pe = op("tensor", tr(banks[2][:, 0:NE], idf[0:NE, :], NE), Q.last("vector"))
        op("vector", cp(IDF[:, :], banks[2][:, 0:NE]), pe)
        chain(cp(IDG[:, :], IDF[:, :]), ts(IDF[:, :], IDF[:, :], -8000.0, None, ALU.add), tt(IDF[:, :], IDF[:, :], MK[:, :], ALU.mult),
              ts(IDF[:, :], IDF[:, :], 8000.0, None, ALU.add), cp(IDI[:, :], IDF[:, :]))
        op("vector", [lambda e: e.memset(edl[0:1, :], 0.0)], Q.last("vector"))
        op("vector", tt(edl[0:1, 1:NE], ES[0:1, 1:NE], ES[0:1, 0:NE - 1], ALU.subtract), Q.last("vector"), wpw)
        chain(tt(edl[0:1, :], edl[0:1, :], pw1[0:1, :], ALU.mult),
              lambda e: e.tensor_reduce(ewf[0:1, 0:3], edl[0:1, :].rearrange("p (w i) -> p w i", i=24), AX.X, ALU.add),
              cp(ewi[0:1, 0:3], ewf[0:1, 0:3]))
        Q.barrier("ffn1c", *slots, *wslots, *gslots)

        keep = Arena(ARK, 256)
        kMK, kG, kI, kW = keep.take(NE), keep.take(NE, dt=I32), keep.take(NE, dt=I32), keep.take(4, dt=I32)
        v = op("vector", [cp(kMK[:, :], MK[:, :]), cp(kG[:, :], IDG[:, :]), cp(kI[:, :], IDI[:, :]), cp(kW[0:1, 0:3], ewi[0:1, 0:3])])
        Q.barrier("ffn1d")
        AR.reset(mark)
        XA = Arena(X[:, :, :].rearrange("p b f -> p (b f)"), NB * 256)
        rG = Ring([XA.take(260) for _ in range(12)])
        rO = Ring([XA.take(256) for _ in range(8)])
        rx = Ring([XA.take(256) for _ in range(4)])
        rc = Ring([XA.take(2) for _ in range(12)])
        rH = Ring([AR.take(8, 512), XA.take(8, 512)])
        rxt = ring(2, 2, 512)
        orow1 = AR.take(128)
        vo = op("vector", lambda e: e.memset(orow1[:, :], 1.0))
        rp = Ring(banks[0:8])
        oslots = []

        def ffn1(q):
            gs = []
            for i in range(4):
                s = 4 * q + i
                kg, g_, fg = rG.get()
                sl = gslots[s % 12]
                w = dma("gpsimd", sl, (lambda g_, s: lambda e: e.indirect_dma_start(
                    out=g_[:, :], out_offset=None, in_=D_xt, in_offset=bass.IndirectOffsetOnAxis(ap=kG[:, s:s + 1], axis=0)))(g_, s), *fg)
                gs.append((kg, g_, w))
            yield
            kX, xt, fX = rxt.get()
            for i in range(4):
                kg, g_, w = gs[i]
                k, x_, fx = rx.get()
                v = op("vector", ts(x_[:, :], g_[:, 0:256], g_[:, 256:257], g_[:, 257:258], ALU.subtract, ALU.mult), w, *fx)
                kp, ps, fp = rp.get()
                pe = op("tensor", [tr(ps[:, 0:128], x_[:, 0:128]), tr(ps[:, 128:256], x_[:, 128:256])], v, *fp)
                rx.free(k, pe)
                a = op("scalar", copy_act(xt[:, :, 128 * i:128 * i + 128], ps[:, 0:256].rearrange("p (k t) -> p k t", k=2)), pe, *fX)
                rp.free(kp, a)
            kH, h, fH = rH.get()
            for m in range(8):
                kp, ps, fp = rp.get()
                pe = op("tensor", [mm(ps[:, :], W1[:, k, 128 * m:128 * m + 128], xt[:, k, :], k == 0, k == 1) for k in range(2)], a, *fp)
                a2 = op("scalar", gelu(h[:, m, :], ps[:, :], b1[:, m:m + 1]), pe, *fH)
                rp.free(kp, a2)
            rxt.free(kX, pe)
            yield
            for i in range(4):
                s = 4 * q + i
                kg, g_, w = gs[i]
                box = []
                Q.free("tensor", (lambda s, box: lambda e: box.append(block_of(e, "pe_e", s, 256, kW, 7)))(s, box))
                kp, ps, fp = rp.get()

                def bias_mm(e, ps=ps, box=box):
                    return e.matmul(ps[:, 0:256], orow1[0:1, :], bd[0:1, bass.ds(box[0], 256)], start=True, stop=False)

                def e_mm(m, i=i, ps=ps, box=box):
                    return lambda e: e.matmul(ps[:, 0:256], h[:, m, 128 * i:128 * i + 128], Wd[:, m, bass.ds(box[0], 256)], start=False, stop=(m == 7))

                pe = op("tensor", [bias_mm] + [e_mm(m) for m in range(8)], a2, vo, *fp)
                kc, c_, fc = rc.get()
                v = op("vector", tt(c_[:, 0:1], g_[:, 258:259], kMK[:, s:s + 1], ALU.mult), *fc)
                ko, o, fo = rO.get()
                v = op("vector", stt(o[:, :], ps[:, 0:256], c_[:, 0:1], g_[:, 0:256], ALU.mult, ALU.add), pe, v, *fo)
                rp.free(kp, v)
                rc.free(kc, v)
                rG.free(kg, v)
                sl = oslot8[s % 8]
                t = dma("gpsimd", sl, (lambda o, s: lambda e: e.indirect_dma_start(
                    out=out, out_offset=bass.IndirectOffsetOnAxis(ap=kI[:, s:s + 1], axis=0), in_=o[:, :], in_offset=None,
                    bounds_check=N - 1, oob_is_err=False))(o, s), v)
                rO.free(ko, t)
                oslots.append(t)
            rH.free(kH, pe)

        pipeline(ffn1(q) for q in range(NG))
        Q.barrier("end", *oslot8)
        finish(nc, ctx, Q, X, out, None)


def finish(nc, ctx, Q, X, out, slots):
    s = slots[0] if slots else None
    v = Q.last("vector")
    if s:
      Q.dma("sync", s, lambda e: e.dma_start(out[0:6144, :].rearrange("(b p) f -> p b f", p=128), X[:, 0:48, :]), v, (s.sem, s.n))
    if s:
      t = Q.dma("sync", slots[1], lambda e: e.dma_start(out[6144:N, :], X[0:LAST, 48, :]), v, (slots[1].sem, slots[1].n))
      Q.q["sync"].append(([t, (s.sem, s.n)], [], None, 0))
    ctx.enter_context(nc.allow_non_contiguous_dma(reason="short columns of tables"))
    block = ctx.enter_context(nc.Block())

    @block.sync
    def _(e):
        Q.play("sync", e)

    @block.scalar
    def _(e):
        Q.play("scalar", e)

    @block.vector
    def _(e):
        Q.play("vector", e)

    @block.tensor
    def _(e):
        Q.play("tensor", e)

    @block.gpsimd
    def _(e):
        Q.play("gpsimd", e)


def kernel(debug=None, **inputs):
    import numpy as _np
    import concourse.bacc as _bacc
    from concourse import mybir as _mybir
    from concourse.bass_utils import run_bass_kernel_spmd as _run

    x = {k: _np.asarray(v) for k, v in inputs.items()}
    w1 = x["L1_gnn_W1"]
    arrays = {
        "pow2": (2.0 ** (_np.arange(NW * 24) % 24)).astype(_np.float32),
        "x": x["x"], "src": x["src"], "dst": x["dst"],
        "gW0": x["L0_gnn_W"].reshape(256, 256),
        "ga_s0": x["L0_gnn_att_src"].reshape(256), "ga_d0": x["L0_gnn_att_dst"].reshape(256),
        "qkv0T": x["L0_mix_Wqkv"].T, "m0W1T": x["L0_mix_W1"].T, "m0W2T": x["L0_mix_W2"].T,
        "routerT": x["L0_ffn_router_w"].T,
        "gW1T": w1.reshape(256, 256).T,
        "ga_s1": x["L1_gnn_a1"][:, :64].reshape(256), "ga_d1": x["L1_gnn_a1"][:, 64:].reshape(256),
        "gW2T": x["L1_gnn_W2"].T,
        "ga_s2": x["L1_gnn_a2"][:256], "ga_d2": x["L1_gnn_a2"][256:],
    }
    for k in ("L0_gnn_bias", "L0_mix_ln1_g", "L0_mix_ln1_b", "L0_mix_b1", "L0_mix_b2", "L0_mix_ln2_g", "L0_mix_ln2_b",
              "L0_ffn_w1", "L0_ffn_b1", "L0_ffn_w2", "L0_ffn_b2", "L1_mix_W_qkv", "L1_mix_b_qkv", "L1_mix_W_out", "L1_mix_b_out",
              "L1_ffn_W1", "L1_ffn_b1", "L1_ffn_Wg", "L1_ffn_bg", "L1_ffn_Wd", "L1_ffn_bd"):
        arrays[k] = x[k]
    nc = _bacc.Bacc("TRN2", target_bir_lowering=False, num_devices=1)
    fed, args = {}, {}
    for k, v in arrays.items():
        v = _np.ascontiguousarray(v)
        fed[f"in_{k}"] = v
        args[k] = nc.dram_tensor(f"in_{k}", v.shape, _mybir.dt.from_np(v.dtype), kind="ExternalInput").ap()
    out = nc.dram_tensor("out_0", (N, 256), _mybir.dt.float32, kind="ExternalOutput").ap()
    program(nc, args, out, debug)
    r = _run(nc, [fed], core_ids=[0])
    return r.results[0]["out_0"]
```

```python
from contextlib import ExitStack

import numpy as np

import concourse.bass as bass
from concourse import mybir

F32 = mybir.dt.float32
I32 = mybir.dt.int32
U32 = mybir.dt.uint32
BF16 = mybir.dt.bfloat16
ALU = mybir.AluOpType
ACT = mybir.ActivationFunctionType
AX = mybir.AxisListType

N = 6250
NB = 49
NP = NB * 128
LAST = N - 48 * 128
E = 106250
NT = 832
NS = NT + 48
NSP = 896
NW = 37
BIG = 1e30
ENGINES = ("sync", "scalar", "vector", "tensor", "gpsimd")


class Queues:

    def __init__(self, nc, ctx):
        self.nc, self.ctx = nc, ctx
        self.q = {e: [] for e in ENGINES}
        self.n_sems = 0
        self.sem = {}
        self.count = {}
        self.dmas = []
        self.phase("p")

    def new_sem(self, name):
        self.n_sems += 1
        return self.ctx.enter_context(self.nc.semaphore(f"{name}_{self.n_sems}"))

    def phase(self, name, engines=ENGINES):
        for e in engines:
            self.sem[e] = self.new_sem(f"{name}_{e}")
            self.count[e] = 0

    def op(self, eng, fns, *waits):
        if not isinstance(fns, (list, tuple)):
            fns = [fns]
        self.count[eng] += 1
        self.q[eng].append(([w for w in waits if w], fns, self.sem[eng], 1))
        return (self.sem[eng], self.count[eng])

    def free(self, eng, fn):
        self.q[eng].append(([], [fn], None, 0))

    def last(self, eng):
        return (self.sem[eng], self.count[eng]) if self.count[eng] else None

    def dma(self, eng, slot, fn, *waits):
        slot.n += 16
        self.q[eng].append(([w for w in waits if w], [fn], slot.sem, 16))
        return (slot.sem, slot.n)

    def barrier(self, name, *slots, pool=True):
        engines = ENGINES if pool else ENGINES[:-1]
        marks = [self.last(e) for e in engines] + [(s.sem, s.n) for s in slots if s.n]
        for e in engines:
            self.q[e].append(([m for m in marks if m], [], None, 0))
        self.phase(name, engines)

    def play(self, eng, e):
        seen = {}
        for waits, fns, sem, inc in self.q[eng]:
            for s, v in waits:
                if seen.get(id(s), 0) < v:
                    e.wait_ge(s, v)
                    seen[id(s)] = v
            for f in fns:
                r = f(e)
            if inc:
                r.then_inc(sem, inc)


class Slot:

    def __init__(self, Q, name):
        self.sem, self.n = Q.new_sem(name), 0


class Ring:

    def __init__(self, aps):
        self.aps, self.i = aps, 0
        self.freed = [() for _ in aps]

    def get(self):
        k = self.i % len(self.aps)
        self.i += 1
        assert self.freed[k] is not None, "a buffer is still in use"
        w, self.freed[k] = self.freed[k], None
        return k, self.aps[k], w

    def free(self, k, *tokens):
        self.freed[k] = tokens


def pipeline(gens):
    gens, live = list(gens), []
    while gens or live:
        if gens:
            live.append(gens.pop(0))
        for g in list(live):
            try:
                next(g)
            except StopIteration:
                live.remove(g)


class Arena:
    def __init__(self, t, size):
        self.t, self.size, self.at = t, size, 0

    def reset(self, at=0):
        self.at = at

    def take(self, *shape, dt=F32):
        n = int(np.prod(shape))
        words = n if dt in (F32, I32, U32) else (n + 1) // 2
        words += words % 2
        assert self.at + words <= self.size, (self.at, words, self.size)
        v = self.t[:, self.at:self.at + words]
        self.at += words
        if dt != F32:
            v = v.bitcast(dt)
        v = v[:, 0:n]
        if len(shape) == 2:
            v = v.rearrange("p (a b) -> p a b", b=shape[1])
        elif len(shape) == 3:
            v = v.rearrange("p (a b c) -> p a b c", b=shape[1], c=shape[2])
        return v


def program(nc, A, out):
    ctx = ExitStack()
    with ctx:
        def sb(name, shape, dt=F32):
            return ctx.enter_context(nc.sbuf_tensor(name, shape, dt))

        Q = Queues(nc, ctx)
        op, dma = Q.op, Q.dma
        X = sb("X", [128, NB, 256])
        ART = sb("AR", [128, 33500])
        AR = Arena(ART, 33500)
        ident = sb("ident", [128, 128])
        iota_n = sb("iota_n", [128, 128])
        iota8 = sb("iota8", [128, 8])
        ones = sb("ones", [128, 8])
        hmask = sb("hmask", [128, 132])
        eps = sb("eps", [128, 1])
        REL = sb("REL", [128, NSP])
        SRCI = sb("SRCI", [128, NSP], I32)
        HI = sb("HI", [128, NSP])
        WORDS = sb("WORDS", [1, NW], I32)
        iota_p = sb("iota_p", [128, 1])
        ADS = sb("ADS", [128, NB * 8])
        ASS = sb("ASS", [128, NB])
        AD3 = sb("AD3", [128, NB * 32], BF16)
        AS3 = [sb(f"AS3_{i}", [128, NB], BF16) for i in range(3)]
        FAX = sb("FAX", [128, 392])
        rows4 = sb("rows4", [1, 4, 128])
        MV = sb("MV", [128, NB, 2])
        RS = sb("RS", [128, NB])
        BN = sb("BN", [128, 8, 6])
        banks = [ctx.enter_context(nc.psum_tensor(f"ps{i}", [128, 512], F32)) for i in range(8)]

        def scratch(name, shape, dt=F32):
            return nc.dram_tensor(name, shape, dt, kind="Internal").ap()

        D_se = scratch("D_se", (NT, 128), I32)
        D_de = scratch("D_de", (NT, 128), I32)
        D_b = scratch("D_b", (7, 128), I32)
        D_rel = scratch("D_rel", (NSP, 128), BF16)
        D_lo = scratch("D_lo", (NSP, 128), BF16)
        D_key = scratch("D_key", (NSP * 128 + 2, 1))
        D_h = scratch("D_h", (NP, 256))
        D_as8 = scratch("D_as8", (NP, 8))
        D_z = scratch("D_z", (NP, 256))
        D_as4 = scratch("D_as4", (NP, 4))
        D_z2 = scratch("D_z2", (NP, 256))
        D_as1 = scratch("D_as1", (NP, 1))
        slots = [Slot(Q, f"d{i}") for i in range(12)]
        wslots = [Slot(Q, f"w{i}") for i in range(4)]
        D_xt = scratch("D_xt", (NP, 260))
        D_idx = scratch("D_idx", (NP, 1), I32)
        oslot8 = [Slot(Q, f"o{i}") for i in range(8)]
        ARK = sb("ARK", [128, 256])
        O0 = sb("O0", [128, NB])
        gslots = [Slot(Q, f"g{i}") for i in range(12)]

        def copy_act(o, i):
            return lambda e: e.activation(o, i, ACT.Copy)

        def tt(o, a, b, f):
            return lambda e: e.tensor_tensor(o, a, b, f)

        def ts(o, a, s1, s2, f1, f2=None):
            if f2 is None:
                return lambda e: e.tensor_scalar(o, a, s1, None, f1)
            return lambda e: e.tensor_scalar(o, a, s1, s2, f1, f2)

        def stt(o, a, s, b, f1, f2):
            return lambda e: e.scalar_tensor_tensor(out=o, in0=a, scalar=s, in1=b, op0=f1, op1=f2)

        def rcp(o, i):
            return lambda e: e.reciprocal(o, i)

        def top8(o, i):
            return lambda e: e.max(o, i)

        def top8_at(o, v, i):
            return lambda e: e.max_index(o, v, i)

        def gelu(o, i, b):
            return lambda e: e.activation(o, i, ACT.Gelu, bias=b)

        def cp(o, i):
            return lambda e: e.tensor_copy(o, i)

        def mm(o, l, r, start=True, stop=True):
            return lambda e: e.matmul(o, l, r, start=start, stop=stop)

        def tr(o, i, k=128):
            return lambda e: e.transpose(o, i, ident[0:k, 0:k])

        def chain(*fns):
            t = None
            for f in fns:
                t = op("vector", f, Q.last("vector"))
            return t

        class Loader:

            def __init__(self):
                self.toks = []

            def load(self, o, i):
                s = slots[len(self.toks) % len(slots)]
                self.toks.append(dma("sync", s, lambda e: e.dma_start(o, i), (s.sem, s.n) if s.n else None))
                return self.toks[-1]

        L = Loader()
        w_edge = [dma("sync", slots[0], lambda e: e.dma_start(D_se.rearrange("t e -> (t e)")[0:E].rearrange("(a b) -> a b", a=10), A["src"].rearrange("(a b) -> a b", a=10))),
                  dma("sync", slots[1], lambda e: e.dma_start(D_de.rearrange("t e -> (t e)")[0:E].rearrange("(a b) -> a b", a=10), A["dst"].rearrange("(a b) -> a b", a=10)))]
        m0 = op("vector", lambda e: e.memset(X[:, NB - 1, :], 0.0))
        wx = [dma("sync", slots[2], lambda e: e.dma_start(X[:, 0:48, :], A["x"][0:6144, :].rearrange("(b p) f -> p b f", p=128))),
              dma("sync", slots[3], lambda e: e.dma_start(X[0:LAST, 48, :], A["x"][6144:N, :]), m0)]
        AR.reset()
        padi = AR.take(2, 246, dt=I32)
        sval = AR.take(7)
        gi = AR.take(NT, dt=I32)
        gf = AR.take(NT)
        it = AR.take(NT)
        gb = AR.take(NT)
        gm = AR.take(NT)
        cnt = AR.take(7)
        tsf = AR.take(7)
        tsi = AR.take(7, dt=I32)
        bsf = AR.take(7)
        bsi = AR.take(7, dt=I32)
        b128 = AR.take(7)
        guard = AR.take(2)
        seven = AR.take(8)
        di = AR.take(7, 128, dt=I32)
        si = AR.take(7, 128, dt=I32)
        df = AR.take(7, 128)
        sf = AR.take(7, 128)
        rel = AR.take(7, 128)
        key = AR.take(7, 128)
        vm = AR.take(7, 128)
        hi_, lo_ = AR.take(7, 128, dt=I32), AR.take(7, 128, dt=I32)
        hf, lf = AR.take(7, 128), AR.take(7, 128)
        relb, lob = AR.take(7, 128, dt=BF16), AR.take(7, 128, dt=BF16)
        bi, bf, dl, pw, wf = AR.take(NSP + 2, dt=I32), AR.take(NSP + 2), AR.take(NW * 24), AR.take(NW * 24), AR.take(NW)

        c1 = op("gpsimd", [lambda e: e.memset(ident[:, :], 0.0), lambda e: e.memset(padi[:, 0, :], 0),
                           lambda e: e.memset(padi[:, 1, :], NP - 1), lambda e: e.memset(eps[:, :], 1e-5),
                           lambda e: e.memset(ones[:, :], 1.0), lambda e: e.memset(guard[:, :], -7.0),])
        op("vector", lambda e: e.memset(hmask[:, :], 0.0))
        op("vector", [(lambda h: lambda e: e.memset(hmask[32 * h:32 * h + 32, 32 * h:32 * h + 32], 1.0))(h) for h in range(4)]
           + [(lambda h: lambda e: e.memset(hmask[32 * h:32 * h + 32, 128 + h:129 + h], 1.0))(h) for h in range(4)], Q.last("vector"))
        c2 = op("gpsimd", [lambda e: e.affine_select(out=ident[:, :], in_=ident[:, :], compare_op=ALU.not_equal, fill=1.0, base=0, pattern=[[-1, 128]], channel_multiplier=1)]
                + [lambda e: e.iota(iota_n[:, :], pattern=[[1, 128]], base=0, channel_multiplier=0, allow_small_or_imprecise_dtypes=True),
                   lambda e: e.iota(iota_p[:, :], pattern=[[0, 1]], base=0, channel_multiplier=1, allow_small_or_imprecise_dtypes=True),
                   lambda e: e.iota(iota8[:, :], pattern=[[1, 8]], base=0, channel_multiplier=0, allow_small_or_imprecise_dtypes=True),
                   lambda e: e.iota(sval[:, :], pattern=[[128, 7]], base=0, channel_multiplier=1, allow_small_or_imprecise_dtypes=True),
                   lambda e: e.iota(it[:, :], pattern=[[1, NT]], base=0, channel_multiplier=0, allow_small_or_imprecise_dtypes=True)], c1)
        w_edge += [dma("sync", slots[4], lambda e: e.dma_start(D_se.rearrange("t e -> (t e)")[E:NT * 128].unsqueeze(0), padi[0:1, 0, :]), c1),
                   dma("sync", slots[5], lambda e: e.dma_start(D_de.rearrange("t e -> (t e)")[E:NT * 128].unsqueeze(0), padi[0:1, 1, :]), c1),
                   dma("sync", slots[6], lambda e: e.dma_start(D_key[0:1, :], guard[0:1, 0:1]), c1),
                   dma("sync", slots[7], lambda e: e.dma_start(D_key[NSP * 128 + 1:NSP * 128 + 2, :], guard[0:1, 0:1]), c1)]
        wg = dma("sync", slots[8], lambda e: e.dma_start(gi[0:1, :], D_de[:, 127:128].rearrange("t a -> a t")), *w_edge)
        op("vector", lambda e: e.tensor_scalar(gi[0:1, :], gi[0:1, :], 7, None, ALU.logical_shift_right), wg, c2)
        g = chain(cp(gf[0:1, :], gi[0:1, :]), tt(gf[0:1, :], gf[0:1, :], it[0:1, :], ALU.add),
                  cp(seven[0:1, :], ones[0:1, :]))
        orow = AR.take(128)
        g = op("vector", lambda e: e.memset(orow[:, :], 1.0), g)
        p = op("tensor", [mm(banks[0][:, 0:416], orow[0:1, :], gf[0:1, 0:416]), mm(banks[1][:, 0:416], orow[0:1, :], gf[0:1, 416:832])], g)
        op("vector", [cp(gb[:, 0:416], banks[0][:, 0:416]), cp(gb[:, 416:832], banks[1][:, 0:416])], p)
        for j in range(7):
            chain(ts(gm[:, :], gb[:, :], sval[:, j:j + 1], None, ALU.is_lt),
                  (lambda j: lambda e: e.tensor_reduce(cnt[:, j:j + 1], gm[:, :], AX.X, ALU.add))(j))
        t = chain(ts(tsf[:, :], cnt[:, :], float(NT - 1), None, ALU.min), cp(tsi[:, :], tsf[:, :]),
                  tt(bsf[:, :], sval[:, :], cnt[:, :], ALU.subtract), cp(bsi[:, :], bsf[:, :]),
                  ts(b128[:, :], bsf[:, :], 128.0, None, ALU.mult))
        wb = dma("sync", slots[9], lambda e: e.dma_start(D_b.rearrange("j p -> p j"), bsi[:, :]), t)
        wb = dma("sync", slots[10], lambda e: e.dma_start(bi[0:1, 1:NSP + 1], D_b.rearrange("j p -> (j p)").unsqueeze(0)), wb)
        wp = dma("sync", slots[11], lambda e: e.dma_start(pw[0:1, :], A["pow2"].unsqueeze(0)))
        op("vector", cp(bf[0:1, 1:NSP + 1], bi[0:1, 1:NSP + 1]), wb)
        op("vector", lambda e: e.memset(bf[0:1, 0:1], 0.0))
        op("vector", tt(dl[0:1, :], bf[0:1, 1:NW * 24 + 1], bf[0:1, 0:NW * 24], ALU.subtract), Q.last("vector"), wp)
        chain(tt(dl[0:1, :], dl[0:1, :], pw[0:1, :], ALU.mult),
              lambda e: e.tensor_reduce(wf[0:1, :], dl[0:1, :].rearrange("p (w i) -> p w i", i=24), AX.X, ALU.add),
              cp(WORDS[0:1, :], wf[0:1, :]))
        for j in range(7):
            a = dma("gpsimd", gslots[0], (lambda j: lambda e: e.indirect_dma_start(
                out=di[:, j, :], out_offset=None, in_=D_de, in_offset=bass.IndirectOffsetOnAxis(ap=tsi[:, j:j + 1], axis=0)))(j), t, (gslots[0].sem, gslots[0].n), *w_edge)
            b = dma("gpsimd", gslots[1], (lambda j: lambda e: e.indirect_dma_start(
                out=si[:, j, :], out_offset=None, in_=D_se, in_offset=bass.IndirectOffsetOnAxis(ap=tsi[:, j:j + 1], axis=0)))(j), t, (gslots[1].sem, gslots[1].n))
            op("vector", cp(df[:, j, :], di[:, j, :]), a)
            u = chain(ts(rel[:, j, :], df[:, j, :], b128[:, j:j + 1], None, ALU.subtract))
            v = op("vector", cp(sf[:, j, :], si[:, j, :]), b)
            op("vector", ts(hi_[:, j, :], si[:, j, :], 7, None, ALU.logical_shift_right))
            op("vector", ts(lo_[:, j, :], si[:, j, :], 127, None, ALU.bitwise_and))
            op("vector", [cp(hf[:, j, :], hi_[:, j, :]), cp(lf[:, j, :], lo_[:, j, :])], Q.last("vector"))
            k = chain(ts(vm[:, j, :], rel[:, j, :], -0.5, None, ALU.is_gt),
                      stt(vm[:, j, :], rel[:, j, :], 127.5, vm[:, j, :], ALU.is_lt, ALU.mult),
                      stt(key[:, j, :], df[:, j, :], 1.0, vm[:, j, :], ALU.add, ALU.mult),
                      ts(key[:, j, :], key[:, j, :], -1.0, None, ALU.add))
            dma("sync", slots[0], (lambda j: lambda e: e.dma_start(
                D_key[1 + j * 16384:1 + (j + 1) * 16384, :].rearrange("(s e) a -> s (e a)", e=128), key[:, j, :]))(j), k, (slots[0].sem, slots[0].n))
            k = op("vector", [cp(relb[:, j, :], rel[:, j, :]), cp(lob[:, j, :], lf[:, j, :])], k)
            for q, D_t, T in ((2, D_rel, relb), (3, D_lo, lob)):
                dma("sync", slots[q], (lambda D_t, T, j: lambda e: e.dma_start(D_t[128 * j:128 * j + 128, :], T[:, j, :]))(D_t, T, j), k, (slots[q].sem, slots[q].n))
            c = slice(128 * j, 128 * j + 128)
            pe = op("tensor", [tr(banks[2][:, 0:128], rel[:, j, :]), tr(banks[2][:, 128:256], sf[:, j, :]), tr(banks[2][:, 256:384], hf[:, j, :])], k, v)
            op("vector", [cp(REL[:, c], banks[2][:, 0:128]), cp(SRCI[:, c], banks[2][:, 128:256]), cp(HI[:, c], banks[2][:, 256:384])], pe)
        for b in range(NB):
            op("vector", (lambda b: lambda e: e.bn_stats(BN[:, b % 8, :], X[:, b, :]))(b), wx[0] if b < 48 else wx[1], wx[1], Q.last("vector"))
            op("vector", (lambda b: lambda e: e.bn_aggr(MV[:, b, :], BN[:, b % 8, :]))(b), Q.last("vector"))
        Q.barrier("t0", *slots, *gslots)

        def stats():
            for b in range(NB):
                op("vector", (lambda b: lambda e: e.bn_stats(BN[:, b % 8, :], X[:, b, :]))(b), Q.last("vector"))
                op("vector", (lambda b: lambda e: e.bn_aggr(MV[:, b, :], BN[:, b % 8, :]))(b), Q.last("vector"))

        def rstd():
            a = op("scalar", lambda e: e.activation(RS[:, :], MV[:, :, 1], ACT.Sqrt, bias=eps[:, 0:1]), Q.last("vector"))
            return op("vector", lambda e: e.reciprocal(RS[:, :], RS[:, :]), a)

        def ring(n, *shape):
            return Ring([AR.take(*shape) for _ in range(n)])

        def xn_of(o, b):
            return ts(o, X[:, b, :], MV[:, b, 0:1], RS[:, b:b + 1], ALU.subtract, ALU.mult)

        def transposed(src_of, dstT, r_x, r_ps, *w):
            toks = [None] * NB

            def one(b):
                k, xt, fw = r_x.get()
                v = op("vector", src_of(b, xt), *fw, *w)
                yield
                kp, ps, fp = r_ps.get()
                pe = op("tensor", [tr(ps[:, 0:128], xt[:, 0:128]), tr(ps[:, 128:256], xt[:, 128:256])], v, *fp)
                r_x.free(k, pe)
                yield
                a = op("scalar", copy_act(dstT[:, :, 128 * b:128 * b + 128], ps[:, 0:256].rearrange("p (k t) -> p k t", k=2)), pe)
                r_ps.free(kp, a)
                toks[b] = a

            pipeline(one(b) for b in range(NB))
            return toks

        def att_columns(WA, base, W_view, a_src, a_dst, H, L):
            D = 256 // H
            tmp = AR.take(256)
            wb = AR.take(2, 256)
            t = [L.load(wb[:, 0, :], a_src.partition_broadcast(128)), L.load(wb[:, 1, :], a_dst.partition_broadcast(128))]
            r = None
            for k in range(2):
                for n in range(2):
                    op("vector", tt(tmp[:, :], W_view[:, k, 0:256], wb[:, n, :], ALU.mult), *L.toks, Q.last("vector"))
                    r = chain((lambda k, n: lambda e: e.tensor_reduce(WA[:, k, base + n * H:base + (n + 1) * H], tmp[:, :].rearrange("p (h d) -> p h d", h=H), AX.X, ALU.add))(k, n))
            return r

        def tables(XT, toks, WA, H, D_row, D_as, ADS, r_o, r_ps, wslots, *w):
            def one(b):
                kp, ps, fp = r_ps.get()
                pe = op("tensor", [mm(ps[:, 0:256 + 2 * H], XT[:, k, 128 * b:128 * b + 128], WA[:, k, 0:256 + 2 * H], k == 0, k == 1) for k in range(2)], toks[b], *w, *fp)
                yield
                ko, o, fo = r_o.get()
                a = op("scalar", [copy_act(o[:, 0:256 + H], ps[:, 0:256 + H]), copy_act(ADS[:, b * H:b * H + H], ps[:, 256 + H:256 + 2 * H])], pe, *fo)
                r_ps.free(kp, a)
                yield
                s = wslots[b % len(wslots)]
                rows = slice(128 * b, 128 * b + 128)
                t = [dma("sync", s, lambda e: e.dma_start(D_row[rows, :], o[:, 0:256]), a),
                     dma("sync", s, lambda e: e.dma_start(D_as[rows, :], o[:, 256:256 + H]), a)]
                r_o.free(ko, t[-1])

            pipeline(one(b) for b in range(NB))

        def ln_tile(src, dst, g, bb, sm, *w):
            op("vector", lambda e: e.bn_stats(sm[:, 0:6], src), *w, Q.last("vector"))
            v = chain(lambda e: e.bn_aggr(sm[:, 6:8], sm[:, 0:6]))
            yield v
            a = op("scalar", lambda e: e.activation(sm[:, 8:9], sm[:, 7:8], ACT.Sqrt, bias=eps[:, 0:1]), v)
            yield a
            op("vector", lambda e: e.reciprocal(sm[:, 9:10], sm[:, 8:9]), a)
            v = chain(ts(dst, src, sm[:, 6:7], sm[:, 9:10], ALU.subtract, ALU.mult),
                      tt(dst, dst, g, ALU.mult), tt(dst, dst, bb, ALU.add))
            yield v

        regs = {}

        def block_of(e, name, s, scale, words=None, most=48):
            words = WORDS if words is None else words
            if name not in regs:
                regs[name] = [e.alloc_register(f"{name}_{r}") for r in ("at", "word", "bit")]
            at_, word, bit = regs[name]
            if s == 0:
                e.reg_mov(at_, 0)
            if s % 24 == 0:
                e.reg_load(word, words[0:1, s // 24:s // 24 + 1])
                if scale in (4, 16, 32):
                    e.reg_alu(word, word, scale.bit_length() - 1, ALU.logical_shift_left)
            if scale in (4, 16, 32):
                e.reg_alu(bit, word, scale, ALU.bitwise_and)
                e.reg_alu(word, word, 1, ALU.logical_shift_right)
            else:
                e.reg_alu(bit, word, 1, ALU.bitwise_and)
                e.reg_alu(word, word, 1, ALU.logical_shift_right)
                e.reg_mul(bit, bit, scale)
            e.reg_add(at_, at_, bit)
            return e.snap(at_, min_val=0, max_val=most * scale)

        EDGE = ART[:, 26332:33500]

        def split3(x, parts, tmp, *w):
            v = op("vector", cp(parts[0], x), *w)
            v = chain(tt(tmp, x, parts[0], ALU.subtract), cp(parts[1], tmp), tt(tmp, tmp, parts[1], ALU.subtract), cp(parts[2], tmp))
            return v

        def place(H, C, J, s):
            return EDGE[:, (s % J * C + s // J) * H:(s % J * C + s // J + 1) * H]

        def gather_scores(H, C, J, D_as):
            toks = []
            for n in range(NSP):
                s = n % C * J + n // C
                g = gslots[n % 12]
                t = dma("gpsimd", g, (lambda s: lambda e: e.indirect_dma_start(
                    out=place(H, C, J, s), out_offset=None, in_=D_as,
                    in_offset=bass.IndirectOffsetOnAxis(ap=SRCI[:, s:s + 1], axis=0)))(s), (g.sem, g.n) if g.n else None)
                toks.append(t)
            return toks

        def onehots(D_t, r_b, r_t, slot0, use, count=NSP // 8):
            def one(q):
                kb, rb, fb = r_b.get()
                sl = slots[slot0 + q % len(r_b.aps)]
                w = dma("sync", sl, lambda e: e.dma_start(rb, D_t[8 * q:8 * q + 8, :].rearrange("s e -> (s e)").partition_broadcast(128)), *fb, (sl.sem, sl.n))
                yield
                kt, st, ft = r_t.get()
                v = op("vector", ts(st, rb, iota_p[:, 0:1], None, ALU.is_equal), w, *ft)
                r_b.free(kb, v)
                yield
                for i in range(8):
                    pe = use(8 * q + i, st[:, 128 * i:128 * i + 128], v)
                r_t.free(kt, pe)

            pipeline(one(q) for q in range(count))

        BY_ROW = 488

        def gnn(H, C, J, slope, D_row, name, gathered, ahead=None):
            W = J * 128
            assert C * H == 128 and C * J == NSP
            YW = 256 + H
            TS = {8: 32, 4: 16, 1: 4}[H]
            AR.reset()
            SC = AR.take(7168)
            B2 = AR.take(7170)
            ADV = SC[:, 0:NSP * H] if H > 1 else SC[:, 1024:1024 + NSP]
            FA = AR.take(7168, dt=BF16)
            FB = AR.take(7168, dt=BF16)
            r_b = Ring([AR.take(1024, dt=BF16) for _ in range(5)])
            r_t = Ring([AR.take(1024, dt=BF16) for _ in range(4)])
            SC, B2w, FA, FB = SC[:, 0:W], B2[:, 0:W], FA[:, 0:W], FB[:, 0:W]
            B1 = EDGE[:, 0:W]
            E1 = EDGE[:, 0:NSP * H]
            sm = AR.take(8)
            row = rows4
            ad_by_chunk = ADV.rearrange("p (j c h) -> p c j h", j=J, h=H)
            by_chunk = E1.rearrange("p (j c h) -> p c j h", j=J, h=H)

            KW = B2[:, 0:W + 2]
            win = bass.AP(D_key.tensor, D_key.offset, [[W, C], [0, H], [1, W + 2]])
            wk = dma("sync", slots[10], lambda e: e.dma_start(KW, win))
            parts = AD3[:, 0:NB * TS].rearrange("p (b n) -> p b n", n=TS)
            split3(ADS[:, 0:NB * H].rearrange("p (b h) -> p b h", h=H), [parts[:, :, n * H:n * H + H] for n in range(3)],
                   FAX[:, 0:NB * H].rearrange("p (b h) -> p b h", h=H))
            if H == 1:
                split3(ASS[:, :], [t[:, :] for t in AS3], FAX[:, 0:NB], Q.last("vector"))
            op("vector", tt(FA, KW[:, 1:W + 1], KW[:, 0:W], ALU.is_equal), wk)
            v = op("vector", tt(FB, KW[:, 1:W + 1], KW[:, 2:W + 2], ALU.is_equal))
            for F in (FA, FB):
                op("vector", ts(F, F, -1.0, BIG, ALU.add, ALU.mult), v)
            op("vector", [(lambda o, F: lambda e: e.tensor_reduce(o, F, AX.X, ALU.min))(sm[:, 4 + i:5 + i], F) for i, F in enumerate((FA, FB))], Q.last("vector"))
            ASV = None
            if H == 1:
                ASV = SC
                mk = FAX
                r_p = Ring(banks[2:6])
                box = {}

                def use(s, st, v):
                    if s % 8 == 0:
                        box["k"], box["ps"], box["w"] = r_p.get()
                    ps = box["ps"]
                    pe = op("tensor", [mm(ps[:, 49 * (s % 8):49 * (s % 8) + 49], st, AS3[n][:, :], n == 0, n == 2) for n in range(3)], v, *box["w"])
                    if s % 8 == 7:
                        op("vector", tt(mk[:, :].rearrange("p (s b) -> p s b", b=49), iota_n[:, 0:49].unsqueeze(1).to_broadcast([128, 8, 49]),
                                        HI[:, s - 7:s + 1].unsqueeze(2).to_broadcast([128, 8, 49]), ALU.is_equal), Q.last("vector"))
                        op("vector", tt(mk[:, :], mk[:, :], ps[:, 0:392], ALU.mult), pe, Q.last("vector"))
                        v = chain((lambda s: lambda e: e.tensor_reduce(ASV[:, s - 7:s + 1], mk[:, :].rearrange("p (s b) -> p s b", b=49), AX.X, ALU.add))(s))
                        r_p.free(box["k"], v)
                    return pe

                gathered = []
                for s in range(BY_ROW, NSP):
                    g = gslots[s % 12]
                    gathered.append(dma("gpsimd", g, (lambda s: lambda e: e.indirect_dma_start(
                        out=ASV[:, s:s + 1], out_offset=None, in_=D_as1,
                        in_offset=bass.IndirectOffsetOnAxis(ap=SRCI[:, s:s + 1], axis=0)))(s), (g.sem, g.n) if g.n else None))
                onehots(D_lo, r_b, r_t, 0, use, BY_ROW // 8)

            r_p = Ring(banks[0:2])
            acc_ = {}

            PER = 112 // H

            def use2(s, st, v):
                i = s % PER
                if i == 0:
                    acc_["k"], acc_["ps"], acc_["w"] = r_p.get()
                ps = acc_["ps"]
                box = []
                if s < NS:
                    Q.free("tensor", lambda e: box.append(block_of(e, "pe", s, TS)))

                def f(e):
                    return e.matmul(ps[:, 3 * H * i:3 * H * i + 3 * H], st, AD3[:, bass.ds(box[0], 3 * H)] if s < NS else AD3[:, 48 * TS:48 * TS + 3 * H],
                                    start=True, stop=True)

                pe = op("tensor", f, v, *acc_["w"])
                if i == PER - 1:
                    c, j = (s + 1 - PER) // J, (s + 1 - PER) % J
                    if PER <= J:
                        o, q = ad_by_chunk[:, c, j:j + PER, :], ps[:, 0:336].rearrange("p (s t h) -> p s h t", t=3, h=H)
                    else:
                        o, q = ad_by_chunk[:, c:c + PER // J, :, 0], ps[:, 0:336].rearrange("p (c j t) -> p c j t", j=J, t=3)
                    a_ = op("vector", lambda e: e.tensor_reduce(o, q, AX.X, ALU.add), pe)
                    r_p.free(acc_["k"], a_)
                return pe

            onehots(D_rel, r_b, r_t, 5, use2)
            if H == 1:
                v = op("vector", tt(by_chunk[:, :, :, 0], ad_by_chunk[:, :, :, 0], ASV[:, 0:NSP].rearrange("p (c j) -> p c j", j=J), ALU.add), Q.last("vector"), *gathered[-12:])

            rp = Ring(banks[2:6])
            ad_done = Q.last("vector")
            for j0 in range(0, J, 4):
                nj = min(4, J - j0)
                c = slice(128 * j0, 128 * (j0 + nj))
                if H > 1:
                    v = op("vector", tt(E1[:, c], E1[:, c], ADV[:, c], ALU.add), ad_done, *gathered[(j0 + nj) * C - 12:(j0 + nj) * C])
                v = op("vector", stt(E1[:, c], E1[:, c], slope, E1[:, c], ALU.mult, ALU.max), v)
                kp, ps, fp = rp.get()
                pe = op("tensor", [tr(ps[:, 128 * i:128 * i + 128], E1[:, 128 * (j0 + i):128 * (j0 + i) + 128]) for i in range(nj)], v, *fp)
                a = op("scalar", copy_act(SC[:, c], ps[:, 0:128 * nj]), pe, v)
                rp.free(kp, a)

            def segscan(o, x, F, rev):
                d = (lambda ap: ap[:, ::-1]) if rev else (lambda ap: ap)
                end = 0 if rev else W - 1
                scan = lambda init: (lambda e: e.tensor_tensor_scan(d(o), d(F), d(x), init, ALU.add, ALU.max))
                low = sm[:, 5:6] if rev else sm[:, 4:5]
                op("vector", scan(-BIG), Q.last("vector"), Q.last("scalar"))
                v = chain(cp(sm[:, 0:1], o[:, end:end + 1]))
                pe = op("tensor", [tr(banks[7][0:1, 0:128], sm[:, 0:1]), tr(banks[7][0:1, 128:256], low)], v)
                r = lambda i: row[0:1, i, :]
                op("vector", [cp(r(0).rearrange("p (h c) -> p h c", h=H), banks[7][0:1, 0:128].rearrange("p (c h) -> p h c", h=H)),
                              cp(r(1).rearrange("p (h c) -> p h c", h=H), banks[7][0:1, 128:256].rearrange("p (c h) -> p h c", h=H)),
                              lambda e: e.memset(r(3), -BIG)], pe)
                hc = r(2).rearrange("p (h c) -> p h c", h=H)
                ch = r(3).rearrange("p (c h) -> p h c", h=H)
                v = chain(lambda e: e.tensor_tensor_scan(d(r(2)), d(r(1)), d(r(0)), -BIG, ALU.add, ALU.max),
                          cp(ch[:, :, 0:C - 1], hc[:, :, 1:C]) if rev else cp(ch[:, :, 1:C], hc[:, :, 0:C - 1]))
                pe = op("tensor", mm(banks[7][:, 256:257], row[0:1, 3, :], ones[0:1, 0:1]), v)
                op("vector", cp(sm[:, 2:3], banks[7][:, 256:257]), pe)
                return chain(scan(sm[:, 2:3]))

            segscan(B1, SC, FA, False)
            segscan(B2w, B1, FB, True)
            m = Q.last("vector")
            for j0 in range(0, J, 4):
                nj = min(4, J - j0)
                c = slice(128 * j0, 128 * (j0 + nj))
                v = op("vector", tt(SC[:, c], SC[:, c], B2w[:, c], ALU.subtract), m)
                a = op("scalar", (lambda c: lambda e: e.activation(SC[:, c], SC[:, c], ACT.Exp))(c), v)
                kp, ps, fp = rp.get()
                pe = op("tensor", [tr(ps[:, 128 * i:128 * i + 128], SC[:, 128 * (j0 + i):128 * (j0 + i) + 128]) for i in range(nj)], a, *fp)
                a2 = op("scalar", copy_act(E1[:, 128 * j0:128 * (j0 + nj)], ps[:, 0:128 * nj]), pe)
                rp.free(kp, a2)
            Q.barrier(name + "b", *slots, *gslots)

            if ahead:
                ahead()
            AR.reset()
            Yf = AR.take(NB * YW)
            G = ring(10, YW if H == 1 else 256)
            M = ring(4, YW)
            S = ring(4, 128)
            rp = Ring(banks[0:8])
            if H == 1:
                op("vector", [(lambda g: lambda e: e.memset(g[:, 256:257], 1.0))(g) for g in G.aps])
            filled = Q.last("vector")
            state = {"y": op("vector", lambda e: e.memset(Yf, 0.0))}

            def step(s):
                kg, gt, fg = G.get()
                sl = gslots[s % 10]
                gk = dma("gpsimd", sl, lambda e: e.indirect_dma_start(
                    out=gt[:, 0:256], out_offset=None, in_=D_row,
                    in_offset=bass.IndirectOffsetOnAxis(ap=SRCI[:, s:s + 1], axis=0)), *fg)
                for _ in range(6):
                    yield
                kS, st, fS = S.get()
                ee = place(H, C, J, s)
                if H == 1:
                    w = v = op("vector", ts(st[:, :], iota_n[:, :], REL[:, s:s + 1], ee, ALU.is_equal, ALU.mult), *fS)
                    mt, w = gt, gk
                else:
                    kM, mt, fM = M.get()
                    op("vector", ts(st[:, :], iota_n[:, :], REL[:, s:s + 1], None, ALU.is_equal), *fS)
                    w = op("scalar", copy_act(mt[:, 256:YW], ee), *fM)
                    v = op("vector", tt(mt[:, 0:256].rearrange("p (h d) -> p h d", h=H), gt[:, :].rearrange("p (h d) -> p h d", h=H),
                                            ee.unsqueeze(2).to_broadcast([128, H, 256 // H]), ALU.mult), gk, *fM)
                    G.free(kg, v)
                kp, ps, fp = rp.get()
                pe = op("tensor", mm(ps[:, 0:YW], st[:, :], mt[:, :]), v, w, filled, *fp)
                S.free(kS, pe)
                if H == 1:
                    G.free(kg, pe)
                else:
                    M.free(kM, pe)
                for _ in range(4):
                    yield
                box = []
                Q.free("vector", lambda e: box.append(block_of(e, "dve", s, YW)))

                def add(e):
                    o = Yf[:, bass.ds(box[0], YW)]
                    return e.tensor_tensor(o, ps[:, 0:YW], o, ALU.add)

                v = op("vector", add, pe, state["y"])
                state["y"] = v
                rp.free(kp, v)

            pipeline(step(s) for s in range(NS))
            Y = Yf.rearrange("p (b n) -> p b n", b=NB)
            den = AR.take(NB, H)
            v = chain(ts(den[:, :, :], Y[:, :, 256:YW], 1e-16, None, ALU.add), rcp(den[:, :, :], den[:, :, :]))
            for b in range(NB):
                v2 = op("gpsimd" if b % 3 == 2 else "vector", tt(Y[:, b, 0:256].rearrange("p (h d) -> p h d", h=H), Y[:, b, 0:256].rearrange("p (h d) -> p h d", h=H),
                                     den[:, b, :].unsqueeze(2).to_broadcast([128, H, 256 // H]), ALU.mult), v)
            Q.barrier(name + "c", *gslots)
            return Y[:, :, 0:256]

        rstd()
        AR.reset()
        XT = AR.take(2, NP)
        WA = AR.take(2, 272)
        Wkv = AR.take(2, 768)
        W1 = AR.take(2, 256)
        W2 = AR.take(2, 256)
        bcs = AR.take(5, 256)
        b1c = AR.take(2)
        KVB = AR.take(2, 132)
        L = Loader()
        L.load(WA[:, :, 0:256], A["gW0"].rearrange("(k p) n -> p k n", p=128))
        L.load(Wkv[:, :, :], A["qkv0T"].rearrange("(k p) n -> p k n", p=128))
        L.load(W1[:, :, :], A["m0W1T"].rearrange("(k p) n -> p k n", p=128))
        L.load(W2[:, :, :], A["m0W2T"].rearrange("(k p) n -> p k n", p=128))
        for i, n in enumerate(("L0_mix_ln1_g", "L0_mix_ln1_b", "L0_mix_b2", "L0_mix_ln2_g", "L0_mix_ln2_b")):
            L.load(bcs[:, i, :], A[n].partition_broadcast(128))
        L.load(b1c[:, :], A["L0_mix_b1"].rearrange("(k p) -> p k", p=128))
        mark = AR.at
        wa = att_columns(WA, 256, WA, A["ga_s0"], A["ga_d0"], 8, L)
        rp = Ring(banks[0:4])
        toks = transposed(lambda b, o: xn_of(o, b), XT, ring(3, 256), rp, Q.last("vector"))
        tables(XT, toks, WA, 8, D_h, D_as8, ADS, ring(4, 272), rp, wslots, wa)
        Q.barrier("mix0a", *slots, *wslots)
        gathered = gather_scores(8, 16, 56, D_as8)

        AR.reset(mark)
        rk, rv, re = ring(4, 256), ring(4, 2, 130), ring(4, 256)
        m1 = op("vector", [(lambda r: lambda e: e.memset(r[:, :, 128:130], 1.0))(r) for r in rv.aps])
        rp = Ring(banks[0:4])
        acc = []

        def kv_tile(b):
            K = 128 if b < 48 else LAST
            kp, ps, fp = rp.get()
            pe = op("tensor", [mm(ps[:, 0:512], XT[:, k, 128 * b:128 * b + 128], Wkv[:, k, 256:768], k == 0, k == 1) for k in range(2)], *fp)
            yield
            ke, e_, fe = re.get()
            kk, kt, fk = rk.get()
            kv, vt, fv = rv.get()
            v = op("vector", ts(e_[:, :], ps[:, 0:256], 0.0, None, ALU.min), pe, *fe)
            a2 = op("scalar", copy_act(vt[:, :, 0:128], ps[:, 256:512].rearrange("p (j n) -> p j n", j=2)), v, *fv, m1)
            a = op("scalar", lambda e: e.activation(e_[:, :], e_[:, :], ACT.Exp), v)
            yield
            v = op("vector", stt(kt[:, :], ps[:, 0:256], 0.0, e_[:, :], ALU.max, ALU.add), a, *fk)
            rp.free(kp, v, a2)
            re.free(ke, v)
            yield
            pe = op("tensor", [mm(banks[6 + j][:, 0:129], kt[0:K, 128 * j:128 * j + 128], vt[0:K, j, 0:129], b == 0, b == NB - 1) for j in range(2)], v, a2)
            rk.free(kk, pe)
            rv.free(kv, pe)
            acc.append(pe)

        pipeline(kv_tile(b) for b in range(NB))
        for j in range(2):
            op("vector", tt(KVB[:, j, 0:128], banks[6 + j][:, 0:128], hmask[:, 0:128], ALU.mult), acc[-1])
            chain(ts(KVB[:, j, 128:132], hmask[:, 128:132], banks[6 + j][:, 128:129], None, ALU.mult))
        Q.barrier("mix0b", pool=False)

        AR.reset(mark)
        groups = [(4 * g, 4) for g in range(12)] + [(48, 1)]
        rq, rqe = ring(2, 2, 512), ring(1, 2, 512)
        r1 = ring(5, 256)
        rt = ring(2, 256)
        rx1T = ring(1, 2, 512)
        rhT = ring(1, 2, 512)
        rsm = ring(4, 10)
        rz = ring(2, 8)
        rp = Ring(banks[0:8])

        def mix0_group(b0, nb):
            w = 128 * nb
            kq, qt, fq = rq.get()
            ke, qe, fe = rqe.get()
            vs = []
            for m in range(2):
                kp, ps, fp = rp.get()
                pe = op("tensor", [mm(ps[:, 0:w], Wkv[:, k, 128 * m:128 * m + 128], XT[:, k, 128 * b0:128 * b0 + w], k == 0, k == 1) for k in range(2)], *fp)
                v = op("vector", ts(qe[:, m, 0:w], ps[:, 0:w], 0.0, None, ALU.min), pe, *fe)
                a = op("scalar", (lambda m: lambda e: e.activation(qe[:, m, 0:w], qe[:, m, 0:w], ACT.Exp))(m), v)
                v = op("vector", stt(qt[:, m, 0:w], ps[:, 0:w], 0.0, qe[:, m, 0:w], ALU.max, ALU.add), a, *fq)
                rp.free(kp, v)
                vs.append(v)
            rqe.free(ke, v)
            sms, x1s = [], []
            for i in range(nb):
                b = b0 + i
                kp, ps, fp = rp.get()
                pe = op("tensor", [mm(ps[:, 132 * j:132 * j + 132], qt[:, j, 128 * i:128 * i + 128], KVB[:, j, :]) for j in range(2)], v, *fp)
                kt, t_, ft = rt.get()
                kz, z_, fz = rz.get()
                k1, x1, f1 = r1.get()
                ks, sm, fs = rsm.get()
                pv = ps[:, 0:264].rearrange("p (j n) -> p j n", j=2)
                op("vector", ts(z_[:, 0:8].rearrange("p (j h) -> p j h", j=2), pv[:, :, 128:132], 1e-6, None, ALU.add), pe, *fz, *ft, *f1, *fs)
                v1 = chain(rcp(z_[:, 0:8], z_[:, 0:8]),
                           tt(t_[:, :].rearrange("p (j h d) -> p j h d", j=2, h=4), pv[:, :, 0:128].rearrange("p j (h d) -> p j h d", h=4),
                              z_[:, 0:8].rearrange("p (j h) -> p j h", j=2).unsqueeze(3).to_broadcast([128, 2, 4, 32]), ALU.mult))
                rp.free(kp, v1)
                op("vector", xn_of(x1[:, :], b))
                v1 = chain(tt(x1[:, :], x1[:, :], t_[:, :], ALU.add))
                rt.free(kt, v1)
                rz.free(kz, v1)
                gen = ln_tile(x1[:, :], x1[:, :], bcs[:, 0, :], bcs[:, 1, :], sm, v1)
                next(gen)
                sms.append((ks, gen))
                x1s.append((k1, x1))
            rq.free(kq, pe)
            for _, g in sms:
                next(g)
            for ks, g in sms:
                v = next(g)
                rsm.free(ks, v)
            kT, x1T, fT = rx1T.get()
            for i in range(nb):
                x1 = x1s[i][1]
                kp, ps, fp = rp.get()
                pe = op("tensor", [tr(ps[:, 0:128], x1[:, 0:128]), tr(ps[:, 128:256], x1[:, 128:256])], v, *fp)
                a = op("scalar", copy_act(x1T[:, :, 128 * i:128 * i + 128], ps[:, 0:256].rearrange("p (k t) -> p k t", k=2)), pe, *fT)
                rp.free(kp, a)
            kh, hT, fh = rhT.get()
            for m in range(2):
                kp, ps, fp = rp.get()
                pe = op("tensor", [mm(ps[:, 0:w], W1[:, k, 128 * m:128 * m + 128], x1T[:, k, 0:w], k == 0, k == 1) for k in range(2)], a, *fp)
                a2 = op("scalar", (lambda m, ps: lambda e: e.activation(hT[:, m, 0:w], ps[:, 0:w], ACT.Gelu, bias=b1c[:, m:m + 1]))(m, ps), pe, *fh)
                rp.free(kp, a2)
            rx1T.free(kT, pe)
            sms = []
            for i in range(nb):
                k1, x1 = x1s[i]
                kp, ps, fp = rp.get()
                pe = op("tensor", [mm(ps[:, 0:256], hT[:, k, 128 * i:128 * i + 128], W2[:, k, :], k == 0, k == 1) for k in range(2)], a2, *fp)
                op("vector", tt(x1[:, :], x1[:, :], bcs[:, 2, :], ALU.add), a)
                v = op("vector", tt(x1[:, :], x1[:, :], ps[:, 0:256], ALU.add), pe, Q.last("vector"))
                rp.free(kp, v)
                ks, sm, fs = rsm.get()
                gen = ln_tile(x1[:, :], x1[:, :], bcs[:, 3, :], bcs[:, 4, :], sm, v, *fs)
                next(gen)
                sms.append((ks, gen))
            rhT.free(kh, pe)
            for _, g in sms:
                next(g)
            for i, (ks, g) in enumerate(sms):
                k1, x1 = x1s[i]
                v = next(g)
                rsm.free(ks, v)
                v = chain(tt(X[:, b0 + i, :], X[:, b0 + i, :], x1[:, :], ALU.add))
                r1.free(k1, v)

        for b0, nb in groups:
            mix0_group(b0, nb)
        Q.barrier("gnn0", pool=False)

        WH = ART[:, 17500:25692].rearrange("p (w e k n) -> p w e k n", w=2, e=8, k=2)
        EW = []

        def ahead0():
            for i, n in enumerate(("L0_ffn_w1", "L0_ffn_w2")):
                for q in range(2):
                    sl = wslots[2 * i + q]
                    EW.append(dma("sync", sl, (lambda i, q, n: lambda e: e.dma_start(
                        WH[:, i, 4 * q:4 * q + 4], A[n][4 * q:4 * q + 4].rearrange("e (k p) n -> p e k n", p=128)))(i, q, n), (sl.sem, sl.n)))

        Y = gnn(8, 16, 56, 0.2, D_h, "g0", gathered, ahead0)
        AR.reset(NB * 264)
        bg = AR.take(256)
        L = Loader()
        t = L.load(bg[:, :], A["L0_gnn_bias"].partition_broadcast(128))
        for b in range(NB):
            op("vector", tt(Y[:, b, :], Y[:, b, :], bg[:, :], ALU.add), t)
            chain(stt(X[:, b, :], Y[:, b, :], 0.0, X[:, b, :], ALU.max, ALU.add))
        v = Q.last("vector")
        stats()
        Q.barrier("ffn0", *slots)

        rs_tok = rstd()
        AR.reset()
        RW = AR.take(2, 8)
        b1e = AR.take(8, 2)
        b2e = AR.take(256)
        COMB = AR.take(NB, 8)
        rx = ring(4, 256)
        rxt = ring(2, 2, 512)
        rh = ring(2, 2, 512)
        sm = ring(2, 4, 64)
        rc = ring(2, 512)
        assert AR.at <= 17500
        L = Loader()
        L.load(RW[:, :, :], A["routerT"].rearrange("(k p) n -> p k n", p=128))
        L.load(b1e[:, :, :], A["L0_ffn_b1"].rearrange("e (k p) -> p e k", p=128))
        L.load(b2e[0:8, :], A["L0_ffn_b2"])
        rf = Ring(banks[0:2])
        rp = Ring(banks[2:8])
        front_of, x_of = {}, {}

        def front(b0, nb):
            kX, xt, fX = rxt.get()
            pairs = [range(i, min(i + 2, nb)) for i in range(0, nb, 2)]
            ts_ = []
            for pr in pairs:
                kp, ps, fp = rf.get()
                for i in pr:
                    b = b0 + i
                    k, x_, fx = rx.get()
                    v = op("vector", xn_of(x_[:, :], b), rs_tok, *fx)
                    pe = op("tensor", [tr(ps[:, 256 * (i % 2) + 128 * j:256 * (i % 2) + 128 * j + 128], x_[:, 128 * j:128 * j + 128]) for j in range(2)], v, *fp)
                    v = op("vector", tt(X[:, b, :], X[:, b, :], x_[:, :], ALU.add), v)
                    rx.free(k, v, pe)
                    x_of[b] = v
                ts_.append((kp, ps, pe))
            front_of[b0] = (kX, xt, None)
            yield
            for pr, (kp, ps, pe) in zip(pairs, ts_):
                n = len(pr)
                c = slice(128 * pr[0], 128 * pr[0] + 128 * n)
                v = op("scalar", copy_act(xt[:, :, c].rearrange("p k (i t) -> p i k t", t=128), ps[:, 0:256 * n].rearrange("p (i k t) -> p i k t", k=2, t=128)), pe, *fX)
                rf.free(kp, v)
            front_of[b0] = (kX, xt, v)
            yield
            kp, ps, fp = rf.get()
            pe = op("tensor", [mm(ps[:, 8 * i:8 * i + 8], xt[:, k, 128 * i:128 * i + 128], RW[:, k, :], k == 0, k == 1)
                               for i in range(nb) for k in range(2)], v, *L.toks, *fp)
            yield
            ks, s_, fs = sm.get()
            lt = s_[:, 0, 0:8 * nb].rearrange("p (t e) -> p t e", e=8)
            top = s_[:, 1, 0:8 * nb].rearrange("p (t e) -> p t e", e=8)
            iu = s_[:, 2, :].bitcast(U32)[:, 0:8 * nb].rearrange("p (t e) -> p t e", e=8)
            fi = s_[:, 3, 0:8 * nb].rearrange("p (t e) -> p t e", e=8)
            q = lambda n: s_[:, 3, 32 + 4 * n:32 + 4 * n + nb]
            bc = lambda a: a.unsqueeze(2).to_broadcast([128, nb, 8])
            i8 = iota8[:, :].unsqueeze(1).to_broadcast([128, nb, 8])
            op("vector", cp(lt, ps[:, 0:8 * nb].rearrange("p (t e) -> p t e", e=8)), pe, *fs)
            v = chain(lambda e: e.tensor_reduce(q(0), lt, AX.X, ALU.max), tt(lt, lt, bc(q(0)), ALU.subtract))
            rf.free(kp, v)
            a = op("scalar", lambda e: e.activation(lt, lt, ACT.Exp), v)
            yield
            op("vector", lambda e: e.tensor_reduce(q(1), lt, AX.X, ALU.add), a)
            v = chain(rcp(q(2), q(1)), tt(lt, lt, bc(q(2)), ALU.mult))
            v = op("vector", [top8(top[:, i, :], lt[:, i, :]) for i in range(nb)], v)
            v = op("vector", [top8_at(iu[:, i, :], top[:, i, :], lt[:, i, :]) for i in range(nb)], v)
            C = COMB[:, b0:b0 + nb, :]
            v = chain(cp(fi, iu), tt(q(3), top[:, :, 0], top[:, :, 1], ALU.add), ts(q(3), q(3), 1e-12, None, ALU.max), rcp(q(4), q(3)),
                      tt(top[:, :, 0], top[:, :, 0], q(4), ALU.mult), tt(top[:, :, 1], top[:, :, 1], q(4), ALU.mult),
                      tt(C, i8, bc(fi[:, :, 0]), ALU.is_equal), tt(C, C, bc(top[:, :, 0]), ALU.mult),
                      tt(lt, i8, bc(fi[:, :, 1]), ALU.is_equal), tt(lt, lt, bc(top[:, :, 1]), ALU.mult), tt(C, C, lt, ALU.add))
            sm.free(ks, v)
            yield
            kp, ps, fp = rf.get()
            pe = op("tensor", [tr(ps[0:8, 128 * i:128 * i + 128], COMB[:, b0 + i, :]) for i in range(nb)], v, *fp)
            kc, c_, fc = rc.get()
            a = op("scalar", copy_act(c_[0:8, 0:128 * nb], ps[0:8, 0:128 * nb]), pe, *fc)
            rf.free(kp, a)
            yield
            ts_ = []
            for pr in pairs:
                kp, ps, fp = rf.get()
                pe = op("tensor", [mm(ps[:, 256 * (i % 2):256 * (i % 2) + 256], c_[0:8, 128 * i:128 * i + 128], b2e[0:8, :]) for i in pr], a, *fp)
                ts_.append((kp, ps, pe))
            rc.free(kc, pe)
            yield
            for pr, (kp, ps, pe) in zip(pairs, ts_):
                b, n = b0 + pr[0], len(pr)
                v1 = op("vector", tt(X[:, b:b + n, :], X[:, b:b + n, :], ps[:, 0:256 * n].rearrange("p (i f) -> p i f", f=256), ALU.add), pe, *[x_of[b + i] for i in range(n)])
                rf.free(kp, v1)
                for i in range(n):
                    x_of[b + i] = v1


        def expert(b0, nb, e_):
            w = 128 * nb
            kX, xt, vx = front_of[b0]
            kh, h, fh = rh.get()
            for m in range(2):
                kp, ps, fp = rp.get()
                pe = op("tensor", [mm(ps[:, 0:w], WH[:, 0, e_, k, 128 * m:128 * m + 128], xt[:, k, 0:w], k == 0, k == 1) for k in range(2)], *EW, vx, *fp)
                a = op("scalar", gelu(h[:, m, 0:w], ps[:, 0:w], b1e[:, e_, m:m + 1]), pe, *fh)
                rp.free(kp, a)
            if e_ == 7:
                rxt.free(kX, pe)
            yield
            yield
            for i in range(nb):
                b = b0 + i
                kp, ps, fp = rp.get()
                pe = op("tensor", [mm(ps[:, 0:256], h[:, k, 128 * i:128 * i + 128], WH[:, 1, e_, k, :], k == 0, k == 1) for k in range(2)], a, *fp)
                v = op("vector", stt(X[:, b, :], ps[:, 0:256], COMB[:, b, e_:e_ + 1], X[:, b, :], ALU.mult, ALU.add), pe, x_of[b])
                x_of[b] = v
                rp.free(kp, v)
            rh.free(kh, pe)

        pipeline([front(*groups[0])])
        order = []
        for g, (b0, nb) in enumerate(groups):
            for e_ in range(8):
                if e_ == 0 and g + 1 < len(groups):
                    order.append(front(*groups[g + 1]))
                order.append(expert(b0, nb, e_))
        pipeline(order)
        v = Q.last("vector")
        Q.op("vector", lambda e: e.memset(BN[:, 0, 0:1], 0.0), v)
        stats()
        Q.barrier("t1", *wslots)

        rstd()
        AR.reset()
        XT = AR.take(2, NP)
        WA = AR.take(2, 264)
        Wq = AR.take(2, 768)
        bq = AR.take(768)
        Wo = AR.take(2, 256)
        bo = AR.take(256)
        L = Loader()
        L.load(WA[:, :, 0:256], A["gW1T"].rearrange("(k p) n -> p k n", p=128))
        L.load(Wq[:, :, :], A["L1_mix_W_qkv"].rearrange("(k p) n -> p k n", p=128))
        L.load(bq[:, :], A["L1_mix_b_qkv"].partition_broadcast(128))
        L.load(Wo[:, :, :], A["L1_mix_W_out"].rearrange("(k p) n -> p k n", p=128))
        L.load(bo[:, :], A["L1_mix_b_out"].partition_broadcast(128))
        KV = AR.take(2, 256)
        mark = AR.at
        wa = att_columns(WA, 256, WA, A["ga_s1"], A["ga_d1"], 4, L)
        rp = Ring(banks[0:4])
        toks = transposed(lambda b, o: xn_of(o, b), XT, ring(3, 256), rp, Q.last("vector"))
        tables(XT, toks, WA, 4, D_z, D_as4, ADS, ring(4, 264), rp, wslots, wa)
        Q.barrier("mix1a", *slots, *wslots)
        gathered = gather_scores(4, 32, 28, D_as4)

        AR.reset(mark)
        rp = Ring(banks[0:4])
        rkv, rsq = ring(4, 512), ring(4, 512)
        rs = ring(4, 8)
        acc = []

        def centered_square(kv, sq, sm, v):
            v = op("vector", lambda e: e.tensor_reduce(sm[:, 0:1], kv[:, 0:256], AX.X, ALU.add), v)
            v = chain(ts(sm[:, 0:1], sm[:, 0:1], -1.0 / 256, None, ALU.mult))
            a = op("scalar", lambda e: e.activation(sq[:, 0:256], kv[:, 0:256], ACT.Square, bias=sm[:, 0:1], accum_out=sm[:, 1:2]), v)
            op("vector", ts(sm[:, 2:3], sm[:, 1:2], 1e-7, None, ALU.add), a)
            return chain(lambda e: e.reciprocal(sm[:, 3:4], sm[:, 2:3]), ts(sq[:, 0:256], sq[:, 0:256], sm[:, 3:4], None, ALU.mult))

        def kv1(b):
            K = 128 if b < 48 else LAST
            kp, ps, fp = rp.get()
            pe = op("tensor", [mm(ps[:, 0:512], XT[:, k, 128 * b:128 * b + 128], Wq[:, k, 256:768], k == 0, k == 1) for k in range(2)], *fp)
            yield
            kk, kv, fk = rkv.get()
            kq, sq, fq = rsq.get()
            k3, sm, f3 = rs.get()
            v = op("vector", tt(kv[:, :], ps[:, :], bq[:, 256:768], ALU.add), pe, *fk)
            rp.free(kp, v)
            v = centered_square(kv, sq, sm, v)
            a = op("scalar", lambda e: e.activation(sq[:, 256:512], sq[:, 0:256], ACT.Square), v, *fq, *f3)
            rs.free(k3, a)
            yield
            pe = op("tensor", [mm(banks[4 + j][:, 0:256], sq[0:K, 128 * j:128 * j + 128], kv[0:K, 256:512], b == 0, b == NB - 1) for j in range(2)]
                    + [mm(banks[6 + j][:, 0:1], sq[0:K, 256 + 128 * j:384 + 128 * j], ones[0:K, 0:1], b == 0, b == NB - 1) for j in range(2)], v, a)
            rkv.free(kk, pe)
            rsq.free(kq, pe)
            acc.append(pe)

        pipeline(kv1(b) for b in range(NB))
        nm = AR.take(8)
        for j in range(2):
            a = op("scalar", (lambda j: lambda e: e.activation(nm[:, j:j + 1], banks[6 + j][:, 0:1], ACT.Sqrt))(j), acc[-1])
            op("vector", ts(nm[:, 2 + j:3 + j], nm[:, j:j + 1], 1e-12, None, ALU.max), a)
            chain((lambda j: lambda e: e.reciprocal(nm[:, 4 + j:5 + j], nm[:, 2 + j:3 + j]))(j),
                  ts(KV[:, j, :], banks[4 + j][:, 0:256], nm[:, 4 + j:5 + j], None, ALU.mult))
        Q.barrier("mix1b", pool=False)

        AR.reset(mark)
        rp = Ring(banks[0:8])
        rq, rs = ring(4, 512), ring(4, 16)
        rsq, rT, rat, raT = ring(4, 512), ring(4, 256), ring(4, 256), ring(4, 256)

        def out1(b):
            kp, ps, fp = rp.get()
            xs = lambda k: XT[:, k, 128 * b:128 * b + 128]
            pe = op("tensor", [mm(ps[:, 0:256], xs(k), Wq[:, k, 0:256], k == 0, k == 1) for k in range(2)]
                    + [mm(ps[:, 256:512], xs(k), Wq[:, k, 512:768], k == 0, k == 1) for k in range(2)], *fp)
            yield
            kk, q, fk = rq.get()
            kq, sq, fq = rsq.get()
            k3, sm, f3 = rs.get()
            op("vector", tt(q[:, 0:256], ps[:, 0:256], bq[:, 0:256], ALU.add), pe, *fk, *fq, *f3)
            v = chain(tt(q[:, 256:512], ps[:, 256:512], bq[:, 512:768], ALU.add))
            rp.free(kp, v)
            v = centered_square(q, sq, sm, v)
            a = op("scalar", lambda e: e.activation(sq[:, 256:512], sq[:, 0:256], ACT.Square, accum_out=sm[:, 4:5]), v)
            a = op("scalar", lambda e: e.activation(sm[:, 5:6], sm[:, 4:5], ACT.Sqrt), a)
            op("vector", ts(sm[:, 6:7], sm[:, 5:6], 1e-12, None, ALU.max), a)
            v2 = chain(lambda e: e.reciprocal(sm[:, 7:8], sm[:, 6:7]), ts(sm[:, 8:9], sm[:, 7:8], float(N) ** -0.5, None, ALU.mult))
            kp, ps, fp = rp.get()
            pe = op("tensor", [tr(ps[:, 0:128], sq[:, 0:128]), tr(ps[:, 128:256], sq[:, 128:256])], v, *fp)
            rsq.free(kq, pe, a)
            yield
            kt, qT, ft = rT.get()
            a = op("scalar", copy_act(qT[:, :], ps[:, 0:256]), pe, *ft)
            rp.free(kp, a)
            kp, ps, fp = rp.get()
            pe = op("tensor", [mm(ps[:, 0:256], qT[:, 128 * j:128 * j + 128], KV[:, j, :], j == 0, j == 1) for j in range(2)], a, *fp)
            rT.free(kt, pe)
            yield
            ka, at, fa = rat.get()
            v = op("vector", stt(at[:, :], ps[:, 0:256], sm[:, 8:9], q[:, 256:512], ALU.mult, ALU.add), pe, v2, *fa)
            rp.free(kp, v)
            rs.free(k3, v)
            rq.free(kk, v)
            kp, ps, fp = rp.get()
            pe = op("tensor", [tr(ps[:, 0:128], at[:, 0:128]), tr(ps[:, 128:256], at[:, 128:256])], v, *fp)
            rat.free(ka, pe)
            yield
            kt, aT, ft = raT.get()
            a = op("scalar", copy_act(aT[:, :], ps[:, 0:256]), pe, *ft)
            rp.free(kp, a)
            kp, ps, fp = rp.get()
            pe = op("tensor", [mm(ps[:, 0:256], aT[:, 128 * k:128 * k + 128], Wo[:, k, :], k == 0, k == 1) for k in range(2)], a, *fp)
            raT.free(kt, pe)
            yield
            op("vector", tt(X[:, b, :], X[:, b, :], bo[:, :], ALU.add))
            v = op("vector", tt(X[:, b, :], X[:, b, :], ps[:, 0:256], ALU.add), pe, Q.last("vector"))
            rp.free(kp, v)

        pipeline(out1(b) for b in range(NB))
        Q.barrier("gnn1", pool=False)
        Y = gnn(4, 32, 28, 0.01, D_z, "g1", gathered)
        AR.reset(NB * 260)
        WA = AR.take(2, 258)
        L = Loader()
        L.load(WA[:, :, 0:256], A["gW2T"].rearrange("(k p) n -> p k n", p=128))
        wa = att_columns(WA, 256, WA, A["ga_s2"], A["ga_d2"], 1, L)
        t1 = ring(3, 256)
        t2 = ring(3, 256)
        tT = ring(3, 2, 128)
        ro = ring(4, 258)
        rp = Ring(banks[0:8])

        def z2_tile(b):
            k1, u, f1 = t1.get()
            v = op("vector", ts(u[:, :], Y[:, b, :], 0.0, None, ALU.min), *f1, wa)
            a = op("scalar", lambda e: e.activation(u[:, :], u[:, :], ACT.Exp), v)
            yield
            k2, h, f2 = t2.get()
            op("vector", ts(u[:, :], u[:, :], -1.0, None, ALU.add), a)
            v = op("vector", stt(h[:, :], Y[:, b, :], 0.0, u[:, :], ALU.max, ALU.add), Q.last("vector"), *f2)
            t1.free(k1, v)
            kp, ps, fp = rp.get()
            pe = op("tensor", [tr(ps[:, 0:128], h[:, 0:128]), tr(ps[:, 128:256], h[:, 128:256])], v, *fp)
            t2.free(k2, pe)
            yield
            kt, hT, ft = tT.get()
            a = op("scalar", copy_act(hT[:, :, :], ps[:, 0:256].rearrange("p (k t) -> p k t", k=2)), pe, *ft)
            rp.free(kp, a)
            kp, ps, fp = rp.get()
            pe = op("tensor", [mm(ps[:, 0:258], hT[:, k, :], WA[:, k, :], k == 0, k == 1) for k in range(2)], a, *fp)
            tT.free(kt, pe)
            yield
            ko, o, fo = ro.get()
            a = op("scalar", [copy_act(o[:, 0:256], ps[:, 0:256]), copy_act(ASS[:, b:b + 1], ps[:, 256:257]), copy_act(ADS[:, b:b + 1], ps[:, 257:258])], pe, *fo)
            rp.free(kp, a)
            s = wslots[b % 4]
            rows = slice(128 * b, 128 * b + 128)
            t = [dma("sync", s, lambda e: e.dma_start(D_z2[rows, :], o[:, 0:256]), a),
                 dma("sync", s, lambda e: e.dma_start(D_as1[rows, :], ASS[:, b:b + 1]), a)]
            ro.free(ko, t[-1])

        pipeline(z2_tile(b) for b in range(NB))
        Q.barrier("gnn2", *slots, *wslots)
        Y = gnn(1, 128, 7, 0.01, D_z2, "g2", ())
        for b in range(NB):
            op("vector", tt(X[:, b, :], X[:, b, :], Y[:, b, :], ALU.add))
        Q.op("vector", lambda e: e.memset(BN[:, 0, 0:1], 0.0), Q.last("vector"))
        stats()
        Q.barrier("ffn1")

        rstd()
        AR.reset()
        NE = NB + 7
        NG = NE // 4
        Wd = AR.take(8, 2048)
        W1 = AR.take(2, 1024)
        Wg = AR.take(8, 8)
        b1 = AR.take(8)
        bgc = AR.take(2)
        bd = AR.take(2048)
        L = Loader()
        L.load(W1[:, :, :], A["L1_ffn_W1"].rearrange("(k p) n -> p k n", p=128))
        L.load(Wg[:, :, :], A["L1_ffn_Wg"].rearrange("(m p) n -> p m n", p=128))
        L.load(b1[:, :], A["L1_ffn_b1"].rearrange("(m p) -> p m", p=128))
        L.load(bgc[0:8, 0:1], A["L1_ffn_bg"].unsqueeze(1))
        LD = [dma("sync", wslots[0], lambda e: e.dma_start(bd[0:1, :], A["L1_ffn_bd"].rearrange("e n -> (e n)").unsqueeze(0)), (wslots[0].sem, wslots[0].n))]
        wxt = dma("sync", wslots[1], lambda e: e.dma_start(D_xt[:, 0:256].rearrange("(b p) f -> p b f", p=128), X[:, :, :]), (wslots[1].sem, wslots[1].n))
        for e_ in range(8):
            LD.append(dma("sync", wslots[2 + e_ % 2], (lambda e_: lambda e: e.dma_start(Wd[:, :, 256 * e_:256 * e_ + 256], A["L1_ffn_Wd"][e_].rearrange("(m p) n -> p m n", p=128)))(e_),
                          (wslots[2 + e_ % 2].sem, wslots[2 + e_ % 2].n)))
        mark = AR.at
        rxt = ring(2, 2, 512)
        rH = ring(2, 8, 512)
        rx = ring(3, 256)
        rl = ring(2, 512)
        rs = ring(3, 4, 32)
        aux = AR.take(NB, 4)
        rp = Ring(banks[0:8])
        op("vector", [cp(aux[:, :, 0], MV[:, :, 0]), cp(aux[:, :, 1], RS[:, :])], Q.last("vector"))

        def route1(b0, nb):
            w = 128 * nb
            kX, xt, fX = rxt.get()
            for i in range(nb):
                k, x_, fx = rx.get()
                v = op("vector", xn_of(x_[:, :], b0 + i), *fx)
                kp, ps, fp = rp.get()
                pe = op("tensor", [tr(ps[:, 0:128], x_[:, 0:128]), tr(ps[:, 128:256], x_[:, 128:256])], v, *fp)
                rx.free(k, pe)
                a = op("scalar", copy_act(xt[:, :, 128 * i:128 * i + 128], ps[:, 0:256].rearrange("p (k t) -> p k t", k=2)), pe, *fX)
                rp.free(kp, a)
            yield
            kH, h, fH = rH.get()
            for m in range(8):
                kp, ps, fp = rp.get()
                pe = op("tensor", [mm(ps[:, 0:w], W1[:, k, 128 * m:128 * m + 128], xt[:, k, 0:w], k == 0, k == 1) for k in range(2)], a, *L.toks, *fp)
                a2 = op("scalar", gelu(h[:, m, 0:w], ps[:, 0:w], b1[:, m:m + 1]), pe, *fH)
                rp.free(kp, a2)
            rxt.free(kX, pe)
            kp, ps, fp = rp.get()
            pe = op("tensor", [mm(ps[0:8, 0:w], Wg[:, m, :], h[:, m, 0:w], m == 0, m == 7) for m in range(8)], a2, *fp)
            rH.free(kH, pe)
            kl, l_, fl = rl.get()
            v = op("vector", ts(l_[0:8, 0:w], ps[0:8, 0:w], bgc[0:8, 0:1], None, ALU.add), pe, *fl)
            rp.free(kp, v)
            kp, ps, fp = rp.get()
            pe = op("tensor", [tr(ps[:, 8 * i:8 * i + 8], l_[0:8, 128 * i:128 * i + 128], 8) for i in range(nb)], v, *fp)
            rl.free(kl, pe)
            yield
            k, s_, fs = rs.get()
            lt = s_[:, 0, 0:8 * nb].rearrange("p (t e) -> p t e", e=8)
            top = s_[:, 1, 0:8 * nb].rearrange("p (t e) -> p t e", e=8)
            iu = s_[:, 2, :].bitcast(U32)[:, 0:8 * nb].rearrange("p (t e) -> p t e", e=8)
            q = lambda n: s_[:, 3, 4 * n:4 * n + nb]
            bc = lambda a: a.unsqueeze(2).to_broadcast([128, nb, 8])
            op("vector", cp(lt, ps[:, 0:8 * nb].rearrange("p (t e) -> p t e", e=8)), pe, *fs)
            v = chain(lambda e: e.tensor_reduce(q(0), lt, AX.X, ALU.max), tt(lt, lt, bc(q(0)), ALU.subtract))
            rp.free(kp, v)
            a = op("scalar", lambda e: e.activation(lt, lt, ACT.Exp), v)
            op("vector", lambda e: e.tensor_reduce(q(1), lt, AX.X, ALU.add), a)
            v = chain(rcp(q(2), q(1)), tt(lt, lt, bc(q(2)), ALU.mult))
            v = op("vector", [top8(top[:, i, :], lt[:, i, :]) for i in range(nb)], v)
            v = op("vector", [top8_at(iu[:, i, :], top[:, i, :], lt[:, i, :]) for i in range(nb)], v)
            v = op("vector", [cp(aux[:, b0:b0 + nb, 2], top[:, :, 0]), cp(aux[:, b0:b0 + nb, 3], iu[:, :, 0])], v)
            rs.free(k, v)

        pipeline(route1(b0, nb) for b0, nb in groups)
        wau = dma("sync", wslots[0], lambda e: e.dma_start(D_xt[:, 256:260].rearrange("(b p) f -> p b f", p=128), aux[:, :, :]), Q.last("vector"), (wslots[0].sem, wslots[0].n))
        Q.barrier("sort1", *slots, *wslots)

        AR.reset(mark)
        aux2 = AR.take(NB, 4)
        O, PF, BS = AR.take(NB, 8), AR.take(NB, 8), AR.take(8, NB)
        CUM, TE = AR.take(8 * NB), AR.take(8, NB)
        tri, one_ = AR.take(128), AR.take(128)
        pos, posi, ni = AR.take(NB), AR.take(NB, dt=I32), AR.take(NB, dt=I32)
        q127, itl = AR.take(NB), AR.take(NB)
        gt_, cmpt = AR.take(NB), AR.take(NE, NB)
        sr, ES, TS, QP = AR.take(NE), AR.take(NE), AR.take(NE), AR.take(NE)
        cs, tsp, cmp8 = AR.take(NB), AR.take(2), AR.take(NE, 8)
        eq, MK, IDF, IDI = AR.take(NE), AR.take(NE), AR.take(NE), AR.take(NE, dt=I32)
        tspi = AR.take(2, dt=I32)
        idr, idf = AR.take(128, dt=I32), AR.take(128)
        edl, ewf, ewi, pw1 = AR.take(72), AR.take(4), AR.take(4, dt=I32), AR.take(72)
        IDG = AR.take(NE, dt=I32)
        assert AR.at <= 33500
        wpw = dma("sync", slots[0], lambda e: e.dma_start(pw1[0:1, :], A["pow2"][0:72].unsqueeze(0)), (slots[0].sem, slots[0].n))
        IT = dict(allow_small_or_imprecise_dtypes=True)
        g1 = op("gpsimd", [lambda e: e.iota(ni[:, :], pattern=[[128, NB]], base=0, channel_multiplier=1),
                           lambda e: e.iota(q127[:, :], pattern=[[128, NB]], base=127, channel_multiplier=0, **IT),
                           lambda e: e.iota(itl[:, :], pattern=[[1, NB]], base=0, channel_multiplier=0, **IT),
                           lambda e: e.iota(sr[:, :], pattern=[[1, NE]], base=0, channel_multiplier=0, **IT)])
        EI = aux[:, :, 3]
        v = op("vector", cp(O0[:, :], EI))
        op("vector", lambda e: e.memset(one_[:, :], 1.0), v)
        op("vector", tt(O[:, :, :], iota8[:, :].unsqueeze(1).to_broadcast([128, NB, 8]), O0[:, :].unsqueeze(2).to_broadcast([128, NB, 8]), ALU.is_equal), v)
        v = op("vector", ts(tri[:, :], iota_n[:, :], iota_p[:, 0:1], None, ALU.is_gt))
        pe = op("tensor", [mm(banks[0][:, 0:392], tri[:, :], O[:, :, :].rearrange("p b e -> p (b e)")),
                           mm(banks[1][:, 0:392], one_[:, :], O[:, :, :].rearrange("p b e -> p (b e)"))], v)
        op("vector", [cp(PF[:, :, :].rearrange("p b e -> p (b e)"), banks[0][:, 0:392]),
                      cp(TE[:, :, :], banks[1][:, 0:392].rearrange("p (b e) -> p e b", e=8))], pe)
        TEf = TE[:, :, :].rearrange("p e b -> p (e b)")
        v = chain(lambda e: e.memset(cmp8[:, :, :].rearrange("p s e -> p (s e)")[:, 0:392], 1.0),
                  lambda e: e.tensor_tensor_scan(CUM[:, :], cmp8[:, :, :].rearrange("p s e -> p (s e)")[:, 0:392], TEf, 0.0, ALU.mult, ALU.add),
                  tt(BS[:, :, :].rearrange("p e b -> p (e b)"), CUM[:, :], TEf, ALU.subtract),
                  tt(PF[:, :, :], PF[:, :, :], BS[:, :, :].rearrange("p e b -> p b e"), ALU.add),
                  tt(PF[:, :, :], PF[:, :, :], O[:, :, :], ALU.mult),
                  lambda e: e.tensor_reduce(pos[:, :], PF[:, :, :], AX.X, ALU.add),
                  cp(posi[:, :], pos[:, :]))
        for b in range(NB):
            g_ = gslots[b % 12]
            dma("gpsimd", g_, (lambda b: lambda e: e.indirect_dma_start(
                out=D_idx, out_offset=bass.IndirectOffsetOnAxis(ap=posi[:, b:b + 1], axis=0), in_=ni[:, b:b + 1], in_offset=None))(b), v, g1)
        END = CUM[:, :].rearrange("p (e b) -> p e b", b=NB)[:, 0:7, NB - 1]
        op("vector", tt(cmp8[:, 0:NB, 0:7], END.unsqueeze(1).to_broadcast([128, NB, 7]), q127[:, :].unsqueeze(2).to_broadcast([128, NB, 7]), ALU.is_le), Q.last("vector"), g1)
        v = chain(lambda e: e.tensor_reduce(gt_[:, :], cmp8[:, 0:NB, 0:7], AX.X, ALU.add),
                  tt(gt_[:, :], gt_[:, :], itl[:, :], ALU.add),
                  tt(cmpt[:, :, :], gt_[:, :].unsqueeze(1).to_broadcast([128, NE, NB]), sr[:, :].unsqueeze(2).to_broadcast([128, NE, NB]), ALU.is_lt),
                  lambda e: e.tensor_reduce(TS[:, :], cmpt[:, :, :], AX.X, ALU.add),
                  tt(ES[:, :], sr[:, :], TS[:, :], ALU.subtract),
                  ts(cs[:, :], gt_[:, :], iota_p[:, 0:1], None, ALU.is_lt),
                  lambda e: e.tensor_reduce(tsp[:, 0:1], cs[:, :], AX.X, ALU.add),
                  ts(tsp[:, 0:1], tsp[:, 0:1], float(NB - 1), None, ALU.min), cp(tspi[:, 0:1], tsp[:, 0:1]))
        gi_ = dma("gpsimd", gslots[0], lambda e: e.indirect_dma_start(
            out=idr[0:NE, :], out_offset=None, in_=D_idx.rearrange("(t p) a -> t (p a)", p=128),
            in_offset=bass.IndirectOffsetOnAxis(ap=tspi[0:NE, 0:1], axis=0)), v, *[(g_.sem, g_.n) for g_ in gslots])
        v = chain(ts(QP[:, :], TS[:, :], 128.0, iota_p[:, 0:1], ALU.mult, ALU.add),
                  tt(cmp8[:, :, 0:7], END.unsqueeze(1).to_broadcast([128, NE, 7]), QP[:, :].unsqueeze(2).to_broadcast([128, NE, 7]), ALU.is_le),
                  lambda e: e.tensor_reduce(eq[:, :], cmp8[:, :, 0:7], AX.X, ALU.add),
                  tt(MK[:, :], eq[:, :], ES[:, :], ALU.is_equal))
        op("vector", cp(idf[0:NE, :], idr[0:NE, :]), gi_)
        pe = op("tensor", tr(banks[2][:, 0:NE], idf[0:NE, :], NE), Q.last("vector"))
        op("vector", cp(IDF[:, :], banks[2][:, 0:NE]), pe)
        chain(cp(IDG[:, :], IDF[:, :]), ts(IDF[:, :], IDF[:, :], -8000.0, None, ALU.add), tt(IDF[:, :], IDF[:, :], MK[:, :], ALU.mult),
              ts(IDF[:, :], IDF[:, :], 8000.0, None, ALU.add), cp(IDI[:, :], IDF[:, :]))
        op("vector", [lambda e: e.memset(edl[0:1, :], 0.0)], Q.last("vector"))
        op("vector", tt(edl[0:1, 1:NE], ES[0:1, 1:NE], ES[0:1, 0:NE - 1], ALU.subtract), Q.last("vector"), wpw)
        chain(tt(edl[0:1, :], edl[0:1, :], pw1[0:1, :], ALU.mult),
              lambda e: e.tensor_reduce(ewf[0:1, 0:3], edl[0:1, :].rearrange("p (w i) -> p w i", i=24), AX.X, ALU.add),
              cp(ewi[0:1, 0:3], ewf[0:1, 0:3]))
        Q.barrier("ffn1c", *slots, *wslots, *gslots)

        keep = Arena(ARK, 256)
        kMK, kG, kI, kW = keep.take(NE), keep.take(NE, dt=I32), keep.take(NE, dt=I32), keep.take(4, dt=I32)
        v = op("vector", [cp(kMK[:, :], MK[:, :]), cp(kG[:, :], IDG[:, :]), cp(kI[:, :], IDI[:, :]), cp(kW[0:1, 0:3], ewi[0:1, 0:3])])
        Q.barrier("ffn1d")
        AR.reset(mark)
        XA = Arena(X[:, :, :].rearrange("p b f -> p (b f)"), NB * 256)
        rG = Ring([XA.take(260) for _ in range(12)])
        rO = Ring([XA.take(256) for _ in range(8)])
        rx = Ring([XA.take(256) for _ in range(4)])
        rc = Ring([XA.take(2) for _ in range(12)])
        rH = Ring([AR.take(8, 512), XA.take(8, 512)])
        rxt = ring(2, 2, 512)
        orow1 = AR.take(128)
        vo = op("vector", lambda e: e.memset(orow1[:, :], 1.0))
        rp = Ring(banks[0:8])

        def ffn1(q):
            gs = []
            for i in range(4):
                s = 4 * q + i
                kg, g_, fg = rG.get()
                sl = gslots[s % 12]
                w = dma("gpsimd", sl, (lambda g_, s: lambda e: e.indirect_dma_start(
                    out=g_[:, :], out_offset=None, in_=D_xt, in_offset=bass.IndirectOffsetOnAxis(ap=kG[:, s:s + 1], axis=0)))(g_, s), *fg)
                gs.append((kg, g_, w))
            yield
            kX, xt, fX = rxt.get()
            for i in range(4):
                kg, g_, w = gs[i]
                k, x_, fx = rx.get()
                v = op("vector", ts(x_[:, :], g_[:, 0:256], g_[:, 256:257], g_[:, 257:258], ALU.subtract, ALU.mult), w, *fx)
                kp, ps, fp = rp.get()
                pe = op("tensor", [tr(ps[:, 0:128], x_[:, 0:128]), tr(ps[:, 128:256], x_[:, 128:256])], v, *fp)
                rx.free(k, pe)
                a = op("scalar", copy_act(xt[:, :, 128 * i:128 * i + 128], ps[:, 0:256].rearrange("p (k t) -> p k t", k=2)), pe, *fX)
                rp.free(kp, a)
            kH, h, fH = rH.get()
            for m in range(8):
                kp, ps, fp = rp.get()
                pe = op("tensor", [mm(ps[:, :], W1[:, k, 128 * m:128 * m + 128], xt[:, k, :], k == 0, k == 1) for k in range(2)], a, *fp)
                a2 = op("scalar", gelu(h[:, m, :], ps[:, :], b1[:, m:m + 1]), pe, *fH)
                rp.free(kp, a2)
            rxt.free(kX, pe)
            yield
            for i in range(4):
                s = 4 * q + i
                kg, g_, w = gs[i]
                box = []
                Q.free("tensor", (lambda s, box: lambda e: box.append(block_of(e, "pe_e", s, 256, kW, 7)))(s, box))
                kp, ps, fp = rp.get()

                def bias_mm(e, ps=ps, box=box):
                    return e.matmul(ps[:, 0:256], orow1[0:1, :], bd[0:1, bass.ds(box[0], 256)], start=True, stop=False)

                def e_mm(m, i=i, ps=ps, box=box):
                    return lambda e: e.matmul(ps[:, 0:256], h[:, m, 128 * i:128 * i + 128], Wd[:, m, bass.ds(box[0], 256)], start=False, stop=(m == 7))

                pe = op("tensor", [bias_mm] + [e_mm(m) for m in range(8)], a2, vo, *fp)
                kc, c_, fc = rc.get()
                v = op("vector", tt(c_[:, 0:1], g_[:, 258:259], kMK[:, s:s + 1], ALU.mult), *fc)
                ko, o, fo = rO.get()
                v = op("vector", stt(o[:, :], ps[:, 0:256], c_[:, 0:1], g_[:, 0:256], ALU.mult, ALU.add), pe, v, *fo)
                rp.free(kp, v)
                rc.free(kc, v)
                rG.free(kg, v)
                sl = oslot8[s % 8]
                t = dma("gpsimd", sl, (lambda o, s: lambda e: e.indirect_dma_start(
                    out=out, out_offset=bass.IndirectOffsetOnAxis(ap=kI[:, s:s + 1], axis=0), in_=o[:, :], in_offset=None,
                    bounds_check=N - 1, oob_is_err=False))(o, s), v)
                rO.free(ko, t)
            rH.free(kH, pe)

        pipeline(ffn1(q) for q in range(NG))
        Q.barrier("end", *oslot8)
        finish(nc, ctx, Q)


def finish(nc, ctx, Q):
    ctx.enter_context(nc.allow_non_contiguous_dma(reason="short columns of tables"))
    block = ctx.enter_context(nc.Block())

    @block.sync
    def _(e):
        Q.play("sync", e)

    @block.scalar
    def _(e):
        Q.play("scalar", e)

    @block.vector
    def _(e):
        Q.play("vector", e)

    @block.tensor
    def _(e):
        Q.play("tensor", e)

    @block.gpsimd
    def _(e):
        Q.play("gpsimd", e)


def kernel(**inputs):
    import numpy as _np
    import concourse.bacc as _bacc
    from concourse import mybir as _mybir
    from concourse.bass_utils import run_bass_kernel_spmd as _run

    x = {k: _np.asarray(v) for k, v in inputs.items()}
    w1 = x["L1_gnn_W1"]
    arrays = {
        "pow2": (2.0 ** (_np.arange(NW * 24) % 24)).astype(_np.float32),
        "x": x["x"], "src": x["src"], "dst": x["dst"],
        "gW0": x["L0_gnn_W"].reshape(256, 256),
        "ga_s0": x["L0_gnn_att_src"].reshape(256), "ga_d0": x["L0_gnn_att_dst"].reshape(256),
        "qkv0T": x["L0_mix_Wqkv"].T, "m0W1T": x["L0_mix_W1"].T, "m0W2T": x["L0_mix_W2"].T,
        "routerT": x["L0_ffn_router_w"].T,
        "gW1T": w1.reshape(256, 256).T,
        "ga_s1": x["L1_gnn_a1"][:, :64].reshape(256), "ga_d1": x["L1_gnn_a1"][:, 64:].reshape(256),
        "gW2T": x["L1_gnn_W2"].T,
        "ga_s2": x["L1_gnn_a2"][:256], "ga_d2": x["L1_gnn_a2"][256:],
    }
    for k in ("L0_gnn_bias", "L0_mix_ln1_g", "L0_mix_ln1_b", "L0_mix_b1", "L0_mix_b2", "L0_mix_ln2_g", "L0_mix_ln2_b",
              "L0_ffn_w1", "L0_ffn_b1", "L0_ffn_w2", "L0_ffn_b2", "L1_mix_W_qkv", "L1_mix_b_qkv", "L1_mix_W_out", "L1_mix_b_out",
              "L1_ffn_W1", "L1_ffn_b1", "L1_ffn_Wg", "L1_ffn_bg", "L1_ffn_Wd", "L1_ffn_bd"):
        arrays[k] = x[k]
    nc = _bacc.Bacc("TRN2", target_bir_lowering=False, num_devices=1)
    fed, args = {}, {}
    for k, v in arrays.items():
        v = _np.ascontiguousarray(v)
        fed[f"in_{k}"] = v
        args[k] = nc.dram_tensor(f"in_{k}", v.shape, _mybir.dt.from_np(v.dtype), kind="ExternalInput").ap()
    out = nc.dram_tensor("out_0", (N, 256), _mybir.dt.float32, kind="ExternalOutput").ap()
    program(nc, args, out)
    r = _run(nc, [fed], core_ids=[0])
    return r.results[0]["out_0"]
```
